# Optimizing a Trainium2 kernel written in Bass

```python
import numpy as np
import jax
import jax.numpy as jnp

def _softmax(x, axis=-1):
    return jax.nn.softmax(x, axis=axis)

def _gelu(x):
    return jax.nn.gelu(x, approximate=True)

def _silu(x):
    return jax.nn.silu(x)

def _sigmoid(x):
    return jax.nn.sigmoid(x)

def _layernorm(x, axis=-1, eps=1e-05):
    m = jnp.mean(x, axis=axis, keepdims=True)
    v = jnp.var(x, axis=axis, keepdims=True)
    return (x - m) / jnp.sqrt(v + eps)

def _scatter_add(tgt, idx, src, axis=0):
    return tgt.at[idx].add(src)

def _segment_sum(src, seg, n):
    return jax.ops.segment_sum(src, seg, n)
kernel_name = 'mk_gps_d2_gnn_r8_e9a270'

def setup_inputs(seed: int=0):
    np.random.seed(seed)
    _w = jnp.asarray

    def _rec_inputs():
        import jax
        import jax.numpy as jnp
        _gk = jax.random.key(seed)
        x = -8.776e-05 + 1 * jax.random.normal(jax.random.fold_in(_gk, 1), (1250, 512), jnp.float32)
        _s = jax.random.randint(jax.random.fold_in(_gk, 2), (10000,), 0, 1250, jnp.int32)
        _d = jax.random.randint(jax.random.fold_in(_gk, 3), (10000,), 0, 1250, jnp.int32)
        _loop = jnp.arange(1250, dtype=jnp.int32)
        src = jnp.concatenate([_s, _d, _loop])
        dst = jnp.concatenate([_d, _s, _loop])
        _o = jnp.argsort(dst, stable=True)
        src = src[_o]
        dst = dst[_o]
        return (x, src, dst)
    x, src, dst = _rec_inputs()

    def _L0_gnn_setup():
        import jax, jax.numpy as jnp
        import numpy as np
        N_NODES = 1250
        N_EDGES = 20000
        D = 512

        def _sage_conv(x, src, dst, Wl, bl, Wr, num_nodes):
            msg = x[src]
            agg = jax.ops.segment_sum(msg, dst, num_segments=num_nodes)
            cnt = jax.ops.segment_sum(jnp.ones((src.shape[0],), x.dtype), dst, num_segments=num_nodes)
            agg = agg / jnp.maximum(cnt, 1.0)[:, None]
            return agg @ Wl.T + bl + x @ Wr.T
        key = jax.random.key(seed)
        ks = jax.random.split(key, 8)
        s = 1.0 / np.sqrt(D)
        x = jax.random.normal(ks[0], (N_NODES, D), dtype=jnp.float32)
        edge_index = jax.random.randint(ks[1], (2, N_EDGES), 0, N_NODES, dtype=jnp.int64)
        Wl1 = jax.random.uniform(ks[2], (D, D), jnp.float32, -s, s)
        bl1 = jax.random.uniform(ks[3], (D,), jnp.float32, -s, s)
        Wr1 = jax.random.uniform(ks[4], (D, D), jnp.float32, -s, s)
        Wl2 = jax.random.uniform(ks[5], (D, D), jnp.float32, -s, s)
        bl2 = jax.random.uniform(ks[6], (D,), jnp.float32, -s, s)
        Wr2 = jax.random.uniform(ks[7], (D, D), jnp.float32, -s, s)
        return {'x': x, 'edge_index': edge_index, 'Wl1': Wl1, 'bl1': bl1, 'Wr1': Wr1, 'Wl2': Wl2, 'bl2': bl2, 'Wr2': Wr2}
    _L0_gnn_all = _L0_gnn_setup()
    _L0_gnn_in = {k: v for k, v in _L0_gnn_all.items() if k in ('Wl1', 'bl1', 'Wr1', 'Wl2', 'bl2', 'Wr2')}
    del _L0_gnn_all

    def _L0_mix_setup():
        import jax, jax.numpy as jnp
        import numpy as np
        B, N, C = (8, 512, 512)
        key = jax.random.key(seed)
        ks = jax.random.split(key, 6)
        s = 1.0 / np.sqrt(C)
        return {'x': jax.random.normal(ks[0], (B, N, C), jnp.float32), 'Wq': jax.random.normal(ks[1], (C, C), jnp.float32) * s, 'Wk': jax.random.normal(ks[2], (C, C), jnp.float32) * s, 'Wv': jax.random.normal(ks[3], (C, C), jnp.float32) * s, 'W1': jax.random.normal(ks[4], (C, C), jnp.float32) * s, 'W2': jax.random.normal(ks[5], (C, C), jnp.float32) * s}
    _L0_mix_all = _L0_mix_setup()
    _L0_mix_in = {k: v for k, v in _L0_mix_all.items() if k in ('Wq', 'Wk', 'Wv', 'W1', 'W2')}
    del _L0_mix_all

    def _L0_ffn_setup():
        import jax, jax.numpy as jnp
        import numpy as np
        B, S, D, H, E = (4, 1024, 512, 256, 8)
        key = jax.random.key(seed)
        ks = jax.random.split(key, 7)
        scale = 1.0 / np.sqrt(D)
        return {'x': jax.random.normal(ks[0], (B, S, D), dtype=jnp.float32), 'Wg': jax.random.normal(ks[1], (D, E), dtype=jnp.float32) * scale, 'bg': jnp.zeros((E,), dtype=jnp.float32), 'W1': jax.random.normal(ks[2], (E, D, H), dtype=jnp.float32) * scale, 'b1': jnp.zeros((E, H), dtype=jnp.float32), 'W2': jax.random.normal(ks[3], (E, H, D), dtype=jnp.float32) * (1.0 / np.sqrt(H)), 'b2': jnp.zeros((E, D), dtype=jnp.float32)}
    _L0_ffn_all = _L0_ffn_setup()
    _L0_ffn_in = {k: v for k, v in _L0_ffn_all.items() if k in ('Wg', 'bg', 'W1', 'b1', 'W2', 'b2')}
    del _L0_ffn_all

    def _L1_gnn_setup():
        import jax, jax.numpy as jnp
        import numpy as np
        N_NODES = 1250

        def gcn_conv(x, edge_index, W, b):
            n = x.shape[0]
            loop = jnp.arange(n)
            src = jnp.concatenate([edge_index[0], loop])
            dst = jnp.concatenate([edge_index[1], loop])
            deg = jax.ops.segment_sum(jnp.ones_like(dst, dtype=x.dtype), dst, num_segments=n)
            dinv = jnp.where(deg > 0, jax.lax.rsqrt(deg), 0.0)
            norm = dinv[src] * dinv[dst]
            h = x @ W
            msg = h[src] * norm[:, None]
            out = jax.ops.segment_sum(msg, dst, num_segments=n)
            return out + b
        key = jax.random.key(seed)
        k1, k2, k3, k4 = jax.random.split(key, 4)
        c = [512, 1024, 512]
        x = jax.random.normal(k1, (N_NODES, c[0]), dtype=jnp.float32)
        edge_index = jax.random.randint(k2, (2, 20000), 0, N_NODES, dtype=jnp.int64)
        W1 = jax.random.normal(k3, (c[0], c[1]), dtype=jnp.float32) / np.sqrt(c[0])
        b1 = jnp.zeros((c[1],), dtype=jnp.float32)
        W2 = jax.random.normal(k4, (c[1], c[2]), dtype=jnp.float32) / np.sqrt(c[1])
        b2 = jnp.zeros((c[2],), dtype=jnp.float32)
        return {'x': x, 'edge_index': edge_index, 'W1': W1, 'b1': b1, 'W2': W2, 'b2': b2}
    _L1_gnn_all = _L1_gnn_setup()
    _L1_gnn_in = {k: v for k, v in _L1_gnn_all.items() if k in ('W1', 'b1', 'W2', 'b2')}
    del _L1_gnn_all

    def _L1_mix_setup():
        import jax, jax.numpy as jnp
        import numpy as np
        EPS = 1e-06
        key = jax.random.key(seed)
        k1, k2 = jax.random.split(key)
        B, N, C = (8, 512, 512)
        x = jax.random.normal(k1, (B, N, C), dtype=jnp.float32)
        W_qk = jax.random.normal(k2, (2 * C, C), dtype=jnp.float32) * (1.0 / np.sqrt(C))
        return {'x': x, 'W_qk': W_qk}
    _L1_mix_all = _L1_mix_setup()
    _L1_mix_in = {k: v for k, v in _L1_mix_all.items() if k in ('W_qk',)}
    del _L1_mix_all

    def _L1_ffn_setup():
        import jax, jax.numpy as jnp
        import numpy as np
        B, N, DIM = (1, 256, 512)
        DH, H = (64, 8)
        E, FF = (8, 256)

        def _layernorm(x, g, b, eps=1e-05):
            mu = jnp.mean(x, axis=-1, keepdims=True)
            var = jnp.mean(jnp.square(x - mu), axis=-1, keepdims=True)
            return (x - mu) * jax.lax.rsqrt(var + eps) * g + b

        def _l2norm(x, eps=1e-12):
            return x / jnp.sqrt(jnp.sum(jnp.square(x), axis=-1, keepdims=True) + eps)
        key = jax.random.key(seed)
        ks = jax.random.split(key, 12)
        g = lambda k, shape: jax.random.normal(k, shape, jnp.float32) * 0.02
        return {'x': jax.random.normal(ks[0], (B, N, DIM), jnp.float32), 'ln_g': jnp.ones((DIM,), jnp.float32), 'ln_b': jnp.zeros((DIM,), jnp.float32), 'Wq': g(ks[1], (DIM, DIM)), 'Wk': g(ks[2], (DIM, DIM)), 'Wv': g(ks[3], (DIM, DIM)), 'Wo': g(ks[4], (DIM, DIM)), 'qn_g': jnp.ones((DH,), jnp.float32), 'kn_g': jnp.ones((DH,), jnp.float32), 'gate_W': g(ks[5], (DIM, E)), 'gate_b': jnp.zeros((E,), jnp.float32), 'W1': g(ks[6], (E, DIM, FF)), 'b1': jnp.zeros((E, FF), jnp.float32), 'W2': g(ks[7], (E, FF, DIM)), 'b2': jnp.zeros((E, DIM), jnp.float32)}
    _L1_ffn_all = _L1_ffn_setup()
    _L1_ffn_in = {k: v for k, v in _L1_ffn_all.items() if k in ('ln_g', 'ln_b', 'Wq', 'Wk', 'Wv', 'Wo', 'qn_g', 'kn_g', 'gate_W', 'gate_b', 'W1', 'b1', 'W2', 'b2')}
    del _L1_ffn_all
    return {'x': x, 'src': src, 'dst': dst, 'L0_gnn_Wl1': _L0_gnn_in['Wl1'], 'L0_gnn_bl1': _L0_gnn_in['bl1'], 'L0_gnn_Wr1': _L0_gnn_in['Wr1'], 'L0_gnn_Wl2': _L0_gnn_in['Wl2'], 'L0_gnn_bl2': _L0_gnn_in['bl2'], 'L0_gnn_Wr2': _L0_gnn_in['Wr2'], 'L0_mix_Wq': _L0_mix_in['Wq'], 'L0_mix_Wk': _L0_mix_in['Wk'], 'L0_mix_Wv': _L0_mix_in['Wv'], 'L0_mix_W1': _L0_mix_in['W1'], 'L0_mix_W2': _L0_mix_in['W2'], 'L0_ffn_Wg': _L0_ffn_in['Wg'], 'L0_ffn_bg': _L0_ffn_in['bg'], 'L0_ffn_W1': _L0_ffn_in['W1'], 'L0_ffn_b1': _L0_ffn_in['b1'], 'L0_ffn_W2': _L0_ffn_in['W2'], 'L0_ffn_b2': _L0_ffn_in['b2'], 'L1_gnn_W1': _L1_gnn_in['W1'], 'L1_gnn_b1': _L1_gnn_in['b1'], 'L1_gnn_W2': _L1_gnn_in['W2'], 'L1_gnn_b2': _L1_gnn_in['b2'], 'L1_mix_W_qk': _L1_mix_in['W_qk'], 'L1_ffn_ln_g': _L1_ffn_in['ln_g'], 'L1_ffn_ln_b': _L1_ffn_in['ln_b'], 'L1_ffn_Wq': _L1_ffn_in['Wq'], 'L1_ffn_Wk': _L1_ffn_in['Wk'], 'L1_ffn_Wv': _L1_ffn_in['Wv'], 'L1_ffn_Wo': _L1_ffn_in['Wo'], 'L1_ffn_qn_g': _L1_ffn_in['qn_g'], 'L1_ffn_kn_g': _L1_ffn_in['kn_g'], 'L1_ffn_gate_W': _L1_ffn_in['gate_W'], 'L1_ffn_gate_b': _L1_ffn_in['gate_b'], 'L1_ffn_W1': _L1_ffn_in['W1'], 'L1_ffn_b1': _L1_ffn_in['b1'], 'L1_ffn_W2': _L1_ffn_in['W2'], 'L1_ffn_b2': _L1_ffn_in['b2']}

def reference(x, src, dst, L0_gnn_Wl1, L0_gnn_bl1, L0_gnn_Wr1, L0_gnn_Wl2, L0_gnn_bl2, L0_gnn_Wr2, L0_mix_Wq, L0_mix_Wk, L0_mix_Wv, L0_mix_W1, L0_mix_W2, L0_ffn_Wg, L0_ffn_bg, L0_ffn_W1, L0_ffn_b1, L0_ffn_W2, L0_ffn_b2, L1_gnn_W1, L1_gnn_b1, L1_gnn_W2, L1_gnn_b2, L1_mix_W_qk, L1_ffn_ln_g, L1_ffn_ln_b, L1_ffn_Wq, L1_ffn_Wk, L1_ffn_Wv, L1_ffn_Wo, L1_ffn_qn_g, L1_ffn_kn_g, L1_ffn_gate_W, L1_ffn_gate_b, L1_ffn_W1, L1_ffn_b1, L1_ffn_W2, L1_ffn_b2):
    import jax
    import jax.numpy as jnp

    def _L0_gnn_ref(x, edge_index, Wl1, bl1, Wr1, Wl2, bl2, Wr2):
        import jax, jax.numpy as jnp
        import numpy as np
        N_NODES = 1250
        N_EDGES = 20000
        D = 512

        def _sage_conv(x, src, dst, Wl, bl, Wr, num_nodes):
            msg = x[src]
            agg = jax.ops.segment_sum(msg, dst, num_segments=num_nodes)
            cnt = jax.ops.segment_sum(jnp.ones((src.shape[0],), x.dtype), dst, num_segments=num_nodes)
            agg = agg / jnp.maximum(cnt, 1.0)[:, None]
            return agg @ Wl.T + bl + x @ Wr.T
        src, dst = (edge_index[0], edge_index[1])
        num_nodes = x.shape[0]
        h = jax.nn.relu(_sage_conv(x, src, dst, Wl1, bl1, Wr1, num_nodes))
        return _sage_conv(h, src, dst, Wl2, bl2, Wr2, num_nodes)

    def _L0_mix_ref(x, Wq, Wk, Wv, W1, W2):
        import jax, jax.numpy as jnp
        import numpy as np
        B, N, C = (8, 512, 512)
        q = x @ Wq.T
        k = x @ Wk.T
        v = x @ Wv.T
        dim = q.shape[-1]
        q = jax.nn.softmax(q, axis=-1) * dim ** (-0.5)
        k = jax.nn.softmax(k, axis=-2)
        context = jnp.einsum('bnd,bne->bde', k, v)
        attn = jnp.einsum('bnd,bde->bne', q, context)
        x = attn + x
        return x @ W1.T @ W2.T + x

    def _L0_ffn_ref(x, Wg, bg, W1, b1, W2, b2):
        import jax, jax.numpy as jnp
        import numpy as np
        B, S, D, H, E = (4, 1024, 512, 256, 8)
        b, s, d = x.shape
        xf = x.reshape(-1, d)
        logits = xf @ Wg + bg
        scores = jax.nn.softmax(logits, axis=-1)
        top_s, top_i = jax.lax.top_k(scores, 1)
        idx = top_i[:, 0]
        sc = top_s[:, 0]
        n_experts = Wg.shape[1]
        out = jnp.zeros_like(xf)
        for e in range(n_experts):
            h = jax.nn.relu(xf @ W1[e] + b1[e]) @ W2[e] + b2[e]
            out = jnp.where((idx == e)[:, None], h, out)
        out = out * sc[:, None]
        return out.reshape(b, s, d)

    def _L1_gnn_ref(x, edge_index, W1, b1, W2, b2):
        import jax, jax.numpy as jnp
        import numpy as np
        N_NODES = 1250

        def gcn_conv(x, edge_index, W, b):
            n = x.shape[0]
            loop = jnp.arange(n)
            src = jnp.concatenate([edge_index[0], loop])
            dst = jnp.concatenate([edge_index[1], loop])
            deg = jax.ops.segment_sum(jnp.ones_like(dst, dtype=x.dtype), dst, num_segments=n)
            dinv = jnp.where(deg > 0, jax.lax.rsqrt(deg), 0.0)
            norm = dinv[src] * dinv[dst]
            h = x @ W
            msg = h[src] * norm[:, None]
            out = jax.ops.segment_sum(msg, dst, num_segments=n)
            return out + b
        h = jax.nn.relu(gcn_conv(x, edge_index, W1, b1))
        h = jax.nn.relu(gcn_conv(h, edge_index, W2, b2))
        return h

    def _L1_mix_ref(x, W_qk):
        import jax, jax.numpy as jnp
        import numpy as np
        EPS = 1e-06
        B, N, C = x.shape
        qk = jnp.einsum('bnc,dc->bnd', x, W_qk).reshape(B, N, 2, C)
        q = jax.nn.elu(qk[:, :, 0]) + 1.0
        k = jax.nn.elu(qk[:, :, 1]) + 1.0
        kv = jnp.einsum('bnd,bne->bde', k, x)
        z = 1.0 / (jnp.einsum('bnd,bd->bn', q, k.sum(axis=1)) + EPS)
        out = jnp.einsum('bnd,bde,bn->bne', q, kv, z)
        return out

    def _L1_ffn_ref(x, ln_g, ln_b, Wq, Wk, Wv, Wo, qn_g, kn_g, gate_W, gate_b, W1, b1, W2, b2):
        import jax, jax.numpy as jnp
        import numpy as np
        B, N, DIM = (1, 256, 512)
        DH, H = (64, 8)
        E, FF = (8, 256)

        def _layernorm(x, g, b, eps=1e-05):
            mu = jnp.mean(x, axis=-1, keepdims=True)
            var = jnp.mean(jnp.square(x - mu), axis=-1, keepdims=True)
            return (x - mu) * jax.lax.rsqrt(var + eps) * g + b

        def _l2norm(x, eps=1e-12):
            return x / jnp.sqrt(jnp.sum(jnp.square(x), axis=-1, keepdims=True) + eps)
        b, n, d = x.shape
        dh = qn_g.shape[0]
        h = d // dh
        hx = _layernorm(x, ln_g, ln_b)
        q = (hx @ Wq).reshape(b, n, h, dh).transpose(0, 2, 1, 3)
        k = (hx @ Wk).reshape(b, n, h, dh).transpose(0, 2, 1, 3)
        v = (hx @ Wv).reshape(b, n, h, dh).transpose(0, 2, 1, 3)
        scale = jnp.sqrt(jnp.float32(dh))
        q = _l2norm(q) * scale * qn_g
        k = _l2norm(k) * scale * kn_g
        scores = jnp.einsum('bhqd,bhkd->bhqk', q, k) * dh ** (-0.5)
        causal = jnp.tril(jnp.ones((n, n), bool))
        scores = jnp.where(causal, scores, jnp.finfo(scores.dtype).min)
        attn = jax.nn.softmax(scores, axis=-1)
        o = jnp.einsum('bhqk,bhkd->bhqd', attn, v)
        y = o.transpose(0, 2, 1, 3).reshape(b, n, d) @ Wo
        gate = jax.nn.softmax(y @ gate_W + gate_b, axis=-1)
        hid = jax.nn.gelu(jnp.einsum('bnd,edf->bnef', y, W1) + b1)
        eo = jnp.einsum('bnef,efd->bned', hid, W2) + b2
        out = jnp.einsum('bned,bne->bnd', eo, gate)
        return out
    edge_index = jnp.stack([src, dst])
    xn = _layernorm(x, axis=-1)
    x = x + _L0_gnn_ref(xn, edge_index, L0_gnn_Wl1, L0_gnn_bl1, L0_gnn_Wr1, L0_gnn_Wl2, L0_gnn_bl2, L0_gnn_Wr2) + _L0_mix_ref(xn[None], L0_mix_Wq, L0_mix_Wk, L0_mix_Wv, L0_mix_W1, L0_mix_W2)[0]
    x = x + _L0_ffn_ref(_layernorm(x, axis=-1)[None], L0_ffn_Wg, L0_ffn_bg, L0_ffn_W1, L0_ffn_b1, L0_ffn_W2, L0_ffn_b2)[0]
    xn = _layernorm(x, axis=-1)
    x = x + _L1_gnn_ref(xn, edge_index, L1_gnn_W1, L1_gnn_b1, L1_gnn_W2, L1_gnn_b2) + _L1_mix_ref(xn[None], L1_mix_W_qk)[0]
    x = x + _L1_ffn_ref(_layernorm(x, axis=-1)[None], L1_ffn_ln_g, L1_ffn_ln_b, L1_ffn_Wq, L1_ffn_Wk, L1_ffn_Wv, L1_ffn_Wo, L1_ffn_qn_g, L1_ffn_kn_g, L1_ffn_gate_W, L1_ffn_gate_b, L1_ffn_W1, L1_ffn_b1, L1_ffn_W2, L1_ffn_b2)[0]
    return x

_drawn_inputs = setup_inputs


def setup_inputs(seed=0):
    import zlib

    import numpy as np

    out = dict(_drawn_inputs(seed))
    spreads = {'L0_ffn_bg': (0.0, 0.285),
     'L0_ffn_b1': (0.0, 0.645),
     'L0_ffn_b2': (0.0, 0.431),
     'L1_gnn_b1': (0.0, 0.52),
     'L1_gnn_b2': (0.0, 0.1),
     'L1_ffn_ln_g': (1.0, 0.6),
     'L1_ffn_ln_b': (0.0, 0.8),
     'L1_ffn_qn_g': (1.0, 0.6),
     'L1_ffn_kn_g': (1.0, 0.6),
     'L1_ffn_gate_b': (0.0, 0.8),
     'L1_ffn_b1': (0.0, 2.0),
     'L1_ffn_b2': (0.0, 2.0)}
    factors = {'L0_gnn_bl1': 6.903,
     'L0_gnn_bl2': 2.976,
     'L0_mix_Wq': 8.0,
     'L0_mix_Wk': 8.0,
     'L0_mix_Wv': 8.0,
     'L1_mix_W_qk': 44.605,
     'L1_ffn_Wq': 8.0,
     'L1_ffn_Wk': 8.0,
     'L1_ffn_Wv': 8.0,
     'L1_ffn_Wo': 8.0,
     'L1_ffn_gate_W': 8.0,
     'L1_ffn_W1': 8.0,
     'L1_ffn_W2': 8.0}
    for name, (base, spread) in spreads.items():
        noise = np.random.default_rng([zlib.crc32(name.encode()), seed]).standard_normal(out[name].shape)
        drawn = base * np.exp(spread * noise) if base else spread * noise
        out[name] = jnp.asarray(drawn.astype(out[name].dtype))
    for name, factor in factors.items():
        out[name] = (out[name] * factor).astype(out[name].dtype)
    return out
```

```python
from contextlib import ExitStack

import concourse.bass as bass
from concourse import mybir

F32 = mybir.dt.float32
F32R = mybir.dt.float32r
BF16 = mybir.dt.bfloat16
F16 = mybir.dt.float16
I32 = mybir.dt.int32
ALU = mybir.AluOpType
ACT = mybir.ActivationFunctionType
AX_X = mybir.AxisListType.X

N = 1250
D = 512
TILE = 125
NT = N // TILE
FB = D // 128
CH = [(0, 500), (500, 500), (1000, 250)]
E = 8
HID = 256
HEADS, DH = 8, 64
EDGES = 21250
GROUPS, GT = 17, 10
NOH = 4
PRIME = 2 * GT
WIN = 128
LASTWIN = N - WIN
FEW = 3
EPS = 1e-5
BANKS = 8


def build(nc, x, src, dst, L0_gnn_Wl1, L0_gnn_bl1, L0_gnn_Wr1, L0_gnn_Wl2, L0_gnn_bl2, L0_gnn_Wr2,
          L0_mix_Wq, L0_mix_Wk, L0_mix_Wv, L0_mix_W1, L0_mix_W2,
          L0_ffn_Wg, L0_ffn_bg, L0_ffn_W1, L0_ffn_b1, L0_ffn_W2, L0_ffn_b2,
          L1_gnn_W1, L1_gnn_b1, L1_gnn_W2, L1_gnn_b2, L1_mix_W_qk,
          L1_ffn_ln_g, L1_ffn_ln_b, L1_ffn_Wq, L1_ffn_Wk, L1_ffn_Wv, L1_ffn_Wo, L1_ffn_qn_g, L1_ffn_kn_g,
          L1_ffn_gate_W, L1_ffn_gate_b, L1_ffn_W1, L1_ffn_b1, L1_ffn_W2, L1_ffn_b2, out):
    COL = {"bl1": 0, "gb1": 4, "m0b1": 12, "m1b1": 28, "ln_g": 44, "ln_b": 48, "qn_g": 52, "kn_g": 53}
    ctx = ExitStack()
    ctx = ExitStack()
    with ctx:
        def at(name, shape, dt, offset):
            return nc.alloc_sbuf_tensor_at(name, shape, dt, offset=offset)

        class AsF32:

            def __init__(self, t):
                self.t = t

            def __getitem__(self, idx):
                return self.t[idx].bitcast(F32)

        class Pair:

            def __init__(self, name, shape, offset, size=None, lo_at=None):
                size = lo_at - offset if lo_at else size or 4 * width(shape[1:])
                self.hi = at(name + "_hi", shape, F32R, offset)
                self.hi32 = AsF32(self.hi)
                self.lo = at(name + "_lo", shape, F32R, offset + size)
                self.lo32 = at(name + "_was", shape, F32, offset + size)

        def width(xs):
            p = 1
            for v in xs:
                p *= v
            return p

        BASE = 16512
        A0 = BASE
        SLOT = 20480
        S = [A0 + 50016 + SLOT * k for k in range(6)]
        WA0 = S[5] + SLOT
        WB0 = WA0 + 16384
        M0 = WB0 + 16384

        CNTB = at("CNTB", [128, N], F32, M0)
        ident = at("ident", [128, 128], F32, M0 + 5024)
        identb = at("identb", [128, 128], BF16, M0 + 5536)
        causal = at("causal", [125, 125], BF16, M0 + 5792)
        m = M0 + 6048
        LNS = [at(f"LNS{r}", [125, 16], F32, m + 64 * r) for r in range(2)]
        cols = at("cols", [128, 40], F32, m + 128)
        ccol = at("ccol", [128, 56], F32, m + 288)
        gate = at("gate", [125, NT, E], F32, m + 512)
        invc = at("invc", [125, NT], F32, m + 832)
        dinc = at("dinc", [125, NT], F32, m + 896)
        ones2 = at("ones2", [128, 8], F32, m + 960)
        flags = at("flags", [1, 24], I32, m + 992)
        zero = at("zero", [128, 8], F32, m + 1088)

        xn = Pair("xn", [125, NT, D], S[0], SLOT)
        xnT = Pair("xnT", [128, FB, N], S[2], SLOT)
        rawk = at("rawk", [128, FB, D], F32, S[4])
        raw2 = at("raw2", [128, FB, D], F32, S[4] + 8192)
        vecs = at("vecs", [54, 128], F32, A0 + 40960)
        rawq = at("rawq", [128, FB, D], F32, A0 + 32768)
        MI = Pair("MI", [128, FB, D], S[4])
        G = Pair("G", [128, FB, D], S[4] + 16384)
        T0 = S[4] + 32768
        xt_ = [at(f"x_t{r}", [125, D], F32, T0 + 2048 * r) for r in range(2)]
        xnf = [at(f"xnf{r}", [125, D], F32, T0 + 4096 + 2048 * r) for r in range(2)]
        bl2B = at("bl2B", [125, D], F32, T0 + 4096)
        W1p = Pair("W1p", [128, FB, D], A0)
        W2T = Pair("W2T", [128, FB, D], A0 + 16384)
        Wvp = Pair("Wvp", [128, FB, D], WB0)
        WA = Pair("WA", [128, FB, D], WA0)
        WB = Pair("WB", [128, FB, D], WB0)
        ctxp = Pair("ctx", [128, FB, D], A0)
        kT = [at(f"kT{r}", [128, N], F32, A0 + 16384 + 5024 * r) for r in range(2)]
        ek = Pair("ek", [125, NT, 128], A0 + 26432)
        c1 = [Pair(f"c1{r}", [128, FB, 128], A0 + 36672 + 4096 * r) for r in range(2)]
        cxt = at("cxt", [128, D], F32, A0 + 44864)
        qe = [at(f"qe{r}", [125, D], F32, A0 + 16384 + 2048 * r) for r in range(2)]
        qT = [Pair(f"qT{r}", [128, FB, TILE], A0 + 26432 + 4032 * r, 2016) for r in range(2)]
        AT = at("AT", [125, NT, N], F32R, A0)
        AT32 = at("AT32", [125, NT, N], F32, A0)
        e0 = S[0]
        srcI = at("srcI", [85, 2, 125], I32, e0)
        dstI = at("dstI", [85, 2, 125], I32, e0 + 1024)
        grpI = at("grpI", [GROUPS, N], I32, e0 + 2048)
        srcR = at("srcR", [85, 2, 125], F32, e0 + 7072)
        dstR = at("dstR", [85, 2, 125], F32, e0 + 8096)
        grpR = at("grpR", [GROUPS, N], F32, e0 + 9120)
        srcF = at("srcF", [125, 170], F32, e0 + 14144)
        dstF = at("dstF", [125, 170], F32, e0 + 14848)
        gst = at("gst", [GROUPS, 8], F32, e0 + 15552)
        gD = at("gD", [GROUPS, 2 * GROUPS], F32, e0 + 15584)
        wB = at("wB", [125, 24], F32, e0 + 15744)
        bW = at("bW", [125, 16], F32, e0 + 15872)
        onesA = at("onesA", [125, 128], F32, e0 + 15936)
        e1 = S[1]
        iota = at("iota", [125, N], F16, e1)
        iotaw = at("iotaw", [125, WIN], F16, e1 + 2528)
        colsum = at("colsum", [125, N], F32, e1 + 2784)
        ohs = [at(f"ohs{r}", [125, N], BF16, e1 + 7808 + 2528 * r) for r in range(NOH)]
        ohd = [at("ohd0", [125, GT, WIN], BF16, e1 + 17920), at("ohd1", [125, GT, WIN], BF16, e0 + 16448)]
        rows = at("rows", [125, 4 * GROUPS + 4], F32, e0 + 19712)
        rel = at("rel", [125, GROUPS * GT], F32, e0 + 19008)
        wraw = [at(f"wraw{r}", [128, FB, D], F32, S[4] + 8192 * r) for r in range(2)]
        wout = [at(f"wout{r}", [128, FB, D], F32, S[4] + 16384 + 8192 * r) for r in range(2)]

        PS = ctx.enter_context(nc.psum_tensor("PS", [128, BANKS, 512], F32))

        y = Pair("y", [125, NT, D], S[0], SLOT)
        hT = Pair("hT", [128, FB, N], S[4], SLOT)
        inv0 = at("inv0", [128, N], F32, S[4])
        INVB = at("INVB", [128, N], F32, WB0)
        sc = [at(f"sc{r}", [128, 500], F32, WB0 + 5024 + 2016 * r) for r in range(2)]
        xw = [at(f"xw{r}", [125, D], F32, WA0 + 2048 * r) for r in range(2)]
        xnw = [at(f"xnw{r}", [125, D], F32, WA0 + 4096 + 2048 * r) for r in range(2)]
        BIAS = 32
        acc = at("acc", [125, NT, D], F32, S[0])
        hE = [Pair(f"hE{r}", [128, 2, N], S[4 + r], 10016) for r in range(2)]
        xm = [at(f"xm{r}", [125, D], F32, S[1] + 2048 * r) for r in range(2)]
        xnm = [at(f"xnm{r}", [125, D], F32, S[1] + 4096 + 2048 * r) for r in range(2)]
        GT_ = [WA0 + 8192, A0 + 40000]
        WgP = [Pair(f"WgP{s}", [128, FB, E], GT_[s], 128) for s in range(2)]
        b2s = [at(f"b2s{s}", [E, D], F32, GT_[s] + 256) for s in range(2)]
        bgB = [at(f"bgB{s}", [125, E], F32, GT_[s] + 2304) for s in range(2)]
        iota8 = at("iota8", [125, E], F32, GT_[0] + 2336)
        lgt = [at(f"lgt{s}", [125, NT, E], F32, GT_[s] + 2368) for s in range(2)]
        ex = [at(f"ex{s}", [125, NT, E], F32, GT_[s] + 2688) for s in range(2)]
        cand = at("cand", [125, NT, E], F32, GT_[0] + 3008)
        gred = [at(f"gred{s}", [125, 4, NT], F32, GT_[s] + 3328) for s in range(2)]
        gT = [at(f"gT{s}", [E, N], F32, (WA0, GT_[1] + 3488)[s]) for s in range(2)]
        xn2 = Pair("xn2", [125, NT, D], S[4], lo_at=S[0])
        QC = 2 * TILE
        kx = [at(f"kx{r}", [125, D], F32, S[1] + 2048 * r) for r in range(3)]
        kacc = at("kacc", [125, D], F32, S[1] + 6144)
        kp = [Pair(f"kp{r}", [125, D], S[1] + 8192 + 4096 * r) for r in range(2)]
        ksum = Pair("ksum", [128, FB, 2], S[1] + 16384)
        kv = Pair("kv", [128, FB, D], S[5])
        xq = [at(f"xq{r}", [125, D], F32, S[5] + 16384 + 2048 * r) for r in range(2)]
        q2 = [Pair(f"q2_{r}", [128, FB, QC], S[1] + 8064 * r, 4032) for r in range(2)]
        zT = Pair("zT", [128, FB, N], S[2], SLOT)
        h1T = Pair("h1T", [128, FB, N], S[1], lo_at=S[5])
        y3 = Pair("y3", [125, NT, D], S[4], lo_at=S[0])
        xg = [at(f"xg{r}", [125, D], F32, S[1] + 2048 * r) for r in range(2)]
        xnA = [at(f"xnA{r}", [125, D], F32, S[1] + 4096 + 2048 * r) for r in range(2)]
        xnB = [at(f"xnB{r}", [125, D], F32, S[1] + 8192 + 2048 * r) for r in range(2)]
        b2B = at("b2B", [125, D], F32, S[1] + 12288)
        gt_ = at("gt", [125, D], F32, S[1] + 14336)
        hxT = Pair("hxT", [128, FB, N], S[2], SLOT)
        QA = at("QA", [128, HEADS, N], F32R, A0)
        QA32 = AsF32(QA)
        KA = at("KA", [128, HEADS, N], F32R, S[0])
        KA32 = AsF32(KA)
        KLO = at("KLO", [128, FB, N], F32R, S[4])
        V32 = at("V32", [125, NT, D], F32, S[5])
        V = Pair("V", [125, NT, D], S[2], SLOT)
        sqr = [at(f"sqr{r}", [125, D], F32, A0 + 40000 + 2048 * r) for r in range(2)]
        unit = [at(f"unit{r}", [125, D], F32, A0 + 44096 + 2048 * r) for r in range(2)]
        P = [at(f"P{r}", [125, N], F32, A0 + 40000 + 5024 * r) for r in range(2)]
        NPT = 4
        PT = [Pair(f"PT{r}", [125, 4, TILE], WB0 + 4096 * r, 2048) for r in range(NPT)]
        O = at("O", [125, NT, D], F32, S[5])
        OT = Pair("OT", [128, FB, N], S[0], SLOT)
        yT = Pair("yT", [128, FB, N], S[2], SLOT)
        def dram(name, shape):
            return nc.dram_tensor(name, shape, F32, kind="Internal").ap()

        torch_w = {"Wl1": L0_gnn_Wl1, "Wr1": L0_gnn_Wr1, "Wl2": L0_gnn_Wl2, "Wr2": L0_gnn_Wr2,
                   "Wqk0": L1_mix_W_qk[0:D, :], "Wqk1": L1_mix_W_qk[D:2 * D, :]}
        WT = {k: dram("WT_" + k, (D, D)) for k in torch_w}
        xa = dram("x_mixed", (N, D))
        xb = dram("x_r2", (N, D))
        xc = dram("x_one", (N, D))
        xd = dram("x_two", (N, D))
        xe = dram("x_mix1", (N, D))
        xf = dram("x_three", (N, D))

        def sem(name):
            return ctx.enter_context(nc.semaphore(name))

        filled = [sem(f"filled{b}") for b in range(BANKS)]
        drained = [sem(f"drained{b}") for b in range(BANKS)]
        hi_done = sem("hi_done")
        dve_step, act_step, pool_step = sem("dve_step"), sem("act_step"), sem("pool_step")
        const_ready = sem("const_ready")
        rawk_in, raw2_in, rawq_in = sem("rawk_in"), sem("raw2_in"), sem("rawq_in")
        wraw_in = [sem("wraw_in0"), sem("wraw_in1")]
        unit_in = [sem("unit_in0"), sem("unit_in1")]
        unit_hi, unit_ready = sem("unit_hi"), sem("unit_ready")
        x_in = [sem("x_in0"), sem("x_in1")]
        x_out = [sem("x_out0"), sem("x_out1")]
        ln_var, ln_std, ln_xnf, ln_hi = sem("ln_var"), sem("ln_std"), sem("ln_xnf"), sem("ln_hi")
        ln_lo = sem("ln_lo")
        mi_sum, mi_hi, mi_ready = sem("mi_sum"), sem("mi_hi"), sem("mi_ready")
        k_max = sem("k_max")
        cx_hi, cx_ready = sem("cx_hi"), sem("cx_ready")
        q_max, q_norm = sem("q_max"), sem("q_norm")
        vecs_in, bl2_in = sem("vecs_in"), sem("bl2_in")
        wt_out = [sem("wt_out0"), sem("wt_out1")]
        idx_in, idx_f = sem("idx_in"), sem("idx_f")
        edge_ready = sem("edge_ready")
        src_ready, dst_ready = sem("src_ready"), sem("dst_ready")
        edge_tiles, window_free = sem("edge_tiles"), sem("window_free")
        dst_squared, all_squared = sem("dst_squared"), sem("all_squared")
        all_src, all_dst, all_tiles, all_taken, all_rel = sem("all_src"), sem("all_dst"), sem("all_tiles"), sem("all_taken"), sem("all_rel")
        at_zero, at_built = sem("at_zero"), sem("at_built")
        sum_ready, deg_ready, deg_root = sem("sum_ready"), sem("deg_ready"), sem("deg_root")
        inv_ready = sem("inv_ready")

        inv_placed, a1_sum, a1_hi, a1_ready = sem("inv_placed"), sem("a1_sum"), sem("a1_hi"), sem("a1_ready")
        moe_in = [sem("moe0_in"), sem("moe1_in")]
        iota_ready = sem("iota_ready")
        wg_hi, wg_ready = sem("wg_hi"), sem("wg_ready")
        lg_less, lg_exp, gate_ready = sem("lg_less"), sem("lg_exp"), sem("gate_ready")
        hid_done, hid_hi, hid_ready = sem("hid_done"), sem("hid_hi"), sem("hid_ready")
        bias_placed = sem("bias_placed")
        x2_sum, xn2_lo = sem("x2_sum"), sem("xn2_lo")
        k_min, k_exped, k_hi, k_ready, k_used = (sem(n) for n in ("k_min", "k_exped", "k_hi", "k_ready", "k_used"))
        q_min, q_exped, q_hi, q_ready = (sem(n) for n in ("q_min", "q_exped", "q_hi", "q_ready"))
        kacc_done, self_loops = sem("kacc_done"), sem("self_loops")
        xs_whole, xs_scaled, xs_hi, xs_ready = (sem(n) for n in ("xs_whole", "xs_scaled", "xs_hi", "xs_ready"))
        z_hi, z_ready = sem("z_hi"), sem("z_ready")
        h1_hi, h1_ready = sem("h1_hi"), sem("h1_ready")
        y3_hi, y3_ready = sem("y3_hi"), sem("y3_ready")
        b2_in, x3_sum = sem("b2_in"), sem("x3_sum")
        hx_hi, hx_ready = sem("hx_hi"), sem("hx_ready")
        v_hi, v_ready = sem("v_hi"), sem("v_ready")
        squared, unit_sum, unit_root, unit_done = (sem(n) for n in ("squared", "unit_sum", "unit_root", "unit_done"))
        k_twice = sem("k_twice")
        s_max, pt_used = sem("s_max"), sem("pt_used")
        place, uses = {}, [0] * BANKS

        def plan(key, bank_):
            uses[bank_] += 1
            assert key not in place
            place[key] = (bank_, uses[bank_])

        ring_at = [0]

        def plan_ring(keys, ring=tuple(range(BANKS))):
            for key in keys:
                plan(key, ring[ring_at[0] % len(ring)])
                ring_at[0] += 1

        plan_ring([("xt", 0, i) for i in range(NT)])
        plan_ring([("wt", w, ib) for w in ("k", "2") for ib in range(FB)])
        plan_ring([("vec",)])
        plan_ring([("mi", b) for b in range(FB)])
        plan_ring([("g", b) for b in range(FB)])
        plan_ring([("wt", "q", ib) for ib in range(FB)])
        for b in range(FB + 1):
            if b == 0:
                plan_ring([("k", 0, c) for c in range(3)])
            if b + 1 < FB:
                plan_ring([("k", b + 1, c) for c in range(3)])
            if b < FB:
                plan_ring([("kt", b, q) for q in range(3)])
                plan_ring([("c1", b)])
            if b > 0:
                plan_ring([("cx", b - 1)])
        plan_ring([("q", 0)])
        for i in range(NT):
            if i + 1 < NT:
                plan_ring([("q", i + 1)])
            plan_ring([("qt", i), ("mo", i)])
        plan_ring([("wt", w, ib) for w in torch_w for ib in range(FB)])
        plan_ring([("ix",), ("wv",)])
        before_edges = list(uses)
        plan_ring([("cb", 0), ("cb", 1), ("cb", 2), ("cc",)])

        plan_ring([("y1", i) for i in range(NT)])
        plan_ring([("r1", f, c) for f in range(FB) for c in range(3)])
        plan_ring([("a1", f, c) for f in range(FB) for c in range(3)])
        plan_ring([("y2", i) for i in range(NT)])
        plan_ring([("r2", i) for i in range(NT)])
        for i in range(NT + 1):
            if i < NT:
                plan_ring([("a2", i)])
            if i >= 1:
                plan_ring([("xt", 1, i - 1)])
        lnno = {(s, i): NT * s + i for s in range(3) for i in range(NT)}
        lnno |= {(3 + s, i): 3 * NT + 2 * i + s for s in range(2) for i in range(NT)}
        UNITS = [("W1", 0), ("Wv", 1), ("Wl1", 0), ("Wr1", 1), ("Wl2", 0), ("Wr2", 1)]
        UNITS += [(f"m0e{e}", 1 - e % 2) for e in range(E)]
        UNITS += [("Wqk1", 1), ("Wqk0", 0), ("gW1a", 1), ("gW2a", 0), ("gW1b", 1), ("gW2b", 0)]
        UNITS += [("aWv", 1), ("aWq", 0), ("aWk", 1), ("aWo", 0)]
        UNITS += [(f"m1e{e}", 1 - e % 2) for e in range(E)]
        X_LOADS = ["x", "xmix", "xr2", "xa2", "xm0", "xq", "xa3", "xm1"]
        X_STORES = ["xmix", "xr2", "xa2", "xm0", "xq", "xa3", "xm1"]
        def plan_moe(s):
            plan_ring([("lg", s)])
            plan_ring([("gt", s, q) for q in range(3)])
            plan_ring([("ac", s, i) for i in range(NT)])
            hd = lambda e: plan_ring([("hd", s, e, f, c) for f in range(2) for c in range(3)])
            eo = lambda e: plan_ring([("eo", s, e, i) for i in range(NT)])
            hd(0)
            for h, o in ((1, 0), (2, 1)):
                hd(h)
                eo(o)
            for b in range(BANKS):
                uses[b] += 4 * (PAIRS - 1)
            hd(7)
            eo(6)
            if s == 1:
                eo(7)
            else:
                for i in range(NT + 1):
                    if i < NT:
                        plan_ring([("eo", s, 7, i)])
                    if i >= 1:
                        plan_ring([("xt", 2, i - 1)])

        PAIRS = E // 2 - 1
        plan_moe(0)
        LOW = (0, 1, 2, 3)
        for b in range(FB):
            plan(("kv", b), 4 + b)
        plan_ring([("k2", i) for i in range(NT)], LOW)
        plan(("ks",), 3)
        ring_at[0] = 0
        NQ = N // QC
        for g in range(NQ + 1):
            if g < NQ:
                plan_ring([("q2", g, f) for f in range(FB)])
            if g > 0:
                plan_ring([(k, i) for i in (2 * g - 2, 2 * g - 1) for k in ("dn", "mx")])
        plan_ring([("z", f, c) for f in range(FB) for c in range(3)])
        for hf in range(2):
            plan_ring([("h1", hf, f, c) for f in range(FB) for c in range(3)])
            plan_ring([("yy", hf, i) for i in range(NT)])
        for i in range(NT + 1):
            if i < NT:
                plan_ring([("a3", i)])
            if i >= 1:
                plan_ring([("xt", 4, i - 1)])
        HX = [(f, c) for f in range(FB) for c in range(3)]
        plan_ring([("pv", i) for i in range(NT)])
        for w in ("q", "k"):
            for i in range(NT + 1):
                if i < NT:
                    plan_ring([("p" + w, i)])
                if i >= 1:
                    plan_ring([("t" + w, i - 1)])
        ROWS = [(i, h) for i in range(NT) for h in range(HEADS)]
        SEEN = [-(-(i + 1) // 4) for i, h in ROWS]
        GROUPED = [(n, q) for n in range(len(ROWS)) for q in range(SEEN[n])]
        LAG = 2
        first_of = {n: g for g, (n, q) in reversed(list(enumerate(GROUPED)))}

        def tiles_of(n, q):
            return range(4 * q, min(4 * q + 4, ROWS[n][0] + 1))

        def plan_scores(n):
            plan_ring([("s", n, q) for q in range(SEEN[n])], (0, 1, 2, 3, 4))

        plan_scores(0)
        for g, (n, q) in enumerate(GROUPED):
            if q == 0 and n + 1 < len(ROWS):
                plan_scores(n + 1)
            plan(("pt", n, q), 5 + g % 2)
        for n in range(len(ROWS)):
            plan(("o", n), 7)
        plan_ring([("ot", i) for i in range(NT)])
        plan_ring([("wo", f, c) for f, c in HX])
        plan_moe(1)

        def bank(key):
            return PS[:, place[key][0], :]

        def completed(eng, key, later=0):
            b, n = place[key]
            eng.wait_ge(filled[b], later + n)

        def carried(eng, key, later=0):
            b, n = place[key]
            eng.wait_ge(drained[b], later + n)

        def drain(ins, key):
            ins.then_inc(drained[place[key][0]], 1)

        def natural(w):
            return w.rearrange("(b p) n -> p b n", p=128)

        def row(v, parts=TILE):
            return v.rearrange("(a n) -> a n", a=1).broadcast_to((parts, v.shape[0]))

        xin = x.rearrange("(t p) d -> t p d", p=TILE)
        xav = xa.rearrange("(t p) d -> t p d", p=TILE)

        x_no = {}
        for key in [(s, i) for s in X_LOADS for i in range(NT)]:
            n = len(x_no)
            x_no[key] = (n % 2, n // 2 + 1)
        out_no = {}
        for key in [(s, i) for s in X_STORES for i in range(NT)]:
            n = len(out_no)
            out_no[key] = (n % 2, n // 2 + 1)

        def x_stored(eng, key):
            r, n = out_no[key]
            eng.wait_ge(x_out[r], 16 * n)

        unit_no, landed = {}, [0, 0]
        for name, region in UNITS:
            landed[region] += 32 if name[0] == "m" else 16
            unit_no[name] = (region, landed[region], len(unit_no) + 1)

        def unit_pair(name):
            return {"W1": W1p, "Wv": Wvp}.get(name, (WA, WB)[unit_no[name][0]])

        def unit_split(eng, name):
            eng.wait_ge(unit_ready, unit_no[name][2])

        def x_landed(eng, key):
            r, n = x_no[key]
            eng.wait_ge(x_in[r], 16 * n)

        act_his, dve_los = [], []

        block = ctx.enter_context(nc.Block())

        @block.sync
        def _(sp):
            def load_x(key, view, i):
                r, n = x_no[key]
                sp.dma_start(xt_[r][:], view[i]).then_inc(x_in[r], 16)

            load_x(("x", 0), xin, 0)
            load_x(("x", 1), xin, 1)
            sp.dma_start(rawk[:], natural(L0_mix_Wk)).then_inc(rawk_in, 16)
            sp.dma_start(raw2[:], natural(L0_mix_W2)).then_inc(raw2_in, 16)
            sp.dma_start(W1p.lo32[:], natural(L0_mix_W1)).then_inc(unit_in[0], 16)
            sp.dma_start(Wvp.lo32[:], natural(L0_mix_Wv)).then_inc(unit_in[1], 16)
            sp.dma_start(rawq[:], natural(L0_mix_Wq)).then_inc(rawq_in, 16)
            v2 = lambda v: v.rearrange("(a p) -> a p", p=128)
            for name, v in (("bl1", v2(L0_gnn_bl1)), ("gb1", v2(L1_gnn_b1)),
                            ("m0b1", L0_ffn_b1.rearrange("e (f p) -> (e f) p", p=128)),
                            ("m1b1", L1_ffn_b1.rearrange("e (f p) -> (e f) p", p=128)),
                            ("ln_g", v2(L1_ffn_ln_g)), ("ln_b", v2(L1_ffn_ln_b))):
                sp.dma_start(vecs[COL[name]:COL[name] + v.shape[0], :], v).then_inc(vecs_in, 16)
            for name, v in (("qn_g", L1_ffn_qn_g), ("kn_g", L1_ffn_kn_g)):
                for h in range(2):
                    sp.dma_start(vecs[COL[name]:COL[name] + 1, h * DH:(h + 1) * DH],
                                 v.rearrange("(a n) -> a n", a=1)).then_inc(vecs_in, 16)
            for i in range(2, NT):
                sp.wait_ge(ln_xnf, i - 1)
                load_x(("x", i), xin, i)
            completed(sp, ("xt", 0, NT - 1))
            sp.wait_ge(ln_lo, NT)
            sp.dma_start(bl2B[:], row(L0_gnn_bl2)).then_inc(bl2_in, 16)
            for i in range(NT + 1):
                if i < NT:
                    if i >= 2:
                        sp.wait_ge(x_out[i % 2], 16 * (i // 2))
                    load_x(("xmix", i), xin, i)
                if i >= 1:
                    carried(sp, ("mo", i - 1))
                    sp.dma_start(xav[i - 1], xt_[(i - 1) % 2][:]).then_inc(x_out[(i - 1) % 2], 16)
            hv = lambda a: a.rearrange("(h p c) -> p h c", h=2, c=125)
            completed(sp, ("c1", FB - 1))
            sp.dma_start(srcI[:], hv(src)).then_inc(idx_in, 16)
            sp.dma_start(dstI[:], hv(dst)).then_inc(idx_in, 16)
            sp.dma_start(grpI[:], dst.rearrange("(g c) -> g c", g=GROUPS)).then_inc(idx_in, 16)
            completed(sp, ("mo", NT - 1))
            names = list(torch_w)
            for n in range(len(names) + 1):
                if n < len(names):
                    if n >= 2:
                        completed(sp, ("wt", names[n - 2], FB - 1))
                    sp.dma_start(wraw[n % 2][:], natural(torch_w[names[n]])).then_inc(wraw_in[n % 2], 16)
                if n >= 1:
                    for ib in range(FB):
                        carried(sp, ("wt", names[n - 1], ib))
                    sp.dma_start(natural(WT[names[n - 1]]), wout[(n - 1) % 2][:]).then_inc(wt_out[(n - 1) % 2], 16)
            def load_unit(name, view):
                region = unit_no[name][0]
                sp.dma_start((WA, WB)[region].lo32[:], view).then_inc(unit_in[region], 16)

            def expert_into(region, W1, W2, e):
                flat = (WA, WB)[region].lo32[:].rearrange("p b n -> p (b n)")
                sp.dma_start(flat[:, 0:4 * HID].rearrange("p (b n) -> p b n", b=4),
                             W1[bass.ds(e, 1)].rearrange("a (b p) n -> p (a b) n", p=128))\
                    .then_inc(unit_in[region], 16)
                sp.dma_start(flat[:, 4 * HID:8 * HID].rearrange("p (b n) -> p b n", b=2),
                             W2[bass.ds(e, 1)].rearrange("a (b p) n -> p (a b) n", p=128))\
                    .then_inc(unit_in[region], 16)

            def load_transposed(name):
                n = names.index(name)
                sp.wait_ge(wt_out[n % 2], 16 * (n // 2 + 1))
                load_unit(name, natural(WT[name]))

            def load_tile(stage, i, view, ring):
                r, n = x_no[(stage, i)]
                sp.dma_start(ring[r][:], view[i]).then_inc(x_in[r], 16)

            def store_tile(stage, i, view, ring):
                r, n = out_no[(stage, i)]
                sp.dma_start(view[i], ring[r][:]).then_inc(x_out[r], 16)

            completed(sp, ("k", FB - 1, 2))
            load_transposed("Wl1")
            load_transposed("Wr1")
            completed(sp, ("y1", NT - 1))
            load_transposed("Wl2")
            sp.wait_ge(a1_ready, 3 * FB)
            load_transposed("Wr2")
            completed(sp, ("y2", NT - 1))
            xbv, xcv = (a.rearrange("(t p) d -> t p d", p=TILE) for a in (xb, xc))
            for i in range(NT + 1):
                if i < NT:
                    if i >= 2:
                        x_stored(sp, ("xr2", i - 2))
                    x_stored(sp, ("xmix", i))
                    load_tile("xr2", i, xav, xw)
                if i >= 1:
                    carried(sp, ("r2", i - 1))
                    store_tile("xr2", i - 1, xbv, xw)
            sp.dma_start(WgP[0].lo32[:], natural(L0_ffn_Wg)).then_inc(moe_in[0], 16)
            sp.dma_start(b2s[0][:], L0_ffn_b2).then_inc(moe_in[0], 16)
            sp.dma_start(bgB[0][:], row(L0_ffn_bg)).then_inc(moe_in[0], 16)
            expert_into(1, L0_ffn_W1, L0_ffn_W2, 0)
            for i in range(NT + 1):
                if i < NT:
                    if i >= 2:
                        x_stored(sp, ("xa2", i - 2))
                        sp.wait_ge(ln_xnf, lnno[(1, i - 2)] + 1)
                    x_stored(sp, ("xr2", i))
                    load_tile("xa2", i, xbv, xw)
                if i >= 1:
                    carried(sp, ("a2", i - 1))
                    store_tile("xa2", i - 1, xcv, xw)
            def load_experts(s, W1, W2):
                with sp.Fori(0, PAIRS) as k:
                    completed(sp, ("eo", s, 0, NT - 1), k * 4)
                    expert_into(1, W1, W2, k * 2 + 2)
                    completed(sp, ("eo", s, 1, NT - 1), k * 4)
                    expert_into(0, W1, W2, k * 2 + 3)

            completed(sp, ("xt", 1, NT - 1))
            x_stored(sp, ("xa2", NT - 2))
            x_stored(sp, ("xa2", NT - 1))
            completed(sp, ("ac", 0, NT - 1))
            expert_into(0, L0_ffn_W1, L0_ffn_W2, 1)
            load_experts(0, L0_ffn_W1, L0_ffn_W2)
            completed(sp, ("eo", 0, E - 2, NT - 1))
            load_transposed("Wqk1")
            xdv = xd.rearrange("(t p) d -> t p d", p=TILE)
            for i in range(NT + 1):
                if i < NT:
                    if i >= 2:
                        x_stored(sp, ("xm0", i - 2))
                        sp.wait_ge(ln_xnf, lnno[(2, i - 2)] + 1)
                    load_tile("xm0", i, xcv, xm)
                if i >= 1:
                    sp.wait_ge(x2_sum, i)
                    store_tile("xm0", i - 1, xdv, xm)
            completed(sp, ("eo", 0, E - 1, NT - 1))
            load_transposed("Wqk0")
            completed(sp, ("k2", NT - 1))
            load_unit("gW1a", natural(L1_gnn_W1[:, 0:D]))
            xev, xfv = (a.rearrange("(t p) d -> t p d", p=TILE) for a in (xe, xf))
            for i in range(NT + 1):
                if i < NT:
                    if i >= 2:
                        x_stored(sp, ("xq", i - 2))
                    if i < 2:
                        completed(sp, ("eo", 0, E - 1, NT - 1))
                    x_stored(sp, ("xm0", i))
                    load_tile("xq", i, xdv, xq)
                if i >= 1:
                    carried(sp, ("mx", i - 1))
                    store_tile("xq", i - 1, xev, xq)
                if i == NT - 1:
                    completed(sp, ("q2", NQ - 1, FB - 1))
                    load_unit("gW2a", natural(L1_gnn_W2[0:D, :]))
            completed(sp, ("h1", 0, FB - 1, 2))
            load_unit("gW1b", natural(L1_gnn_W1[:, D:2 * D]))
            completed(sp, ("yy", 0, NT - 1))
            load_unit("gW2b", natural(L1_gnn_W2[D:2 * D, :]))
            completed(sp, ("h1", 1, FB - 1, 2))
            load_unit("aWv", natural(L1_ffn_Wv))
            completed(sp, ("yy", 1, NT - 1))
            load_unit("aWq", natural(L1_ffn_Wq))
            sp.dma_start(b2B[:], row(L1_gnn_b2)).then_inc(b2_in, 16)
            for i in range(NT + 1):
                if i < NT:
                    if i >= 2:
                        x_stored(sp, ("xa3", i - 2))
                        sp.wait_ge(ln_xnf, lnno[(3, i - 2)] + 1)
                    x_stored(sp, ("xq", i))
                    load_tile("xa3", i, xev, xg)
                if i >= 1:
                    sp.wait_ge(x3_sum, i)
                    store_tile("xa3", i - 1, xfv, xg)
            completed(sp, ("pv", NT - 1))
            load_unit("aWk", natural(L1_ffn_Wk))
            completed(sp, ("pq", NT - 1))
            load_unit("aWo", natural(L1_ffn_Wo))
            completed(sp, ("pt", len(ROWS) - 1, SEEN[-1] - 1))
            sp.dma_start(WgP[1].lo32[:], natural(L1_ffn_gate_W)).then_inc(moe_in[1], 16)
            sp.dma_start(b2s[1][:], L1_ffn_b2).then_inc(moe_in[1], 16)
            sp.dma_start(bgB[1][:], row(L1_ffn_gate_b)).then_inc(moe_in[1], 16)
            completed(sp, ("o", len(ROWS) - 1))
            expert_into(1, L1_ffn_W1, L1_ffn_W2, 0)
            completed(sp, ("wo", FB - 1, 2))
            expert_into(0, L1_ffn_W1, L1_ffn_W2, 1)
            load_experts(1, L1_ffn_W1, L1_ffn_W2)
            outv = out.rearrange("(t p) d -> t p d", p=TILE)
            for i in range(NT + 1):
                if i < NT:
                    if i >= 2:
                        x_stored(sp, ("xm1", i - 2))
                    x_stored(sp, ("xa3", i))
                    load_tile("xm1", i, xfv, xm)
                if i >= 1:
                    sp.wait_ge(x2_sum, NT + i)
                    store_tile("xm1", i - 1, outv, xm)
            x_stored(sp, ("xm1", NT - 2))
            x_stored(sp, ("xm1", NT - 1))

        @block.gpsimd
        def _(pool):
            steps = [0]

            def link(ins):
                steps[0] += 1
                ins.then_inc(pool_step, 1)
                pool.wait_ge(pool_step, steps[0])

            link(pool.memset(ident[:], 0.0))
            pool.affine_select(out=ident[:], in_=ident[:], compare_op=ALU.not_equal, fill=1.0, base=0,
                               pattern=[[-1, 128]], channel_multiplier=1).then_inc(const_ready, 1)
            pool.wait_ge(const_ready, 1)
            link(pool.memset(ones2[:], 1.0))
            link(pool.memset(zero[:], 0.0))
            link(pool.memset(causal[:], 0.0))
            link(pool.affine_select(out=causal[:], in_=causal[:], compare_op=ALU.is_ge, fill=-1e30, base=0,
                                    pattern=[[-1, 125]], channel_multiplier=1))
            link(pool.tensor_copy(identb[:], ident[:]))

            def rounded(pair):
                was = pair.lo32[:]
                none = zero[:, 0:1].broadcast_to((128, was.shape[1] * was.shape[2]))\
                    .rearrange("p (b n) -> p b n", b=was.shape[1])
                return pool.tensor_tensor(pair.hi[:], was, none, ALU.add)

            def split(name):
                region, landed_, _ = unit_no[name]
                pair = unit_pair(name)
                pool.wait_ge(unit_in[region], landed_)
                rounded(pair).then_inc(unit_hi, 1)
                pool.wait_ge(unit_hi, unit_no[name][2])
                pool.tensor_tensor(pair.lo[:], pair.lo32[:], pair.hi32[:], ALU.subtract).then_inc(unit_ready, 1)

            split("W1")
            split("Wv")

            completed(pool, ("c1", FB - 1))
            link(pool.iota(iota[:], pattern=[[1, N]], base=0, channel_multiplier=0,
                           allow_small_or_imprecise_dtypes=True))
            link(pool.iota(bW[:, 0:NT], pattern=[[WIN, NT]], base=0, channel_multiplier=0,
                           allow_small_or_imprecise_dtypes=True))
            link(pool.iota(iotaw[:], pattern=[[1, WIN]], base=0, channel_multiplier=0,
                           allow_small_or_imprecise_dtypes=True))
            link(pool.memset(bW[:, NT - 1:NT], float(LASTWIN)))
            pool.memset(onesA[:], 1.0).then_inc(const_ready, 1)
            completed(pool, ("mo", NT - 1))
            pool.memset(AT[:].bitcast(F32), 0.0).then_inc(at_zero, 1)

            for name in ("Wl1", "Wr1", "Wl2", "Wr2"):
                split(name)
            def split_gate_weights(s):
                pool.wait_ge(moe_in[s], 48)
                rounded(WgP[s]).then_inc(wg_hi, 1)
                pool.wait_ge(wg_hi, s + 1)
                pool.tensor_tensor(WgP[s].lo[:], WgP[s].lo32[:], WgP[s].hi32[:], ALU.subtract).then_inc(wg_ready, 1)

            def split_experts(s):
                with pool.Fori(0, E // 2) as k:
                    for e in range(2):
                        region, landed_, n = unit_no[f"m{s}e{e}"]
                        pair = (WA, WB)[region]
                        pool.wait_ge(unit_in[region], k * 32 + landed_)
                        rounded(pair).then_inc(unit_hi, 1)
                        pool.wait_ge(unit_hi, k * 2 + n)
                        pool.tensor_tensor(pair.lo[:], pair.lo32[:], pair.hi32[:], ALU.subtract)\
                            .then_inc(unit_ready, 1)

            completed(pool, ("y2", NT - 1))
            pool.iota(iota8[:], pattern=[[1, E]], base=0, channel_multiplier=0,
                      allow_small_or_imprecise_dtypes=True).then_inc(iota_ready, 1)
            split_gate_weights(0)
            split_experts(0)
            split("Wqk1")
            pool.wait_ge(xn2_lo, NT)
            completed(pool, ("xt", 2, NT - 1))
            pool.memset(kacc[:], 0.0).then_inc(kacc_done, 1)
            for i in range(NT):
                if i == 1:
                    split("Wqk0")
                carried(pool, ("k2", i))
                pool.wait_ge(kacc_done, i + 1)
                pool.tensor_tensor(kacc[:], kacc[:], kx[i % 3][:], ALU.add).then_inc(kacc_done, 1)
            completed(pool, ("kv", FB - 1))
            for i in range(NT):
                pool.tensor_tensor(xn2.lo32[:, i, :], xn2.hi32[:, i, :], xn2.lo[:, i, :].bitcast(F32), ALU.add)\
                    .then_inc(xs_whole, 1)
            for name in ("gW1a", "gW2a", "gW1b", "gW2b", "aWv", "aWq", "aWk"):
                split(name)
            completed(pool, ("pk", NT - 1))
            none = zero[0:TILE, 0:1].broadcast_to((TILE, D))
            for i in range(NT):
                pool.tensor_tensor(V.hi[:, i, :], V32[:, i, :], none, ALU.add).then_inc(v_hi, 1)
                pool.wait_ge(v_hi, i + 1)
                pool.tensor_tensor(V.lo[:, i, :], V32[:, i, :], V.hi32[:, i, :], ALU.subtract).then_inc(v_ready, 1)
            split("aWo")
            split_gate_weights(1)
            split_experts(1)

        @block.scalar
        def _(act):
            def hi(key, dst_, src_):
                completed(act, key)
                act_his.append(key)
                act.activation(dst_, src_, ACT.Copy).then_inc(hi_done, 1)

            def ln_sqrt(s, i):
                n = lnno[(s, i)]
                st = LNS[n % 2]
                act.wait_ge(ln_var, n + 1)
                act.activation(st[:, 9:10], st[:, 8:9], ACT.Sqrt).then_inc(ln_std, 1)

            def ln_T_hi(s, i, T):
                key = ("xt", s, i)
                hi(key, T.hi[:, :, i * TILE:(i + 1) * TILE],
                   bank(key)[:, 0:FB * TILE].rearrange("p (b n) -> p b n", b=FB))

            ln_sqrt(0, 0)
            for i in range(NT + 1):
                if i + 1 < NT:
                    ln_sqrt(0, i + 1)
                if i < NT:
                    act.wait_ge(ln_xnf, i + 1)
                    act.activation(xn.hi[:, i, :], xnf[i % 2][:], ACT.Copy).then_inc(ln_hi, 1)
                if i >= 1:
                    ln_T_hi(0, i - 1, xnT)
            for w, W in (("k", WA), ("2", W2T)):
                for ib in range(FB):
                    hi(("wt", w, ib), W.hi[:, ib, :], bank(("wt", w, ib)))
            for b in range(FB):
                act.wait_ge(mi_sum, b + 1)
                act.activation(MI.hi[:, b, :], MI.lo32[:, b, :], ACT.Copy).then_inc(mi_hi, 1)
            for b in range(FB):
                hi(("g", b), G.hi[:, b, :], bank(("g", b)))
            for ib in range(FB):
                hi(("wt", "q", ib), WB.hi[:, ib, :], bank(("wt", "q", ib)))

            def k_exp(b):
                act.wait_ge(k_max, b + 1)
                if b >= 2:
                    completed(act, ("kt", b - 2, 2))
                o_ = 8 * (b % 2)
                for c, (o, w) in enumerate(CH):
                    drain(act.activation(kT[b % 2][:, o:o + w], bank(("k", b, c))[:, 0:w], ACT.Exp,
                                         bias=cols[:, o_ + 3:o_ + 4],
                                         accum_out=cols[:, o_ + 4 + c:o_ + 5 + c]), ("k", b, c))

            k_exp(0)
            for b in range(FB + 1):
                if b + 1 < FB:
                    k_exp(b + 1)
                if b < FB:
                    for q in range(3):
                        n = min(4, NT - 4 * q)
                        key = ("kt", b, q)
                        hi(key, ek.hi[:, 4 * q:4 * q + n, :],
                           bank(key)[0:TILE, 0:128 * n].rearrange("p (t d) -> p t d", t=n))
                    hi(("c1", b), c1[b % 2].hi[:], bank(("c1", b)).rearrange("p (c d) -> p c d", c=FB))
                if b > 0:
                    carried(act, ("cx", b - 1))
                    act.activation(ctxp.hi[:, b - 1, :], cxt[:], ACT.Copy).then_inc(cx_hi, 1)

            def q_exp(i):
                act.wait_ge(q_max, i + 1)
                if i >= 2:
                    completed(act, ("qt", i - 2))
                c = 16 + 4 * (i % 2)
                drain(act.activation(qe[i % 2][:], bank(("q", i))[0:TILE, :], ACT.Exp,
                                     bias=cols[0:TILE, c:c + 1], accum_out=cols[0:TILE, c + 1:c + 2]), ("q", i))

            q_exp(0)
            for i in range(NT):
                if i + 1 < NT:
                    q_exp(i + 1)
                if i >= 2:
                    completed(act, ("mo", i - 2))
                hi(("qt", i), qT[i % 2].hi[:], bank(("qt", i))[:, 0:FB * TILE].rearrange("p (b n) -> p b n", b=FB))
            for n, name in enumerate(torch_w):
                for ib in range(FB):
                    completed(act, ("wt", name, ib))
                    if n >= 2 and ib == 0:
                        act.wait_ge(wt_out[n % 2], 16 * (n // 2))
                    drain(act.activation(wout[n % 2][:, ib, :], bank(("wt", name, ib)), ACT.Copy), ("wt", name, ib))

            act.wait_ge(edge_ready, 1)
            fit = act.value_load(flags[0:1, 20:21], min_val=0, max_val=1)

            def onehot_dst(g, r, square, ready):
                for t in range(GT):
                    ins = act.activation(ohd[r][:, t, :], iotaw[:], ACT.Square, bias=rel[:, bass.ds(g * GT + t, 1)])
                ins.then_inc(square, 1)
                act.wait_ge(square, g + 1)
                act.activation(ohd[r][:], ohd[r][:], ACT.Relu, bias=1.0, scale=-1.0).then_inc(ready, 1)

            with act.If(fit == 1):
                with act.Fori(0, GROUPS // 2) as k:
                    for r in range(2):
                        act.wait_ge(edge_tiles, k * (2 * GT) + (r * GT + PRIME - GT))
                        onehot_dst(k * 2 + r, r, dst_squared, dst_ready)
                act.wait_ge(edge_tiles, (GROUPS - 1) * GT + PRIME - GT)
                onehot_dst(GROUPS - 1, 0, dst_squared, dst_ready)
            with act.Else():
                with act.Fori(0, NT) as w:
                    act.activation(rel[:], dstF[:], ACT.Identity, bias=bW[:, bass.ds(w, 1)], scale=-1.0)\
                        .then_inc(all_rel, 1)
                    act.wait_ge(all_rel, w + 1)
                    with act.Fori(0, GROUPS) as g:
                        act.wait_ge(all_tiles, w * (GROUPS * GT) + g * GT + 1)
                        for t in range(GT):
                            ins = act.activation(ohd[0][:, t, :], iotaw[:], ACT.Square,
                                                 bias=rel[:, bass.ds(g * GT + t, 1)])
                        ins.then_inc(all_squared, 1)
                        act.wait_ge(all_squared, w * GROUPS + g + 1)
                        act.activation(ohd[0][:], ohd[0][:], ACT.Relu, bias=1.0, scale=-1.0).then_inc(all_dst, 1)
            act.wait_ge(deg_ready, 1)
            act.activation(dinc[:], dinc[:], ACT.Sqrt).then_inc(deg_root, 1)

            for i in range(NT):
                hi(("y1", i), y.hi[:, i, :], bank(("y1", i))[0:TILE, :])
            act.wait_ge(deg_ready, 2)
            act.activation(CNTB[:], CNTB[:], ACT.Sqrt).then_inc(deg_root, 1)
            completed(act, ("ix",))
            for f in range(FB):
                for c, (o, w) in enumerate(CH):
                    key = ("r1", f, c)
                    completed(act, key)
                    drain(act.activation(hT.lo32[:, f, o:o + w], bank(key)[:, 0:w], ACT.Identity,
                                         bias=ccol[:, COL["bl1"] + f:COL["bl1"] + f + 1]), key)
            n = 0
            for f in range(FB):
                for c, (o, w) in enumerate(CH):
                    n += 1
                    act.wait_ge(a1_sum, n)
                    act.activation(hT.hi[:, f, o:o + w], hT.lo32[:, f, o:o + w], ACT.Relu).then_inc(a1_hi, 1)
            for i in range(NT):
                hi(("y2", i), y.hi[:, i, :], bank(("y2", i))[0:TILE, :])
            ln_sqrt(1, 0)
            for i in range(NT):
                if i + 1 < NT:
                    ln_sqrt(1, i + 1)
                ln_T_hi(1, i, xnT)
            def gate_exp(s):
                act.wait_ge(lg_less, s + 1)
                act.activation(ex[s][:], lgt[s][:], ACT.Exp).then_inc(lg_exp, 1)

            def acc_starts(s):
                for i in range(NT):
                    key = ("ac", s, i)
                    completed(act, key)
                    drain(act.activation(acc[:, i, :], bank(key)[0:TILE, :], ACT.Copy), key)

            def hidden(s, e, e_, later, func):
                act.wait_ge(bias_placed, e_ + (E * s + 1))
                for f in range(2):
                    for c, (o, w) in enumerate(CH):
                        key = ("hd", s, e, f, c)
                        completed(act, key, later)
                        b_ = BIAS + 2 * (e % 2) + f
                        drain(act.activation(hE[e % 2].lo32[:, f, o:o + w], bank(key)[:, 0:w], func,
                                             bias=cols[:, b_:b_ + 1]), key)

            def hiddens(s, func):
                hidden(s, 0, 0, 0, func)
                with act.Fori(0, PAIRS) as k:
                    hidden(s, 1, k * 2 + 1, k * 4, func)
                    hidden(s, 2, k * 2 + 2, k * 4, func)
                hidden(s, 7, 7, 0, func)

            gate_exp(0)
            acc_starts(0)
            hiddens(0, ACT.Relu)
            ln_sqrt(2, 0)
            for i in range(NT + 1):
                if i + 1 < NT:
                    ln_sqrt(2, i + 1)
                if i < NT:
                    act.wait_ge(ln_xnf, lnno[(2, i)] + 1)
                    act.activation(xn2.hi[:, i, :], xnm[i % 2][:], ACT.Copy).then_inc(ln_hi, 1)
                if i >= 1:
                    ln_T_hi(2, i - 1, xnT)
            for i in range(NT):
                act.wait_ge(k_min, i + 1)
                act.activation(kx[i % 3][:], kx[i % 3][:], ACT.Exp).then_inc(k_exped, 1)
                carried(act, ("k2", i))
                if i >= 2:
                    act.wait_ge(k_used, i - 1)
                act.activation(kp[i % 2].hi[:], kx[i % 3][:], ACT.Copy).then_inc(k_hi, 1)
            for b in range(FB):
                hi(("kv", b), kv.hi[:, b, :], bank(("kv", b)))
            hi(("ks",), ksum.hi[:], bank(("ks",))[:, 0:2 * FB].rearrange("p (b a) -> p b a", b=FB))

            def q_exps(g, f):
                act.wait_ge(q_min, g * FB + f + 1)
                q_ = q2[g % 2].lo32[:, f, :]
                act.activation(q_, q_, ACT.Exp).then_inc(q_exped, 1)

            def q_his(g, f):
                carried(act, ("q2", g, f))
                act.activation(q2[g % 2].hi[:, f, :], q2[g % 2].lo32[:, f, :], ACT.Copy).then_inc(q_hi, 1)

            for g in range(NQ):
                for f in range(FB + 1):
                    if f < FB:
                        q_exps(g, f)
                    if f > 0:
                        q_his(g, f - 1)
                for i in (2 * g, 2 * g + 1):
                    act.wait_ge(xs_scaled, i + 1)
                    act.activation(xn2.hi[:, i, :], xn2.lo32[:, i, :], ACT.Copy).then_inc(xs_hi, 1)
            for n, (f, c) in enumerate(HX):
                o, w = CH[c]
                carried(act, ("z", f, c))
                act.activation(zT.hi[:, f, o:o + w], zT.lo32[:, f, o:o + w], ACT.Copy).then_inc(z_hi, 1)
            x_stored(act, ("xq", NT - 2))
            x_stored(act, ("xq", NT - 1))
            for hf in range(2):
                for f, c in HX:
                    o, w = CH[c]
                    key = ("h1", hf, f, c)
                    completed(act, key)
                    b_ = COL["gb1"] + FB * hf + f
                    drain(act.activation(h1T.lo32[:, f, o:o + w], bank(key)[:, 0:w], ACT.Relu,
                                         bias=ccol[:, b_:b_ + 1]), key)
                    carried(act, key)
                    act.activation(h1T.hi[:, f, o:o + w], h1T.lo32[:, f, o:o + w], ACT.Copy).then_inc(h1_hi, 1)
                for i in range(NT):
                    key = ("yy", hf, i)
                    if hf == 0:
                        completed(act, key)
                        drain(act.activation(y3.lo32[:, i, :], bank(key)[0:TILE, :], ACT.Copy,
                                             scale=dinc[:, i:i + 1]), key)
                    else:
                        carried(act, key)
                        act.activation(y3.hi[:, i, :], y3.lo32[:, i, :], ACT.Copy).then_inc(y3_hi, 1)

            def gained(i):
                key = ("xt", 4, i)
                completed(act, key)
                sl = slice(i * TILE, (i + 1) * TILE)
                for b in range(FB):
                    g_, b_ = COL["ln_g"] + b, COL["ln_b"] + b
                    ins = act.activation(hxT.lo32[:, b, sl], bank(key)[:, b * TILE:(b + 1) * TILE], ACT.Identity,
                                         bias=ccol[:, b_:b_ + 1], scale=ccol[:, g_:g_ + 1])
                drain(ins, key)
                carried(act, key)
                act.activation(hxT.hi[:, :, sl], hxT.lo32[:, :, sl], ACT.Copy).then_inc(hx_hi, 1)

            for i in range(NT):
                ln_sqrt(3, i)
                ln_sqrt(4, i)
                if i >= 1:
                    gained(i - 1)
            gained(NT - 1)
            for i in range(NT):
                completed(act, ("pv", i))
                drain(act.activation(V32[:, i, :], bank(("pv", i))[0:TILE, :], ACT.Copy), ("pv", i))

            def squares(s, w, i):
                completed(act, ("p" + w, i))
                if i >= 2 or s:
                    act.wait_ge(unit_sum, NT * s + i - 1)
                act.activation(sqr[i % 2][:], bank(("p" + w, i))[0:TILE, :], ACT.Square).then_inc(squared, 1)

            def roots(s, i):
                c = 8 * (i % 2)
                act.wait_ge(unit_sum, NT * s + i + 1)
                act.activation(cols[0:TILE, 16 + c:24 + c], cols[0:TILE, c:c + 8], ACT.Sqrt).then_inc(unit_root, 1)

            even, odd = slice(0, HEADS, 2), slice(1, HEADS, 2)
            up, down = slice(0, DH), slice(DH, 2 * DH)

            def transposed(w, i):
                return bank(("t" + w, i))[:, 0:FB * TILE].rearrange("p (b n) -> p b n", b=FB)

            for s, (w, dst_, gain) in enumerate((("q", QA, "qn_g"), ("k", KA, "kn_g"))):
                g_ = ccol[:, COL[gain]:COL[gain] + 1]
                squares(s, w, 0)
                roots(s, 0)
                for i in range(NT):
                    if i + 1 < NT:
                        squares(s, w, i + 1)
                        roots(s, i + 1)
                    key = ("t" + w, i)
                    sl = slice(i * TILE, (i + 1) * TILE)
                    completed(act, key)
                    t_ = transposed(w, i)
                    act.activation(dst_[up, even, sl], t_[up], ACT.Copy, scale=g_[up])
                    act_his.append(key)
                    act.activation(dst_[down, odd, sl], t_[down], ACT.Copy, scale=g_[down]).then_inc(hi_done, 1)
                    if w == "k":
                        act.wait_ge(hi_done, len(act_his))
                        act.activation(KA[down, even, sl], KA32[up, even, sl], ACT.Copy)
                        act.activation(KA[up, odd, sl], KA32[down, odd, sl], ACT.Copy).then_inc(k_twice, 1)

            def row_exp(n):
                act.wait_ge(s_max, n + 1)
                if n >= 2:
                    completed(act, ("pt", n - 2, SEEN[n - 2] - 1))
                c = 9 * (n % 4)
                for q in range(SEEN[n]):
                    w_ = TILE * len(tiles_of(n, q))
                    drain(act.activation(P[n % 2][:, 500 * q:500 * q + w_], bank(("s", n, q))[0:TILE, 0:w_], ACT.Exp,
                                         bias=cols[0:TILE, c + 3:c + 4], accum_out=cols[0:TILE, c + 4 + q:c + 5 + q]),
                          ("s", n, q))

            def used_by_v(eng, g):
                n, q = GROUPED[g]
                if q == SEEN[n] - 1:
                    completed(eng, ("o", n))
                else:
                    eng.wait_ge(pt_used, g - n + 1)

            completed(act, ("pk", NT - 1))
            row_exp(0)
            for g, (n, q) in enumerate(GROUPED):
                if q == 0 and n + 1 < len(ROWS):
                    row_exp(n + 1)
                if g >= NPT:
                    used_by_v(act, g - NPT)
                m = len(tiles_of(n, q))
                hi(("pt", n, q), PT[g % NPT].hi[:, 0:m, :],
                   bank(("pt", n, q))[0:TILE, 0:TILE * m].rearrange("p (t k) -> p t k", t=m))
            for i in range(NT):
                key = ("ot", i)
                hi(key, OT.hi[:, :, i * TILE:(i + 1) * TILE],
                   bank(key)[:, 0:FB * TILE].rearrange("p (b n) -> p b n", b=FB))
            for f, c in HX:
                o, w = CH[c]
                hi(("wo", f, c), yT.hi[:, f, o:o + w], bank(("wo", f, c))[:, 0:w])
            gate_exp(1)
            acc_starts(1)
            hiddens(1, ACT.Gelu_apprx_tanh)

        @block.vector
        def _(dve):
            steps = [0]

            def link(ins):
                steps[0] += 1
                ins.then_inc(dve_step, 1)
                dve.wait_ge(dve_step, steps[0])

            def lo(key, dst_, src_, hi_):
                dve_los.append(key)
                dve.wait_ge(hi_done, len(dve_los))
                drain(dve.tensor_tensor(dst_, src_, hi_, ALU.subtract), key)

            def ln_stats(s, i, x_):
                n = lnno[(s, i)]
                st = LNS[n % 2]
                if n >= 2:
                    dve.wait_ge(ln_xnf, n - 1)
                link(dve.bn_stats(st[:, 0:6], x_))
                link(dve.bn_aggr(st[:, 6:8], st[:, 0:6]))
                dve.tensor_scalar(st[:, 8:9], st[:, 7:8], EPS, None, ALU.add).then_inc(ln_var, 1)

            def ln_norm(s, i, x_, xnf_):
                n = lnno[(s, i)]
                st = LNS[n % 2]
                dve.wait_ge(ln_std, n + 1)
                link(dve.reciprocal(st[:, 10:11], st[:, 9:10]))
                dve.tensor_scalar(xnf_, x_, st[:, 6:7], st[:, 10:11], ALU.subtract, ALU.mult).then_inc(ln_xnf, 1)

            def ln_T_lo(s, i, T):
                key = ("xt", s, i)
                sl = slice(i * TILE, (i + 1) * TILE)
                lo(key, T.lo[:, :, sl], bank(key)[:, 0:FB * TILE].rearrange("p (b n) -> p b n", b=FB), T.hi32[:, :, sl])

            x_landed(dve, ("x", 0))
            ln_stats(0, 0, xt_[0][:])
            for i in range(NT + 1):
                if i + 1 < NT:
                    x_landed(dve, ("x", i + 1))
                    ln_stats(0, i + 1, xt_[(i + 1) % 2][:])
                if i < NT:
                    if i >= 2:
                        completed(dve, ("xt", 0, i - 2))
                        dve.wait_ge(ln_lo, i - 1)
                    ln_norm(0, i, xt_[i % 2][:], xnf[i % 2][:])
                    dve.wait_ge(ln_hi, i + 1)
                    dve.tensor_tensor(xn.lo[:, i, :], xnf[i % 2][:], xn.hi32[:, i, :], ALU.subtract)\
                        .then_inc(ln_lo, 1)
                if i >= 1:
                    ln_T_lo(0, i - 1, xnT)
            for w, W in (("k", WA), ("2", W2T)):
                for ib in range(FB):
                    lo(("wt", w, ib), W.lo[:, ib, :], bank(("wt", w, ib)), W.hi32[:, ib, :])
            completed(dve, ("vec",))
            drain(dve.tensor_copy(ccol[:, 0:54], bank(("vec",))[:, 0:54]), ("vec",))
            for b in range(FB):
                key = ("mi", b)
                completed(dve, key)
                drain(dve.tensor_copy(MI.lo32[:, b, :], bank(key)), key)
                carried(dve, key)
                sl = slice(b * 128, (b + 1) * 128)
                dve.tensor_tensor(MI.lo32[:, b, sl], MI.lo32[:, b, sl], ident[:], ALU.add).then_inc(mi_sum, 1)
                dve.wait_ge(mi_hi, b + 1)
                dve.tensor_tensor(MI.lo[:, b, :], MI.lo32[:, b, :], MI.hi32[:, b, :], ALU.subtract)\
                    .then_inc(mi_ready, 1)
            for b in range(FB):
                lo(("g", b), G.lo[:, b, :], bank(("g", b)), G.hi32[:, b, :])
            for ib in range(FB):
                lo(("wt", "q", ib), WB.lo[:, ib, :], bank(("wt", "q", ib)), WB.hi32[:, ib, :])

            def k_maxs(b):
                o_ = 8 * (b % 2)
                for c, (o, w) in enumerate(CH):
                    completed(dve, ("k", b, c))
                    link(dve.tensor_reduce(cols[:, o_ + c:o_ + c + 1], bank(("k", b, c))[:, 0:w], AX_X, ALU.max))
                dve.tensor_reduce(cols[:, o_ + 3:o_ + 4], cols[:, o_:o_ + 3], AX_X, ALU.max,
                                  negate=True).then_inc(k_max, 1)

            k_maxs(0)
            for b in range(FB + 1):
                if b + 1 < FB:
                    k_maxs(b + 1)
                if b < FB:
                    for q in range(3):
                        n = min(4, NT - 4 * q)
                        key = ("kt", b, q)
                        lo(key, ek.lo[:, 4 * q:4 * q + n, :],
                           bank(key)[0:TILE, 0:128 * n].rearrange("p (t d) -> p t d", t=n),
                           ek.hi32[:, 4 * q:4 * q + n, :])
                    o_ = 8 * (b % 2)
                    for c in range(3):
                        carried(dve, ("k", b, c))
                    link(dve.tensor_reduce(cols[:, 24 + b:25 + b], cols[:, o_ + 4:o_ + 7], AX_X, ALU.add))
                    link(dve.reciprocal(cols[:, 28 + b:29 + b], cols[:, 24 + b:25 + b]))
                    lo(("c1", b), c1[b % 2].lo[:], bank(("c1", b)).rearrange("p (c d) -> p c d", c=FB), c1[b % 2].hi32[:])
                if b > 0:
                    key = ("cx", b - 1)
                    completed(dve, key)
                    if b > 1:
                        dve.wait_ge(cx_ready, b - 1)
                    drain(dve.tensor_scalar(cxt[:], bank(key), cols[:, 27 + b:28 + b], float(D) ** -0.5,
                                            ALU.mult, ALU.mult), key)
                    dve.wait_ge(cx_hi, b)
                    dve.tensor_tensor(ctxp.lo[:, b - 1, :], cxt[:], ctxp.hi32[:, b - 1, :], ALU.subtract)\
                        .then_inc(cx_ready, 1)

            def q_maxs(i):
                completed(dve, ("q", i))
                c = 16 + 4 * (i % 2)
                dve.tensor_reduce(cols[0:TILE, c:c + 1], bank(("q", i))[0:TILE, :], AX_X, ALU.max,
                                  negate=True).then_inc(q_max, 1)

            def q_norms(i):
                carried(dve, ("q", i))
                c = 16 + 4 * (i % 2)
                link(dve.reciprocal(cols[0:TILE, c + 2:c + 3], cols[0:TILE, c + 1:c + 2]))
                dve.tensor_scalar(qe[i % 2][:], qe[i % 2][:], cols[0:TILE, c + 2:c + 3], None,
                                  ALU.mult).then_inc(q_norm, 1)

            q_maxs(0)
            q_norms(0)
            dve.wait_ge(bl2_in, 16)
            for i in range(NT):
                if i + 1 < NT:
                    q_maxs(i + 1)
                lo(("qt", i), qT[i % 2].lo[:], bank(("qt", i))[:, 0:FB * TILE].rearrange("p (b n) -> p b n", b=FB),
                   qT[i % 2].hi32[:])
                if i + 1 < NT:
                    q_norms(i + 1)
                x_landed(dve, ("xmix", i))
                xr = xt_[i % 2]
                link(dve.tensor_tensor(xr[:], xr[:], bl2B[:], ALU.add))
                completed(dve, ("mo", i))
                drain(dve.tensor_tensor(xr[:], xr[:], bank(("mo", i))[0:TILE, :], ALU.add), ("mo", i))

            dve.wait_ge(idx_in, 48)
            dve.tensor_copy(srcR[:], srcI[:]).then_inc(idx_f, 1)
            dve.tensor_copy(dstR[:], dstI[:]).then_inc(idx_f, 1)
            link(dve.tensor_copy(grpR[:], grpI[:]))
            link(dve.tensor_reduce(gst[:, 0:1], grpR[:], AX_X, ALU.min))
            link(dve.tensor_reduce(gst[:, 1:2], grpR[:], AX_X, ALU.max))
            for a in range(2):
                dve.tensor_scalar(gD[:, a * GROUPS:(a + 1) * GROUPS], ident[0:GROUPS, 0:GROUPS], gst[:, a:a + 1],
                                  None, ALU.mult).then_inc(idx_f, 1)
            completed(dve, ("ix",))
            link(dve.tensor_copy(srcF[:], bank(("ix",))[0:TILE, 0:170]))
            drain(dve.tensor_copy(dstF[:], bank(("ix",))[0:TILE, 170:340]), ("ix",))
            completed(dve, ("wv",))
            drain(dve.tensor_copy(rows[:, 0:2 * GROUPS], bank(("wv",))[0:TILE, 0:2 * GROUPS]), ("wv",))
            carried(dve, ("wv",))
            least, most, r2 = rows[:, 0:GROUPS], rows[:, GROUPS:2 * GROUPS], 2 * GROUPS
            link(dve.tensor_scalar(wB[:, 0:GROUPS], least, float(LASTWIN), None, ALU.min))
            link(dve.tensor_copy(flags[0:1, 0:GROUPS], wB[0:1, 0:GROUPS]))
            link(dve.tensor_tensor(rows[:, r2:r2 + GROUPS], most, wB[:, 0:GROUPS], ALU.subtract))
            link(dve.tensor_scalar(rows[:, r2:r2 + GROUPS], rows[:, r2:r2 + GROUPS], float(WIN - 1), None,
                                   ALU.subtract))
            link(dve.tensor_tensor(rows[:, 3 * GROUPS:4 * GROUPS - 1], most[:, 0:GROUPS - 1], least[:, 1:GROUPS],
                                   ALU.subtract))
            link(dve.tensor_scalar(rows[:, 4 * GROUPS - 1:4 * GROUPS], ones2[0:TILE, 0:1], -1.0, None, ALU.mult))
            link(dve.tensor_reduce(rows[:, 4 * GROUPS:4 * GROUPS + 1], rows[:, r2:4 * GROUPS], AX_X, ALU.max))
            link(dve.tensor_tensor(rows[:, r2:r2 + GROUPS - FEW], most[:, 0:GROUPS - FEW], least[:, FEW:GROUPS],
                                   ALU.subtract))
            link(dve.tensor_scalar(rows[:, r2:r2 + GROUPS - FEW], rows[:, r2:r2 + GROUPS - FEW], 1.0, None, ALU.add))
            link(dve.tensor_reduce(rows[:, 4 * GROUPS + 1:4 * GROUPS + 2], rows[:, r2:r2 + GROUPS - FEW], AX_X,
                                   ALU.max))
            link(dve.tensor_reduce(wB[:, 20:21], rows[:, 4 * GROUPS:4 * GROUPS + 2], AX_X, ALU.max))
            link(dve.tensor_scalar(flags[0:1, 20:21], wB[0:1, 20:21], 0.0, None, ALU.is_le))
            dve.tensor_tensor(rel[:].rearrange("p (g t) -> p g t", g=GROUPS),
                              wB[:, 0:GROUPS].rearrange("p (g a) -> p g a", a=1).broadcast_to((TILE, GROUPS, GT)),
                              dstF[:].rearrange("p (g t) -> p g t", g=GROUPS),
                              ALU.subtract).then_inc(edge_ready, 1)
            dve.wait_ge(edge_ready, 1)
            dve.wait_ge(const_ready, 2)
            dve.memset(cols[:, 39:40], 0.0).then_inc(edge_tiles, PRIME)
            dve.memset(cols[:, 38:39], 0.0).then_inc(window_free, 2)
            dve.memset(cols[:, 37:38], 0.0).then_inc(all_tiles, 1)
            dve.memset(cols[:, 36:37], 0.0).then_inc(all_taken, 1)
            fit = dve.value_load(flags[0:1, 20:21], min_val=0, max_val=1)

            def onehot_src(t, r):
                return dve.tensor_scalar(ohs[r][:], iota[:], srcF[:, bass.ds(t, 1)], None, ALU.is_equal)

            def group_onehots(g, odd):
                for t in range(GT):
                    dve.wait_ge(edge_tiles, g * GT + (t + 1 - NOH + PRIME))
                    onehot_src(g * GT + t, (odd * GT + t) % NOH).then_inc(src_ready, 1)

            def add_group(g, half):
                dve.wait_ge(edge_tiles, g * GT + (GT + PRIME))
                w = dve.value_load(flags[0:1, bass.ds(g, 1)], min_val=0, max_val=LASTWIN)
                a = AT[:, :, bass.ds(w, WIN)]
                a_was = AT[:, :, bass.ds(w, WIN)].bitcast(F32)
                ps = PS[0:TILE, 3 * half:3 * half + 3, :].rearrange("p b (j w) -> p (b j) w", w=WIN)[:, 0:NT, :]
                dve.wait_ge(window_free, g + 2)
                dve.tensor_tensor(a, a_was, ps, ALU.add).then_inc(window_free, 1)

            dve.wait_ge(at_zero, 1)
            with dve.If(fit == 1):
                group_onehots(0, 0)
                with dve.Fori(0, GROUPS // 2) as k:
                    group_onehots(k * 2 + 1, 1)
                    add_group(k * 2, 0)
                    group_onehots(k * 2 + 2, 0)
                    add_group(k * 2 + 1, 1)
                add_group(GROUPS - 1, 0)
                dve.wait_ge(window_free, GROUPS + 2)
                dve.tensor_reduce(colsum[:], AT[:].bitcast(F32).rearrange("p j d -> p d j"), AX_X,
                                  ALU.add).then_inc(sum_ready, 1)
            with dve.Else():
                with dve.Fori(0, NT - 1) as w:
                    with dve.Fori(0, GROUPS) as g:
                        for t in range(GT):
                            dve.wait_ge(all_tiles, w * (GROUPS * GT) + g * GT + (t + 1))
                            onehot_src(g * GT + t, 0).then_inc(all_src, 1)
                    dve.wait_ge(all_tiles, w * (GROUPS * GT) + (GROUPS * GT + 1))
                    dve.tensor_copy(AT32[:, :, bass.ds(w * WIN, WIN)],
                                    PS[0:TILE, 0:3, :].rearrange("p b (j w) -> p (b j) w", w=WIN)[:, 0:NT, :])\
                        .then_inc(all_taken, 1)
                with dve.Fori(0, GROUPS) as g:
                    for t in range(GT):
                        dve.wait_ge(all_tiles, g * GT + (t + 1 + (NT - 1) * GROUPS * GT))
                        onehot_src(g * GT + t, 0).then_inc(all_src, 1)
                dve.wait_ge(all_tiles, NT * GROUPS * GT + 1)
                dve.wait_ge(all_taken, NT)
                dve.tensor_copy(AT32[:, :, LASTWIN:N],
                                PS[0:TILE, 0:3, :].rearrange("p b (j w) -> p (b j) w", w=WIN)[:, 0:NT, :])\
                    .then_inc(all_taken, 1)
                dve.wait_ge(all_taken, NT + 1)
                dve.tensor_reduce(colsum[:], AT32[:].rearrange("p j d -> p d j"), AX_X,
                                  ALU.add).then_inc(sum_ready, 1)
            for c, (o, w) in enumerate(CH):
                completed(dve, ("cb", c))
                drain(dve.tensor_copy(CNTB[:, o:o + w], bank(("cb", c))[:, 0:w]), ("cb", c))
            completed(dve, ("cc",))
            cc = bank(("cc",))[0:TILE, 0:NT]
            link(dve.tensor_scalar(dinc[:], cc, 1.0, None, ALU.add))
            drain(dve.tensor_scalar(invc[:], cc, 1.0, None, ALU.max), ("cc",))
            carried(dve, ("cc",))
            link(dve.reciprocal(invc[:], invc[:]))
            dve.reciprocal(dinc[:], dinc[:]).then_inc(deg_ready, 1)
            link(dve.tensor_scalar(inv0[:], CNTB[:], 1.0, None, ALU.max))
            dve.reciprocal(inv0[:], inv0[:]).then_inc(inv_ready, 1)
            link(dve.tensor_scalar(CNTB[:], CNTB[:], 1.0, None, ALU.add))
            dve.reciprocal(CNTB[:], CNTB[:]).then_inc(deg_ready, 1)
            for i in range(NT):
                lo(("y1", i), y.lo[:, i, :], bank(("y1", i))[0:TILE, :], y.hi32[:, i, :])
            completed(dve, ("r1", FB - 1, 2))
            dve.wait_ge(inv_ready, 1)
            dve.tensor_copy(INVB[:], inv0[:]).then_inc(inv_placed, 1)
            dve.wait_ge(inv_placed, 1)
            n = 0
            for f in range(FB):
                for c, (o, w) in enumerate(CH):
                    key = ("a1", f, c)
                    n += 1
                    t = sc[n % 2][:, 0:w]
                    completed(dve, key)
                    drain(dve.tensor_tensor(t, bank(key)[:, 0:w], INVB[:, o:o + w], ALU.mult), key)
                    carried(dve, key)
                    carried(dve, ("r1", f, c))
                    R = hT.lo32[:, f, o:o + w]
                    dve.tensor_tensor(R, R, t, ALU.add).then_inc(a1_sum, 1)
                    dve.wait_ge(a1_hi, n)
                    dve.scalar_tensor_tensor(out=hT.lo[:, f, o:o + w], in0=R, scalar=0.0,
                                             in1=hT.hi32[:, f, o:o + w], op0=ALU.max, op1=ALU.subtract)\
                        .then_inc(a1_ready, 1)
            for i in range(NT):
                lo(("y2", i), y.lo[:, i, :], bank(("y2", i))[0:TILE, :], y.hi32[:, i, :])
            for i in range(NT):
                x_landed(dve, ("xr2", i))
                completed(dve, ("r2", i))
                drain(dve.tensor_tensor(xw[i % 2][:], xw[i % 2][:], bank(("r2", i))[0:TILE, :], ALU.add), ("r2", i))

            def a2_x(i):
                x_landed(dve, ("xa2", i))
                completed(dve, ("a2", i))
                drain(dve.scalar_tensor_tensor(out=xw[i % 2][:], in0=bank(("a2", i))[0:TILE, :],
                                               scalar=invc[:, i:i + 1], in1=xw[i % 2][:],
                                               op0=ALU.mult, op1=ALU.add), ("a2", i))
                carried(dve, ("a2", i))
                ln_stats(1, i, xw[i % 2][:])

            a2_x(0)
            for i in range(NT):
                if i >= 2:
                    completed(dve, ("xt", 1, i - 2))
                ln_norm(1, i, xw[i % 2][:], xnw[i % 2][:])
                if i + 1 < NT:
                    a2_x(i + 1)
                ln_T_lo(1, i, xnT)
            def over(a):
                return a.rearrange("p (t a) -> p t a", a=1).broadcast_to((TILE, NT, E))

            def logits_less_max(s):
                dve.wait_ge(moe_in[s], 48)
                key = ("lg", s)
                completed(dve, key)
                bg_ = bgB[s][:].rearrange("p (a e) -> p a e", a=1).broadcast_to((TILE, NT, E))
                drain(dve.tensor_tensor(lgt[s][:], bank(key)[0:TILE, 0:NT * E].rearrange("p (t e) -> p t e", t=NT),
                                        bg_, ALU.add), key)
                carried(dve, key)
                link(dve.tensor_reduce(gred[s][:, 0, :], lgt[s][:], AX_X, ALU.max))
                dve.tensor_tensor(lgt[s][:], lgt[s][:], over(gred[s][:, 0, :]), ALU.subtract).then_inc(lg_less, 1)

            def softmax_scale(s):
                dve.wait_ge(lg_exp, s + 1)
                link(dve.tensor_reduce(gred[s][:, 1, :], ex[s][:], AX_X, ALU.add))
                link(dve.reciprocal(gred[s][:, 2, :], gred[s][:, 1, :]))

            def gate_transposed(s):
                for q in range(3):
                    key = ("gt", s, q)
                    completed(dve, key)
                    o, w = CH[q]
                    drain(dve.tensor_copy(gT[s][:, o:o + w], bank(key)[0:E, 0:w]), key)

            def bias_to_place(s, e, e_):
                c, b_ = COL[f"m{s}b1"], BIAS + 2 * (e % 2)
                dve.tensor_scalar(cols[:, b_:b_ + 2], ccol[:, bass.ds(e_ * 2 + c, 2)], 1.0, None, ALU.mult)\
                    .then_inc(bias_placed, 1)

            def hidden_parts(s, e, e_, later):
                h = hE[e % 2]
                for n, (f, c) in enumerate([(f, c) for f in range(2) for c in range(3)]):
                    o, w = CH[c]
                    carried(dve, ("hd", s, e, f, c), later)
                    dve.tensor_copy(h.hi[:, f, o:o + w], h.lo32[:, f, o:o + w]).then_inc(hid_hi, 1)
                    dve.wait_ge(hid_hi, e_ * 6 + (48 * s + n + 1))
                    dve.tensor_tensor(h.lo[:, f, o:o + w], h.lo32[:, f, o:o + w], h.hi32[:, f, o:o + w],
                                      ALU.subtract).then_inc(hid_ready, 1)

            def expert_added(s, e, e_, later, i):
                key = ("eo", s, e, i)
                completed(dve, key, later)
                drain(dve.scalar_tensor_tensor(out=acc[:, i, :], in0=bank(key)[0:TILE, :],
                                               scalar=gate[:, i, bass.ds(e_, 1)], in1=acc[:, i, :],
                                               op0=ALU.mult, op1=ALU.add), key)

            def experts_added(s):
                bias_to_place(s, 0, 0)
                bias_to_place(s, 1, 1)
                hidden_parts(s, 0, 0, 0)
                with dve.Fori(0, PAIRS) as k:
                    bias_to_place(s, 2, k * 2 + 2)
                    hidden_parts(s, 1, k * 2 + 1, k * 4)
                    for i in range(NT):
                        expert_added(s, 0, k * 2, k * 4, i)
                    bias_to_place(s, 3, k * 2 + 3)
                    hidden_parts(s, 2, k * 2 + 2, k * 4)
                    for i in range(NT):
                        expert_added(s, 1, k * 2 + 1, k * 4, i)
                hidden_parts(s, 7, 7, 0)
                for i in range(NT):
                    expert_added(s, 6, 6, 0, i)

            logits_less_max(0)
            softmax_scale(0)
            link(dve.tensor_scalar(cand[:], lgt[0][:], 0.0, None, ALU.is_equal))
            dve.wait_ge(iota_ready, 1)
            io_ = iota8[:].rearrange("p (a e) -> p a e", a=1).broadcast_to((TILE, NT, E))
            link(dve.scalar_tensor_tensor(out=cand[:], in0=cand[:], scalar=-100.0, in1=io_,
                                          op0=ALU.mult, op1=ALU.add))
            link(dve.tensor_reduce(gred[0][:, 3, :], cand[:], AX_X, ALU.min))
            link(dve.tensor_tensor(cand[:], cand[:], over(gred[0][:, 3, :]), ALU.is_equal))
            dve.tensor_tensor(gate[:], cand[:], over(gred[0][:, 2, :]), ALU.mult).then_inc(gate_ready, 1)
            x_stored(dve, ("xa2", NT - 2))
            x_stored(dve, ("xa2", NT - 1))
            gate_transposed(0)
            experts_added(0)

            def x2_(i):
                expert_added(0, 7, 7, 0, i)
                carried(dve, ("eo", 0, 7, i))
                x_landed(dve, ("xm0", i))
                dve.tensor_tensor(xm[i % 2][:], xm[i % 2][:], acc[:, i, :], ALU.add).then_inc(x2_sum, 1)
                dve.wait_ge(x2_sum, i + 1)
                ln_stats(2, i, xm[i % 2][:])

            x2_(0)
            for i in range(NT + 1):
                if i < NT:
                    if i >= 2:
                        completed(dve, ("xt", 2, i - 2))
                        dve.wait_ge(xn2_lo, i - 1)
                    ln_norm(2, i, xm[i % 2][:], xnm[i % 2][:])
                    if i + 1 < NT:
                        x2_(i + 1)
                    dve.wait_ge(ln_hi, NT + i + 1)
                    dve.tensor_tensor(xn2.lo[:, i, :], xnm[i % 2][:], xn2.hi32[:, i, :], ALU.subtract)\
                        .then_inc(xn2_lo, 1)
                if i >= 1:
                    ln_T_lo(2, i - 1, xnT)
            with dve.If(fit == 1):
                for j in range(NT):
                    sl = slice(j * TILE, (j + 1) * TILE)
                    ins = dve.tensor_tensor(AT[:, j, sl], AT[:, j, sl].bitcast(F32), ident[0:TILE, 0:TILE], ALU.add)
                ins.then_inc(self_loops, 1)
            with dve.Else():
                for j in range(NT):
                    sl = slice(j * TILE, (j + 1) * TILE)
                    ins = dve.tensor_tensor(AT32[:, j, sl], AT32[:, j, sl], ident[0:TILE, 0:TILE], ALU.add)
                ins.then_inc(self_loops, 1)

            x_stored(dve, ("xm0", NT - 2))
            x_stored(dve, ("xm0", NT - 1))
            for i in range(NT):
                key = ("k2", i)
                ps = bank(key)[0:TILE, :]
                completed(dve, key)
                if i >= 3:
                    dve.wait_ge(kacc_done, i - 1)
                    dve.wait_ge(k_ready, i - 2)
                dve.tensor_scalar(kx[i % 3][:], ps, 0.0, None, ALU.min).then_inc(k_min, 1)
                dve.wait_ge(k_exped, i + 1)
                drain(dve.scalar_tensor_tensor(out=kx[i % 3][:], in0=ps, scalar=0.0, in1=kx[i % 3][:],
                                               op0=ALU.max, op1=ALU.add), key)
                dve.wait_ge(k_hi, i + 1)
                dve.tensor_tensor(kp[i % 2].lo[:], kx[i % 3][:], kp[i % 2].hi32[:], ALU.subtract).then_inc(k_ready, 1)
            for b in range(FB):
                lo(("kv", b), kv.lo[:, b, :], bank(("kv", b)), kv.hi32[:, b, :])
            lo(("ks",), ksum.lo[:], bank(("ks",))[:, 0:2 * FB].rearrange("p (b a) -> p b a", b=FB), ksum.hi32[:])

            def q_mins(g, f):
                completed(dve, ("q2", g, f))
                dve.tensor_scalar(q2[g % 2].lo32[:, f, :], bank(("q2", g, f))[:, 0:QC], 0.0, None, ALU.min)\
                    .then_inc(q_min, 1)

            def q_sums(g, f):
                q_ = q2[g % 2].lo32[:, f, :]
                dve.wait_ge(q_exped, g * FB + f + 1)
                drain(dve.scalar_tensor_tensor(out=q_, in0=bank(("q2", g, f))[:, 0:QC], scalar=0.0, in1=q_,
                                               op0=ALU.max, op1=ALU.add), ("q2", g, f))

            def q_los(g, f):
                q_ = q2[g % 2]
                dve.wait_ge(q_hi, g * FB + f + 1)
                dve.tensor_tensor(q_.lo[:, f, :], q_.lo32[:, f, :], q_.hi32[:, f, :], ALU.subtract).then_inc(q_ready, 1)

            def mixed(i):
                c = 24 + 2 * (i % 2)
                completed(dve, ("dn", i))
                drain(dve.tensor_scalar(cols[0:TILE, c:c + 1], bank(("dn", i))[0:TILE, 0:1], 1e-6, None, ALU.add),
                      ("dn", i))
                carried(dve, ("dn", i))
                link(dve.reciprocal(cols[0:TILE, c + 1:c + 2], cols[0:TILE, c:c + 1]))
                x_landed(dve, ("xq", i))
                completed(dve, ("mx", i))
                drain(dve.scalar_tensor_tensor(out=xq[i % 2][:], in0=bank(("mx", i))[0:TILE, :],
                                               scalar=cols[0:TILE, c + 1:c + 2], in1=xq[i % 2][:],
                                               op0=ALU.mult, op1=ALU.add), ("mx", i))

            for g in range(NQ + 1):
                if g < NQ:
                    if g >= 2:
                        completed(dve, ("mx", 2 * g - 3))
                    for f in range(FB + 2):
                        if f < FB:
                            q_mins(g, f)
                        if 0 < f <= FB:
                            q_sums(g, f - 1)
                        if f > 1:
                            q_los(g, f - 2)
                    for i in (2 * g, 2 * g + 1):
                        dve.wait_ge(xs_whole, i + 1)
                        dve.tensor_scalar(xn2.lo32[:, i, :], xn2.lo32[:, i, :], dinc[:, i:i + 1], None, ALU.mult)\
                            .then_inc(xs_scaled, 1)
                        dve.wait_ge(xs_hi, i + 1)
                        dve.tensor_tensor(xn2.lo[:, i, :], xn2.lo32[:, i, :], xn2.hi32[:, i, :], ALU.subtract)\
                            .then_inc(xs_ready, 1)
                if g > 0:
                    mixed(2 * g - 2)
                    mixed(2 * g - 1)

            dve.wait_ge(deg_root, 2)
            for n, (f, c) in enumerate(HX):
                o, w = CH[c]
                key = ("z", f, c)
                z_ = zT.lo32[:, f, o:o + w]
                completed(dve, key)
                drain(dve.tensor_tensor(z_, bank(key)[:, 0:w], CNTB[:, o:o + w], ALU.mult), key)
                dve.wait_ge(z_hi, n + 1)
                dve.tensor_tensor(zT.lo[:, f, o:o + w], z_, zT.hi32[:, f, o:o + w], ALU.subtract).then_inc(z_ready, 1)
            for hf in range(2):
                for n, (f, c) in enumerate(HX):
                    o, w = CH[c]
                    dve.wait_ge(h1_hi, hf * len(HX) + n + 1)
                    dve.tensor_tensor(h1T.lo[:, f, o:o + w], h1T.lo32[:, f, o:o + w], h1T.hi32[:, f, o:o + w],
                                      ALU.subtract).then_inc(h1_ready, 1)
                if hf == 0:
                    continue
                for i in range(NT):
                    key = ("yy", 1, i)
                    carried(dve, ("yy", 0, i))
                    completed(dve, key)
                    y_ = y3.lo32[:, i, :]
                    drain(dve.scalar_tensor_tensor(out=y_, in0=bank(key)[0:TILE, :], scalar=dinc[:, i:i + 1], in1=y_,
                                                   op0=ALU.mult, op1=ALU.add), key)
                    dve.wait_ge(y3_hi, i + 1)
                    dve.tensor_tensor(y3.lo[:, i, :], y_, y3.hi32[:, i, :], ALU.subtract).then_inc(y3_ready, 1)
            dve.wait_ge(b2_in, 16)
            for i in range(NT + 1):
                if i < NT:
                    x_landed(dve, ("xa3", i))
                    completed(dve, ("a3", i))
                    drain(dve.scalar_tensor_tensor(out=gt_[:], in0=bank(("a3", i))[0:TILE, :], scalar=dinc[:, i:i + 1],
                                                   in1=b2B[:], op0=ALU.mult, op1=ALU.add), ("a3", i))
                    carried(dve, ("a3", i))
                    dve.scalar_tensor_tensor(out=xg[i % 2][:], in0=gt_[:], scalar=0.0, in1=xg[i % 2][:],
                                             op0=ALU.max, op1=ALU.add).then_inc(x3_sum, 1)
                    dve.wait_ge(x3_sum, i + 1)
                    ln_stats(3, i, xg[i % 2][:])
                    ln_norm(3, i, xg[i % 2][:], xnA[i % 2][:])
                    dve.wait_ge(ln_xnf, lnno[(3, i)] + 1)
                    ln_stats(4, i, xnA[i % 2][:])
                    if i >= 2:
                        completed(dve, ("xt", 4, i - 2))
                    ln_norm(4, i, xnA[i % 2][:], xnB[i % 2][:])
                if i >= 1:
                    sl = slice((i - 1) * TILE, i * TILE)
                    dve.wait_ge(hx_hi, i)
                    dve.tensor_tensor(hxT.lo[:, :, sl], hxT.lo32[:, :, sl], hxT.hi32[:, :, sl], ALU.subtract)\
                        .then_inc(hx_ready, 1)
            def tt(a, b, out_, op):
                return dve.tensor_tensor(out_, a, b, op)

            def unit_sums(s, i):
                c = 8 * (i % 2)
                dve.wait_ge(squared, NT * s + i + 1)
                if i >= 2 or s:
                    dve.wait_ge(unit_root, NT * s + i - 1)
                link(dve.tensor_reduce(cols[0:TILE, c:c + 8], sqr[i % 2][:].rearrange("p (h d) -> p h d", h=HEADS),
                                       AX_X, ALU.add))
                dve.tensor_scalar(cols[0:TILE, c:c + 8], cols[0:TILE, c:c + 8], 1e-12, (1.0, 1.0 / DH)[s], ALU.add,
                                  ALU.mult).then_inc(unit_sum, 1)

            def unit_norm(s, w, i):
                c = 16 + 8 * (i % 2)
                r = cols[0:TILE, c:c + 8]
                dve.wait_ge(unit_root, NT * s + i + 1)
                link(dve.reciprocal(r, r))
                if i >= 2:
                    completed(dve, ("t" + w, i - 2))
                elif s:
                    completed(dve, ("tq", NT - 2 + i))
                drain(dve.tensor_tensor(unit[i % 2][:].rearrange("p (h d) -> p h d", h=HEADS),
                                        bank(("p" + w, i))[0:TILE, :].rearrange("p (h d) -> p h d", h=HEADS),
                                        r.rearrange("p (h a) -> p h a", a=1).broadcast_to((TILE, HEADS, DH)),
                                        ALU.mult), ("p" + w, i))

            even, odd = slice(0, HEADS, 2), slice(1, HEADS, 2)
            up, down = slice(0, DH), slice(DH, 2 * DH)
            for s, (w, gain) in enumerate((("q", "qn_g"), ("k", "kn_g"))):
                g_ = ccol[:, COL[gain]:COL[gain] + 1]
                unit_sums(s, 0)
                unit_norm(s, w, 0)
                for i in range(NT):
                    if i + 1 < NT:
                        unit_sums(s, i + 1)
                        unit_norm(s, w, i + 1)
                    key = ("t" + w, i)
                    sl = slice(i * TILE, (i + 1) * TILE)
                    t_ = bank(key)[:, 0:FB * TILE].rearrange("p (b n) -> p b n", b=FB)
                    dve_los.append(key)
                    dve.wait_ge(hi_done, len(dve_los))
                    if w == "q":
                        outs = (QA[down, even, sl], QA[up, odd, sl])
                        ins = (QA32[up, even, sl], QA32[down, odd, sl])
                    else:
                        outs = (KLO[up, :, sl], KLO[down, :, sl])
                        ins = (KA32[up, even, sl], KA32[down, odd, sl])
                    for a in range(2):
                        half = (up, down)[a]
                        last = dve.scalar_tensor_tensor(out=outs[a], in0=t_[half], scalar=g_[half], in1=ins[a],
                                                        op0=ALU.mult, op1=ALU.subtract)
                    drain(last, key)

            def row_max(n):
                c = 9 * (n % 4)
                if n >= 4:
                    carried(dve, ("o", n - 4))
                for q in range(SEEN[n]):
                    w_ = TILE * len(tiles_of(n, q))
                    completed(dve, ("s", n, q))
                    link(dve.tensor_reduce(cols[0:TILE, c + q:c + q + 1], bank(("s", n, q))[0:TILE, 0:w_], AX_X,
                                           ALU.max))
                dve.tensor_reduce(cols[0:TILE, c + 3:c + 4], cols[0:TILE, c:c + SEEN[n]], AX_X, ALU.max,
                                  negate=True).then_inc(s_max, 1)

            def row_out(n):
                i, h = ROWS[n]
                c = 9 * (n % 4)
                for q in range(SEEN[n]):
                    carried(dve, ("s", n, q))
                link(dve.tensor_reduce(cols[0:TILE, c + 7:c + 8], cols[0:TILE, c + 4:c + 4 + SEEN[n]], AX_X, ALU.add))
                link(dve.reciprocal(cols[0:TILE, c + 8:c + 9], cols[0:TILE, c + 7:c + 8]))
                completed(dve, ("o", n))
                drain(dve.tensor_scalar(O[:, i, h * DH:(h + 1) * DH], bank(("o", n))[0:TILE, 0:DH],
                                        cols[0:TILE, c + 8:c + 9], None, ALU.mult), ("o", n))

            row_max(0)
            for g, (n, q) in enumerate(GROUPED):
                if q == 0 and n + 1 < len(ROWS):
                    row_max(n + 1)
                m = len(tiles_of(n, q))
                lo(("pt", n, q), PT[g % NPT].lo[:, 0:m, :],
                   bank(("pt", n, q))[0:TILE, 0:TILE * m].rearrange("p (t k) -> p t k", t=m),
                   PT[g % NPT].hi32[:, 0:m, :])
                if g >= LAG and GROUPED[g - LAG][1] == SEEN[GROUPED[g - LAG][0]] - 1:
                    row_out(GROUPED[g - LAG][0])
            for g in range(len(GROUPED) - LAG, len(GROUPED)):
                if GROUPED[g][1] == SEEN[GROUPED[g][0]] - 1:
                    row_out(GROUPED[g][0])
            for i in range(NT):
                key = ("ot", i)
                sl = slice(i * TILE, (i + 1) * TILE)
                lo(key, OT.lo[:, :, sl], bank(key)[:, 0:FB * TILE].rearrange("p (b n) -> p b n", b=FB),
                   OT.hi32[:, :, sl])
            for f, c in HX:
                o, w = CH[c]
                lo(("wo", f, c), yT.lo[:, f, o:o + w], bank(("wo", f, c))[:, 0:w], yT.hi32[:, f, o:o + w])

            logits_less_max(1)
            softmax_scale(1)
            dve.tensor_tensor(gate[:], ex[1][:], over(gred[1][:, 2, :]), ALU.mult).then_inc(gate_ready, 1)
            gate_transposed(1)
            experts_added(1)
            for i in range(NT):
                expert_added(1, 7, 7, 0, i)
                carried(dve, ("eo", 1, 7, i))
                x_landed(dve, ("xm1", i))
                dve.tensor_tensor(xm[i % 2][:], xm[i % 2][:], acc[:, i, :], ALU.add).then_inc(x2_sum, 1)

        @block.tensor
        def _(pe):
            def mm3(out_, l, r, start, stop):
                pe.matmul(out_, l[0], r[0], start=start, stop=False)
                pe.matmul(out_, l[0], r[1], start=False, stop=False)
                return pe.matmul(out_, l[1], r[0], start=False, stop=stop)

            def opened(key, later=0):
                b, n = place[key]
                if n > 1:
                    pe.wait_ge(drained[b], later + (n - 1))
                return PS[:, b, :]

            def done(ins, key):
                ins.then_inc(filled[place[key][0]], 1)

            def of(p, *idx):
                return (p.hi[idx], p.lo[idx])

            al = slice(None)

            def blk(b, w=128):
                return slice(b * w, (b + 1) * w)

            def product(key, out_, pairs):
                for n, (l, r) in enumerate(pairs):
                    ins = mm3(out_, l, r, n == 0, n == len(pairs) - 1)
                done(ins, key)

            def ln_T(s, i, xnf_):
                pe.wait_ge(ln_xnf, lnno[(s, i)] + 1)
                o = opened(("xt", s, i))
                for b in range(FB):
                    ins = pe.transpose(o[:, blk(b, TILE)], xnf_[:, blk(b)], ident[0:TILE, 0:TILE])
                done(ins, ("xt", s, i))

            def w_T(w, raw_):
                for ib in range(FB):
                    o = opened(("wt", w, ib))
                    for ob in range(FB):
                        ins = pe.transpose(o[:, blk(ob)], raw_[:, ob, blk(ib)], ident[:])
                    done(ins, ("wt", w, ib))

            pe.wait_ge(const_ready, 1)
            for i in range(NT):
                ln_T(0, i, xnf[i % 2])
            pe.wait_ge(rawk_in, 16)
            w_T("k", rawk)
            pe.wait_ge(raw2_in, 16)
            w_T("2", raw2)
            pe.wait_ge(vecs_in, 16 * 10)
            done(pe.transpose(opened(("vec",))[:, 0:54], vecs[:], ident[0:54, 0:54]), ("vec",))
            pe.wait_ge(unit_ready, 1)
            for ib in range(FB):
                carried(pe, ("wt", "2", ib))
            for ib in range(FB):
                product(("mi", ib), opened(("mi", ib)),
                        [(of(W1p, al, jb, blk(ib)), of(W2T, al, jb, al)) for jb in range(FB)])
            pe.wait_ge(unit_ready, 2)
            pe.wait_ge(mi_ready, FB)
            for cb in range(FB):
                product(("g", cb), opened(("g", cb)),
                        [(of(Wvp, al, eb, blk(cb)), of(MI, al, eb, al)) for eb in range(FB)])
            pe.wait_ge(rawq_in, 16)
            w_T("q", rawq)

            for i in range(NT):
                carried(pe, ("xt", 0, i))
            for ib in range(FB):
                carried(pe, ("wt", "k", ib))
                carried(pe, ("wt", "q", ib))
                carried(pe, ("g", ib))

            def k_block(b):
                for c, (o, w) in enumerate(CH):
                    product(("k", b, c), opened(("k", b, c))[:, 0:w],
                            [(of(WA, al, kb, blk(b)), of(xnT, al, kb, slice(o, o + w))) for kb in range(FB)])

            k_block(0)
            for b in range(FB + 1):
                if b + 1 < FB:
                    k_block(b + 1)
                if b < FB:
                    for c in range(3):
                        carried(pe, ("k", b, c))
                    for q in range(3):
                        o = opened(("kt", b, q))
                        for t in range(min(4, NT - 4 * q)):
                            ins = pe.transpose(o[0:TILE, blk(t)], kT[b % 2][:, blk(4 * q + t, TILE)], ident[:])
                        done(ins, ("kt", b, q))
                    for q in range(3):
                        carried(pe, ("kt", b, q))
                    pe.wait_ge(ln_lo, NT)
                    o = opened(("c1", b))
                    for cb in range(FB):
                        for i in range(NT):
                            ins = mm3(o[:, blk(cb)], of(xn, al, i, blk(cb)), of(ek, al, i, al), i == 0, i == NT - 1)
                    done(ins, ("c1", b))
                if b > 0:
                    carried(pe, ("c1", b - 1))
                    product(("cx", b - 1), opened(("cx", b - 1)),
                            [(of(c1[(b - 1) % 2], al, cb, al), of(G, al, cb, al)) for cb in range(FB)])

            def q_tile(i):
                product(("q", i), opened(("q", i))[0:TILE, :],
                        [(of(xnT, al, kb, blk(i, TILE)), of(WB, al, kb, al)) for kb in range(FB)])

            q_tile(0)
            pe.wait_ge(cx_ready, FB)
            for i in range(NT):
                if i + 1 < NT:
                    q_tile(i + 1)
                pe.wait_ge(q_norm, i + 1)
                o = opened(("qt", i))
                for b in range(FB):
                    ins = pe.transpose(o[:, blk(b, TILE)], qe[i % 2][:, blk(b)], ident[0:TILE, 0:TILE])
                done(ins, ("qt", i))
                o = opened(("mo", i))[0:TILE, :]
                for kb in range(FB):
                    mm3(o, of(xnT, al, kb, blk(i, TILE)), of(MI, al, kb, al), kb == 0, False)
                carried(pe, ("qt", i))
                for b in range(FB):
                    ins = mm3(o, of(qT[i % 2], al, b, al), of(ctxp, al, b, al), False, b == FB - 1)
                done(ins, ("mo", i))
            for n, name in enumerate(torch_w):
                pe.wait_ge(wraw_in[n % 2], 16 * (n // 2 + 1))
                w_T(name, wraw[n % 2])

            pe.wait_ge(idx_f, 4)
            pe.wait_ge(const_ready, 2)
            o = opened(("ix",))
            for a, rows in enumerate((srcR, dstR)):
                for h in range(2):
                    ins = pe.transpose(o[0:TILE, 170 * a + 85 * h:170 * a + 85 * h + 85], rows[:, h, :], ident[0:85, 0:85])
            done(ins, ("ix",))
            o = opened(("wv",))
            done(pe.matmul(o[0:TILE, 0:2 * GROUPS], onesA[0:GROUPS, 0:TILE], gD[:], start=True, stop=True), ("wv",))
            for b in range(BANKS):
                pe.wait_ge(drained[b], before_edges[b])
            pe.wait_ge(edge_ready, 1)
            fit = pe.value_load(flags[0:1, 20:21], min_val=0, max_val=1)

            def tile_counts(half, os, od, first, last):
                for j in range(NT):
                    o_ = PS[0:TILE, 3 * half + j // 4, blk(j % 4)]
                    ins = pe.matmul(o_, os[:, blk(j, TILE)], od, start=(first and j % 4 == 0), stop=last,
                                    skip_group_check=True)
                return ins

            def group_counts(g, half):
                pe.wait_ge(window_free, g + 1)
                pe.wait_ge(dst_ready, g + 1)
                for t in range(GT):
                    pe.wait_ge(src_ready, g * GT + (t + 1))
                    tile_counts(half, ohs[(half * GT + t) % NOH], ohd[half][:, t, :], t == 0, t == GT - 1)\
                        .then_inc(edge_tiles, 1)

            with pe.If(fit == 1):
                with pe.Fori(0, GROUPS // 2) as k:
                    group_counts(k * 2, 0)
                    group_counts(k * 2 + 1, 1)
                group_counts(GROUPS - 1, 0)
            with pe.Else():
                with pe.Fori(0, NT) as w:
                    def all_group(g, first):
                        pe.wait_ge(all_dst, w * GROUPS + g + 1)
                        for t in range(GT):
                            pe.wait_ge(all_src, w * (GROUPS * GT) + g * GT + (t + 1))
                            tile_counts(0, ohs[0], ohd[0][:, t, :], first and t == 0, False)\
                                .then_inc(all_tiles, 1)

                    pe.wait_ge(all_taken, w + 1)
                    all_group(0, True)
                    with pe.Fori(1, GROUPS) as g:
                        all_group(g, False)

            pe.wait_ge(sum_ready, 1)
            for c, (o_, w_) in enumerate(CH):
                o = opened(("cb", c))
                done(pe.matmul(o[:, 0:w_], onesA[:], colsum[:, o_:o_ + w_], start=True, stop=True), ("cb", c))
            o = opened(("cc",))
            for i in range(NT):
                ins = pe.matmul(o[0:TILE, i:i + 1], colsum[:, blk(i, TILE)], onesA[:, 0:1], start=True, stop=True)
            done(ins, ("cc",))
            unit_split(pe, "Wl1")
            for i in range(NT):
                product(("y1", i), opened(("y1", i))[0:TILE, :],
                        [(of(xnT, al, kb, blk(i, TILE)), of(WA, al, kb, al)) for kb in range(FB)])
            unit_split(pe, "Wr1")
            for f in range(FB):
                for c, (o, w) in enumerate(CH):
                    product(("r1", f, c), opened(("r1", f, c))[:, 0:w],
                            [(of(WB, al, kb, blk(f)), of(xnT, al, kb, slice(o, o + w))) for kb in range(FB)])

            def counts_moving(key, p, f, c, fast_):
                o, w = CH[c]
                out_ = opened(key)[:, 0:w]
                for j in range(NT):
                    if fast_:
                        a = AT[:, j, o:o + w]
                        pe.matmul(out_, p.hi[:, j, blk(f)], a, start=(j == 0), stop=False)
                        ins = pe.matmul(out_, p.lo[:, j, blk(f)], a, start=False, stop=(j == NT - 1))
                    else:
                        a = AT32[:, j, o:o + w]
                        pe.matmul(out_, p.hi32[:, j, blk(f)], a, start=(j == 0), stop=False)
                        ins = pe.matmul(out_, p.lo[:, j, blk(f)].bitcast(F32), a, start=False, stop=(j == NT - 1))
                done(ins, key)

            def counts_still(key, p, i, fast_):
                out_ = opened(key)[0:TILE, :]
                for j in range(NT):
                    if fast_:
                        a = AT[:, j, blk(i, TILE)]
                        pe.matmul(out_, a, p.hi[:, j, :], start=(j == 0), stop=False)
                        ins = pe.matmul(out_, a, p.lo[:, j, :], start=False, stop=(j == NT - 1))
                    else:
                        a = AT32[:, j, blk(i, TILE)]
                        pe.matmul(out_, a, p.hi32[:, j, :], start=(j == 0), stop=False)
                        ins = pe.matmul(out_, a, p.lo[:, j, :].bitcast(F32), start=False, stop=(j == NT - 1))
                done(ins, key)

            def on_both_paths(stage):
                with pe.If(fit == 1):
                    stage(True)
                with pe.Else():
                    stage(False)

            for i in range(NT):
                carried(pe, ("y1", i))

            @on_both_paths
            def _(fast_):
                for f in range(FB):
                    for c in range(3):
                        counts_moving(("a1", f, c), y, f, c, fast_)

            pe.wait_ge(a1_ready, 3 * FB)
            unit_split(pe, "Wl2")
            for i in range(NT):
                product(("y2", i), opened(("y2", i))[0:TILE, :],
                        [(of(hT, al, kb, blk(i, TILE)), of(WA, al, kb, al)) for kb in range(FB)])
            unit_split(pe, "Wr2")
            for i in range(NT):
                product(("r2", i), opened(("r2", i))[0:TILE, :],
                        [(of(hT, al, kb, blk(i, TILE)), of(WB, al, kb, al)) for kb in range(FB)])
            for i in range(NT):
                carried(pe, ("y2", i))

            @on_both_paths
            def _(fast_):
                for i in range(NT + 1):
                    if i < NT:
                        counts_still(("a2", i), y, i, fast_)
                    if i >= 1:
                        ln_T(1, i - 1, xnw[(i - 1) % 2])
            def gate_logits(s, T):
                pe.wait_ge(wg_ready, s + 1)
                o = opened(("lg", s))
                for i in range(NT):
                    for kb in range(FB):
                        ins = mm3(o[0:TILE, E * i:E * i + E], of(T, al, kb, blk(i, TILE)), of(WgP[s], al, kb, al),
                                  kb == 0, kb == FB - 1)
                done(ins, ("lg", s))

            def gates_and_biases(s):
                pe.wait_ge(gate_ready, s + 1)
                for q, (o_, w_) in enumerate(CH):
                    o = opened(("gt", s, q))
                    for t in range(w_ // TILE):
                        ins = pe.transpose(o[0:E, blk(t, TILE)], gate[:, o_ // TILE + t, :], ident[0:TILE, 0:TILE])
                    done(ins, ("gt", s, q))
                for q in range(3):
                    carried(pe, ("gt", s, q))
                for i in range(NT):
                    done(pe.matmul(opened(("ac", s, i))[0:TILE, :], gT[s][:, blk(i, TILE)], b2s[s][:],
                                   start=True, stop=True), ("ac", s, i))

            def moe_w(e):
                W = (WA, WB)[1 - e % 2]
                v1 = [p[:].rearrange("p b n -> p (b n)")[:, 0:4 * HID].rearrange("p (b n) -> p b n", b=4)
                      for p in (W.hi, W.lo)]
                v2 = [p[:].rearrange("p b n -> p (b n)")[:, 4 * HID:8 * HID].rearrange("p (b n) -> p b n", b=2)
                      for p in (W.hi, W.lo)]
                return v1, v2

            def hidden_products(s, e, e_, later, T):
                pe.wait_ge(unit_ready, e_ + unit_no[f"m{s}e0"][2])
                v1, _ = moe_w(e)
                for f in range(2):
                    for c, (o, w) in enumerate(CH):
                        key = ("hd", s, e, f, c)
                        product(key, opened(key, later)[:, 0:w],
                                [((v1[0][:, kb, blk(f)], v1[1][:, kb, blk(f)]), of(T, al, kb, slice(o, o + w)))
                                 for kb in range(FB)])

            def output_product(s, e, e_, later, i):
                if i == 0:
                    pe.wait_ge(hid_ready, e_ * 6 + (48 * s + 6))
                _, v2 = moe_w(e)
                key = ("eo", s, e, i)
                product(key, opened(key, later)[0:TILE, :],
                        [(of(hE[e % 2], al, f, blk(i, TILE)), (v2[0][:, f, :], v2[1][:, f, :])) for f in range(2)])

            def experts(s, T):
                hidden_products(s, 0, 0, 0, T)
                with pe.Fori(0, PAIRS) as k:
                    hidden_products(s, 1, k * 2 + 1, k * 4, T)
                    for i in range(NT):
                        output_product(s, 0, k * 2, k * 4, i)
                    hidden_products(s, 2, k * 2 + 2, k * 4, T)
                    for i in range(NT):
                        output_product(s, 1, k * 2 + 1, k * 4, i)
                hidden_products(s, 7, 7, 0, T)
                for i in range(NT):
                    output_product(s, 6, 6, 0, i)

            for i in range(NT):
                carried(pe, ("xt", 1, i))
            gate_logits(0, xnT)
            gates_and_biases(0)
            experts(0, xnT)
            for i in range(NT + 1):
                if i < NT:
                    output_product(0, 7, 7, 0, i)
                if i >= 1:
                    ln_T(2, i - 1, xnm[(i - 1) % 2])
            def k2_tile(i):
                product(("k2", i), opened(("k2", i))[0:TILE, :],
                        [(of(xnT, al, kb, blk(i, TILE)), of(WB, al, kb, al)) for kb in range(FB)])

            for i in range(NT):
                carried(pe, ("xt", 2, i))
            unit_split(pe, "Wqk1")
            k2_tile(0)
            pe.wait_ge(xn2_lo, NT)
            for i in range(NT):
                if i + 1 < NT:
                    k2_tile(i + 1)
                pe.wait_ge(k_ready, i + 1)
                for b in range(FB):
                    o = opened(("kv", b)) if i == 0 else bank(("kv", b))
                    ins = mm3(o, of(kp[i % 2], al, blk(b)), of(xn2, al, i, al), i == 0, i == NT - 1)
                    if i == NT - 1:
                        done(ins, ("kv", b))
                if i < NT - 1:
                    ins.then_inc(k_used, 1)
            pe.wait_ge(kacc_done, NT + 1)
            o = opened(("ks",))
            for b in range(FB):
                ins = pe.matmul(o[:, 2 * b:2 * b + 2], kacc[:, blk(b)], ones2[0:TILE, 0:2], start=True, stop=True)
            done(ins, ("ks",))
            unit_split(pe, "Wqk0")
            for g in range(NQ + 1):
                if g < NQ:
                    for f in range(FB):
                        product(("q2", g, f), opened(("q2", g, f))[:, 0:QC],
                                [(of(WA, al, kb, blk(f)), of(xnT, al, kb, blk(g, QC))) for kb in range(FB)])
                if g > 0:
                    if g == 1:
                        carried(pe, ("kv", FB - 1))
                        carried(pe, ("ks",))
                    pe.wait_ge(q_ready, g * FB)
                    q_ = q2[(g - 1) % 2]
                    for t in range(2):
                        i = 2 * g - 2 + t
                        product(("dn", i), opened(("dn", i))[0:TILE, 0:2],
                                [(of(q_, al, b, blk(t, TILE)), of(ksum, al, b, al)) for b in range(FB)])
                        product(("mx", i), opened(("mx", i))[0:TILE, :],
                                [(of(q_, al, b, blk(t, TILE)), of(kv, al, b, al)) for b in range(FB)])

            pe.wait_ge(self_loops, 1)
            pe.wait_ge(xs_ready, NT)

            @on_both_paths
            def _(fast_):
                for f, c in HX:
                    counts_moving(("z", f, c), xn2, f, c, fast_)

            pe.wait_ge(z_ready, len(HX))
            for hf in range(2):
                unit_split(pe, "gW1" + "ab"[hf])
                for f, c in HX:
                    o, w = CH[c]
                    product(("h1", hf, f, c), opened(("h1", hf, f, c))[:, 0:w],
                            [(of(WB, al, kb, blk(f)), of(zT, al, kb, slice(o, o + w))) for kb in range(FB)])
                unit_split(pe, "gW2" + "ab"[hf])
                pe.wait_ge(h1_ready, (hf + 1) * len(HX))
                for i in range(NT):
                    product(("yy", hf, i), opened(("yy", hf, i))[0:TILE, :],
                            [(of(h1T, al, kb, blk(i, TILE)), of(WA, al, kb, al)) for kb in range(FB)])
            pe.wait_ge(y3_ready, NT)

            @on_both_paths
            def _(fast_):
                for i in range(NT + 1):
                    if i < NT:
                        counts_still(("a3", i), y3, i, fast_)
                    if i >= 1:
                        ln_T(4, i - 1, xnB[(i - 1) % 2])
            pe.wait_ge(hx_ready, NT)
            unit_split(pe, "aWv")
            for i in range(NT):
                product(("pv", i), opened(("pv", i))[0:TILE, :],
                        [(of(hxT, al, kb, blk(i, TILE)), of(WB, al, kb, al)) for kb in range(FB)])
            for w, unit_, W in (("q", "aWq", WA), ("k", "aWk", WB)):
                unit_split(pe, unit_)
                for i in range(NT + 1):
                    if i < NT:
                        product(("p" + w, i), opened(("p" + w, i))[0:TILE, :],
                                [(of(hxT, al, kb, blk(i, TILE)), of(W, al, kb, al)) for kb in range(FB)])
                    if i >= 1:
                        key = ("t" + w, i - 1)
                        carried(pe, ("p" + w, i - 1))
                        o = opened(key)
                        for b in range(FB):
                            ins = pe.transpose(o[:, blk(b, TILE)], unit[(i - 1) % 2][:, blk(b)], ident[0:TILE, 0:TILE])
                        done(ins, key)

            def scores(n):
                i, h = ROWS[n]
                b, hi_rows = h // 2, slice(DH * (h % 2), DH * (h % 2) + DH)
                for q in range(SEEN[n]):
                    key = ("s", n, q)
                    o = opened(key)[0:TILE]
                    w_ = TILE * len(tiles_of(n, q))
                    even_w = w_ + w_ % 2
                    sl = slice(500 * q, 500 * q + even_w)
                    pe.matmul(o[:, 0:even_w], QA[:, h, blk(i, TILE)], KA[:, h, sl], start=True, stop=False)
                    if q == SEEN[n] - 1:
                        pe.matmul(o[:, w_ - TILE:w_], identb[0:TILE, 0:TILE], causal[:], start=False, stop=False)
                    ins = pe.matmul(o[:, 0:even_w], QA[hi_rows, h, blk(i, TILE)], KLO[hi_rows, b, sl],
                                    start=False, stop=True)
                    done(ins, key)

            def product_with_v(g):
                n, q = GROUPED[g]
                i, h = ROWS[n]
                carried(pe, ("pt", n, q))
                pe.wait_ge(v_ready, i + 1)
                o = opened(("o", n)) if q == 0 else bank(("o", n))
                for t, j in enumerate(tiles_of(n, q)):
                    vs = slice(h * DH, (h + 1) * DH)
                    ins = mm3(o[0:TILE, 0:DH], of(PT[g % NPT], al, t, al), of(V, al, j, vs), j == 0, j == i)
                if q == SEEN[n] - 1:
                    done(ins, ("o", n))
                else:
                    ins.then_inc(pt_used, 1)

            pe.wait_ge(k_twice, NT)
            carried(pe, ("tk", NT - 1))
            scores(0)
            for g, (n, q) in enumerate(GROUPED):
                if q == 0:
                    if n + 1 < len(ROWS):
                        scores(n + 1)
                key = ("pt", n, q)
                carried(pe, ("s", n, q))
                o = opened(key)[0:TILE]
                for t, j in enumerate(tiles_of(n, q)):
                    ins = pe.transpose(o[:, blk(t, TILE)], P[n % 2][:, blk(j, TILE)], ident[0:TILE, 0:TILE])
                done(ins, key)
                if g >= LAG:
                    product_with_v(g - LAG)
            for g in range(len(GROUPED) - LAG, len(GROUPED)):
                product_with_v(g)

            for i in range(NT):
                if i == NT - 1:
                    carried(pe, ("o", len(ROWS) - 1))
                else:
                    carried(pe, ("o", HEADS * i + HEADS - 1))
                o = opened(("ot", i))
                for b in range(FB):
                    ins = pe.transpose(o[:, blk(b, TILE)], O[:, i, blk(b)], ident[0:TILE, 0:TILE])
                done(ins, ("ot", i))
            for i in range(NT):
                carried(pe, ("ot", i))
            unit_split(pe, "aWo")
            for f, c in HX:
                o, w = CH[c]
                product(("wo", f, c), opened(("wo", f, c))[:, 0:w],
                        [(of(WA, al, kb, blk(f)), of(OT, al, kb, slice(o, o + w))) for kb in range(FB)])
            for f, c in HX:
                carried(pe, ("wo", f, c))
            gate_logits(1, yT)
            gates_and_biases(1)
            experts(1, yT)
            for i in range(NT):
                output_product(1, 7, 7, 0, i)

        assert act_his == dve_los


_INS = ['x', 'src', 'dst', 'L0_gnn_Wl1', 'L0_gnn_bl1', 'L0_gnn_Wr1', 'L0_gnn_Wl2', 'L0_gnn_bl2', 'L0_gnn_Wr2',
        'L0_mix_Wq', 'L0_mix_Wk', 'L0_mix_Wv', 'L0_mix_W1', 'L0_mix_W2', 'L0_ffn_Wg', 'L0_ffn_bg', 'L0_ffn_W1',
        'L0_ffn_b1', 'L0_ffn_W2', 'L0_ffn_b2', 'L1_gnn_W1', 'L1_gnn_b1', 'L1_gnn_W2', 'L1_gnn_b2', 'L1_mix_W_qk',
        'L1_ffn_ln_g', 'L1_ffn_ln_b', 'L1_ffn_Wq', 'L1_ffn_Wk', 'L1_ffn_Wv', 'L1_ffn_Wo', 'L1_ffn_qn_g',
        'L1_ffn_kn_g', 'L1_ffn_gate_W', 'L1_ffn_gate_b', 'L1_ffn_W1', 'L1_ffn_b1', 'L1_ffn_W2', 'L1_ffn_b2']


def kernel(**inputs):
    import numpy as _np
    import concourse.bacc as _bacc
    from concourse import mybir as _mybir
    from concourse.bass_utils import run_bass_kernel_spmd as _run

    nc = _bacc.Bacc("TRN2", target_bir_lowering=False, num_devices=1)
    arrays, args = {}, []
    for name in _INS:
        a = _np.ascontiguousarray(inputs[name])
        arrays[f"in_{name}_dram"] = a
        args.append(nc.dram_tensor(f"in_{name}_dram", a.shape, _mybir.dt.from_np(a.dtype), kind="ExternalInput").ap())
    args.append(nc.dram_tensor("out_0_dram", (N, D), _mybir.dt.float32, kind="ExternalOutput").ap())
    build(nc, *args)
    r = _run(nc, [arrays], core_ids=[0])
    return r.results[0]["out_0_dram"]
```

```python
from contextlib import ExitStack

import concourse.bass as bass
from concourse import mybir

F32 = mybir.dt.float32
F32R = mybir.dt.float32r
BF16 = mybir.dt.bfloat16
F16 = mybir.dt.float16
I32 = mybir.dt.int32
ALU = mybir.AluOpType
ACT = mybir.ActivationFunctionType
AX_X = mybir.AxisListType.X

N = 1250
D = 512
TILE = 125
NT = N // TILE
FB = D // 128
CH = [(0, 500), (500, 500), (1000, 250)]
E = 8
HID = 256
HEADS, DH = 8, 64
EDGES = 21250
GROUPS, GT = 17, 10
NOH = 4
PRIME = 2 * GT
WIN = 128
LASTWIN = N - WIN
FEW = 3
EPS = 1e-5
BANKS = 8


def build(nc, x, src, dst, L0_gnn_Wl1, L0_gnn_bl1, L0_gnn_Wr1, L0_gnn_Wl2, L0_gnn_bl2, L0_gnn_Wr2,
          L0_mix_Wq, L0_mix_Wk, L0_mix_Wv, L0_mix_W1, L0_mix_W2,
          L0_ffn_Wg, L0_ffn_bg, L0_ffn_W1, L0_ffn_b1, L0_ffn_W2, L0_ffn_b2,
          L1_gnn_W1, L1_gnn_b1, L1_gnn_W2, L1_gnn_b2, L1_mix_W_qk,
          L1_ffn_ln_g, L1_ffn_ln_b, L1_ffn_Wq, L1_ffn_Wk, L1_ffn_Wv, L1_ffn_Wo, L1_ffn_qn_g, L1_ffn_kn_g,
          L1_ffn_gate_W, L1_ffn_gate_b, L1_ffn_W1, L1_ffn_b1, L1_ffn_W2, L1_ffn_b2, out):
    COL = {"bl1": 0, "gb1": 4, "m0b1": 12, "m1b1": 28, "ln_g": 44, "ln_b": 48, "qn_g": 52, "kn_g": 53}
    ctx = ExitStack()
    ctx = ExitStack()
    with ctx:
        def at(name, shape, dt, offset):
            return nc.alloc_sbuf_tensor_at(name, shape, dt, offset=offset)

        class AsF32:

            def __init__(self, t):
                self.t = t

            def __getitem__(self, idx):
                return self.t[idx].bitcast(F32)

        class Pair:

            def __init__(self, name, shape, offset, size=None, lo_at=None):
                size = lo_at - offset if lo_at else size or 4 * width(shape[1:])
                self.hi = at(name + "_hi", shape, F32R, offset)
                self.hi32 = AsF32(self.hi)
                self.lo = at(name + "_lo", shape, F32R, offset + size)
                self.lo32 = at(name + "_was", shape, F32, offset + size)

        def width(xs):
            p = 1
            for v in xs:
                p *= v
            return p

        BASE = 16512
        A0 = BASE
        SLOT = 20480
        S = [A0 + 50016 + SLOT * k for k in range(6)]
        WA0 = S[5] + SLOT
        WB0 = WA0 + 16384
        M0 = WB0 + 16384

        CNTB = at("CNTB", [128, N], F32, M0)
        ident = at("ident", [128, 128], F32, M0 + 5024)
        identb = at("identb", [128, 128], BF16, M0 + 5536)
        causal = at("causal", [125, 125], BF16, M0 + 5792)
        m = M0 + 6048
        LNS = [at(f"LNS{r}", [125, 16], F32, m + 64 * r) for r in range(2)]
        cols = at("cols", [128, 40], F32, m + 128)
        ccol = at("ccol", [128, 56], F32, m + 288)
        gate = at("gate", [125, NT, E], F32, m + 512)
        invc = at("invc", [125, NT], F32, m + 832)
        dinc = at("dinc", [125, NT], F32, m + 896)
        ones2 = at("ones2", [128, 8], F32, m + 960)
        flags = at("flags", [1, 24], I32, m + 992)
        zero = at("zero", [128, 8], F32, m + 1088)

        xn = Pair("xn", [125, NT, D], S[0], SLOT)
        xnT = Pair("xnT", [128, FB, N], S[2], SLOT)
        rawk = at("rawk", [128, FB, D], F32, S[4])
        raw2 = at("raw2", [128, FB, D], F32, S[4] + 8192)
        vecs = at("vecs", [54, 128], F32, A0 + 40960)
        rawq = at("rawq", [128, FB, D], F32, A0 + 32768)
        MI = Pair("MI", [128, FB, D], S[4])
        G = Pair("G", [128, FB, D], S[4] + 16384)
        T0 = S[4] + 32768
        xt_ = [at(f"x_t{r}", [125, D], F32, T0 + 2048 * r) for r in range(2)]
        xnf = [at(f"xnf{r}", [125, D], F32, T0 + 4096 + 2048 * r) for r in range(2)]
        bl2B = at("bl2B", [125, D], F32, T0 + 4096)
        W1p = Pair("W1p", [128, FB, D], A0)
        W2T = Pair("W2T", [128, FB, D], A0 + 16384)
        Wvp = Pair("Wvp", [128, FB, D], WB0)
        WA = Pair("WA", [128, FB, D], WA0)
        WB = Pair("WB", [128, FB, D], WB0)
        ctxp = Pair("ctx", [128, FB, D], A0)
        kT = [at(f"kT{r}", [128, N], F32, A0 + 16384 + 5024 * r) for r in range(2)]
        ek = Pair("ek", [125, NT, 128], A0 + 26432)
        c1 = [Pair(f"c1{r}", [128, FB, 128], A0 + 36672 + 4096 * r) for r in range(2)]
        cxt = at("cxt", [128, D], F32, A0 + 44864)
        c1f = at("c1f", [128, D], F32, A0 + 46912)
        qe = [at(f"qe{r}", [125, D], F32, A0 + 16384 + 2048 * r) for r in range(2)]
        qT = [Pair(f"qT{r}", [128, FB, TILE], A0 + 26432 + 4032 * r, 2016) for r in range(2)]
        AT = at("AT", [125, NT, N], F32R, A0)
        AT32 = at("AT32", [125, NT, N], F32, A0)
        e0 = S[0]
        srcI = at("srcI", [85, 2, 125], I32, e0)
        dstI = at("dstI", [85, 2, 125], I32, e0 + 1024)
        grpI = at("grpI", [GROUPS, N], I32, e0 + 2048)
        srcR = at("srcR", [85, 2, 125], F32, e0 + 7072)
        dstR = at("dstR", [85, 2, 125], F32, e0 + 8096)
        grpR = at("grpR", [GROUPS, N], F32, e0 + 9120)
        srcF = at("srcF", [125, 170], F32, e0 + 14144)
        dstF = at("dstF", [125, 170], F32, e0 + 14848)
        gst = at("gst", [GROUPS, 8], F32, e0 + 15552)
        gD = at("gD", [GROUPS, 2 * GROUPS], F32, e0 + 15584)
        wB = at("wB", [125, 24], F32, e0 + 15744)
        bW = at("bW", [125, 16], F32, e0 + 15872)
        onesA = at("onesA", [125, 128], F32, e0 + 15936)
        e1 = S[1]
        iota = at("iota", [125, N], F16, e1)
        iotaw = at("iotaw", [125, WIN], F16, e1 + 2528)
        colsum = at("colsum", [125, N], F32, e1 + 2784)
        ohs = [at(f"ohs{r}", [125, N], BF16, e1 + 7808 + 2528 * r) for r in range(NOH)]
        ohd = [at("ohd0", [125, GT, WIN], BF16, e1 + 17920), at("ohd1", [125, GT, WIN], BF16, e0 + 16448)]
        rows = at("rows", [125, 4 * GROUPS + 4], F32, e0 + 19712)
        rel = at("rel", [125, GROUPS * GT], F32, e0 + 19008)
        wraw = [at(f"wraw{r}", [128, FB, D], F32, S[4] + 8192 * r) for r in range(2)]
        wout = [at(f"wout{r}", [128, FB, D], F32, S[4] + 16384 + 8192 * r) for r in range(2)]

        PS = ctx.enter_context(nc.psum_tensor("PS", [128, BANKS, 512], F32))

        y = Pair("y", [125, NT, D], S[0], SLOT)
        hT = Pair("hT", [128, FB, N], S[4], SLOT)
        inv0 = at("inv0", [128, N], F32, S[4])
        INVB = at("INVB", [128, N], F32, WB0)
        sc = [at(f"sc{r}", [128, 500], F32, WB0 + 5024 + 2016 * r) for r in range(2)]
        xw = [at(f"xw{r}", [125, D], F32, WA0 + 2048 * r) for r in range(2)]
        xnw = [at(f"xnw{r}", [125, D], F32, WA0 + 4096 + 2048 * r) for r in range(2)]
        BIAS = 32
        acc = at("acc", [125, NT, D], F32, S[0])
        hE = [Pair(f"hE{r}", [128, 2, N], S[4 + r], 10016) for r in range(2)]
        W1P = [Pair(f"mW1{r}", [128, FB, HID], (WA0, WB0)[r]) for r in range(2)]
        W2P = [Pair(f"mW2{r}", [128, 2, D], (WA0, WB0)[r] + 8192) for r in range(2)]
        xm = [at(f"xm{r}", [125, D], F32, S[1] + 2048 * r) for r in range(2)]
        xnm = [at(f"xnm{r}", [125, D], F32, S[1] + 4096 + 2048 * r) for r in range(2)]
        GT_ = [WA0 + 10848, A0 + 40000]
        WgP = [Pair(f"WgP{s}", [128, FB, E], GT_[s], 128) for s in range(2)]
        b2P = [Pair(f"b2P{s}", [E, 1, D], GT_[s] + 256) for s in range(2)]
        bgB = [at(f"bgB{s}", [125, E], F32, GT_[s] + 4352) for s in range(2)]
        iota8 = at("iota8", [125, E], F32, GT_[0] + 4384)
        lgt = [at(f"lgt{s}", [125, NT, E], F32, GT_[s] + 4416) for s in range(2)]
        ex = [at(f"ex{s}", [125, NT, E], F32, GT_[s] + 4736) for s in range(2)]
        cand = at("cand", [125, NT, E], F32, GT_[0] + 5056)
        gred = [at(f"gred{s}", [125, 4, NT], F32, GT_[s] + 5376) for s in range(2)]
        gT = [Pair(f"gT{s}", [E, N], (WA0, A0)[s], 5024) for s in range(2)]
        xn2 = Pair("xn2", [125, NT, D], S[4], lo_at=S[0])
        QC = 2 * TILE
        kx = [at(f"kx{r}", [125, D], F32, S[1] + 2048 * r) for r in range(3)]
        kacc = at("kacc", [125, D], F32, S[1] + 6144)
        kp = [Pair(f"kp{r}", [125, D], S[1] + 8192 + 4096 * r) for r in range(2)]
        ksum = Pair("ksum", [128, FB, 2], S[1] + 16384)
        kv = Pair("kv", [128, FB, D], S[5])
        xq = [at(f"xq{r}", [125, D], F32, S[5] + 16384 + 2048 * r) for r in range(2)]
        q2 = [Pair(f"q2_{r}", [128, FB, QC], S[1] + 8064 * r, 4032) for r in range(2)]
        zT = Pair("zT", [128, FB, N], S[2], SLOT)
        h1T = Pair("h1T", [128, FB, N], S[1], lo_at=S[5])
        y3 = Pair("y3", [125, NT, D], S[4], lo_at=S[0])
        xg = [at(f"xg{r}", [125, D], F32, S[1] + 2048 * r) for r in range(2)]
        xnA = [at(f"xnA{r}", [125, D], F32, S[1] + 4096 + 2048 * r) for r in range(2)]
        xnB = [at(f"xnB{r}", [125, D], F32, S[1] + 8192 + 2048 * r) for r in range(2)]
        b2B = at("b2B", [125, D], F32, S[1] + 12288)
        gt_ = at("gt", [125, D], F32, S[1] + 14336)
        hxT = Pair("hxT", [128, FB, N], S[2], SLOT)
        QA = at("QA", [128, HEADS, N], F32R, A0)
        QA32 = AsF32(QA)
        KA = at("KA", [128, HEADS, N], F32R, S[0])
        KA32 = AsF32(KA)
        KLO = at("KLO", [128, FB, N], F32R, S[4])
        V32 = at("V32", [125, NT, D], F32, S[5])
        V = Pair("V", [125, NT, D], S[2], SLOT)
        sqr = [at(f"sqr{r}", [125, D], F32, A0 + 40000 + 2048 * r) for r in range(2)]
        unit = [at(f"unit{r}", [125, D], F32, A0 + 44096 + 2048 * r) for r in range(2)]
        XA, XB = A0 + 40000, WB0
        sel = at("sel", [128, 2, 128], F32R, XA)
        rowmax = at("rowmax", [128, N], F32R, M0)
        sacc = [at(f"sacc{a}", [125, 500], F32, XA + 1024 + 2016 * a) for a in range(2)]
        NP, NPT = 4, 3
        P = [at(f"P{r}", [125, 500], F32, (XA + 5056, XA + 7072, XB + 12096, XB + 14112)[r]) for r in range(NP)]
        PT = [Pair(f"PT{r}", [125, 500], XB + 4032 * r, 2016) for r in range(NPT)]
        chmax = at("chmax", [125, 2, NT, 3], F32, XA + 9088)
        negm = at("negm", [125, NT, 2], F32, XA + 9344)
        ones64 = at("ones64", [125, DH], F32, XA + 9440)
        maskall = at("maskall", [125, 125], BF16, XA + 9696)
        OT32 = at("OT32", [128, FB, N], F32, S[5])
        OT = at("OT", [128, FB, 2, N], F32R, A0)
        yT = Pair("yT", [128, FB, N], S[2], SLOT)
        def dram(name, shape):
            return nc.dram_tensor(name, shape, F32, kind="Internal").ap()

        torch_w = {"Wl1": L0_gnn_Wl1, "Wr1": L0_gnn_Wr1, "Wl2": L0_gnn_Wl2, "Wr2": L0_gnn_Wr2,
                   "Wqk0": L1_mix_W_qk[0:D, :], "Wqk1": L1_mix_W_qk[D:2 * D, :]}
        WT = {k: dram("WT_" + k, (D, D)) for k in torch_w}
        xa = dram("x_mixed", (N, D))
        xb = dram("x_r2", (N, D))
        xc = dram("x_one", (N, D))
        xd = dram("x_two", (N, D))
        xe = dram("x_mix1", (N, D))
        xf = dram("x_three", (N, D))

        def sem(name):
            return ctx.enter_context(nc.semaphore(name))

        filled = [sem(f"filled{b}") for b in range(BANKS)]
        drained = [sem(f"drained{b}") for b in range(BANKS)]
        hi_done = sem("hi_done")
        dve_step, act_step, pool_step = sem("dve_step"), sem("act_step"), sem("pool_step")
        const_ready = sem("const_ready")
        rawk_in, raw2_in, rawq_in = sem("rawk_in"), sem("raw2_in"), sem("rawq_in")
        wraw_in = [sem("wraw_in0"), sem("wraw_in1")]
        unit_in = [sem("unit_in0"), sem("unit_in1")]
        unit_hi, unit_ready = sem("unit_hi"), sem("unit_ready")
        x_in = [sem("x_in0"), sem("x_in1")]
        x_out = [sem("x_out0"), sem("x_out1")]
        ln_var, ln_std, ln_xnf, ln_hi = sem("ln_var"), sem("ln_std"), sem("ln_xnf"), sem("ln_hi")
        ln_lo = sem("ln_lo")
        mi_sum, mi_hi, mi_ready = sem("mi_sum"), sem("mi_hi"), sem("mi_ready")
        k_max = sem("k_max")
        cx_hi, cx_ready = sem("cx_hi"), sem("cx_ready")
        q_max, q_norm = sem("q_max"), sem("q_norm")
        vecs_in, bl2_in = sem("vecs_in"), sem("bl2_in")
        wt_out = [sem("wt_out0"), sem("wt_out1")]
        idx_in, idx_f = sem("idx_in"), sem("idx_f")
        edge_ready = sem("edge_ready")
        src_ready, dst_ready = sem("src_ready"), sem("dst_ready")
        edge_tiles, window_free = sem("edge_tiles"), sem("window_free")
        dst_squared, all_squared = sem("dst_squared"), sem("all_squared")
        all_src, all_dst, all_tiles, all_taken, all_rel = sem("all_src"), sem("all_dst"), sem("all_tiles"), sem("all_taken"), sem("all_rel")
        at_zero, at_built = sem("at_zero"), sem("at_built")
        sum_ready, deg_ready, deg_root = sem("sum_ready"), sem("deg_ready"), sem("deg_root")
        inv_ready = sem("inv_ready")

        inv_placed, a1_sum, a1_hi, a1_ready = sem("inv_placed"), sem("a1_sum"), sem("a1_hi"), sem("a1_ready")
        moe_in = [sem("moe0_in"), sem("moe1_in")]
        iota_ready = sem("iota_ready")
        wg_hi, wg_ready = sem("wg_hi"), sem("wg_ready")
        lg_less, lg_exp, gate_ready = sem("lg_less"), sem("lg_exp"), sem("gate_ready")
        hid_done, hid_hi, hid_ready = sem("hid_done"), sem("hid_hi"), sem("hid_ready")
        w_in = [[sem(f"w{m + 1}_in{r}") for m in range(2)] for r in range(2)]
        w_hi = [sem(f"w{m + 1}_hi") for m in range(2)]
        w_ready = [sem(f"w{m + 1}_ready") for m in range(2)]
        bias_placed = sem("bias_placed")
        x2_sum, xn2_lo = sem("x2_sum"), sem("xn2_lo")
        k_min, k_exped, k_hi, k_ready, k_used = (sem(n) for n in ("k_min", "k_exped", "k_hi", "k_ready", "k_used"))
        q_min, q_exped, q_hi, q_ready = (sem(n) for n in ("q_min", "q_exped", "q_hi", "q_ready"))
        kacc_done, self_loops = sem("kacc_done"), sem("self_loops")
        xs_whole, xs_scaled, xs_hi, xs_ready = (sem(n) for n in ("xs_whole", "xs_scaled", "xs_hi", "xs_ready"))
        z_hi, z_ready = sem("z_hi"), sem("z_ready")
        h1_hi, h1_ready = sem("h1_hi"), sem("h1_ready")
        y3_hi, y3_ready = sem("y3_hi"), sem("y3_ready")
        b2_in, x3_sum = sem("b2_in"), sem("x3_sum")
        hx_hi, hx_ready = sem("hx_hi"), sem("hx_ready")
        v_hi, v_ready = sem("v_hi"), sem("v_ready")
        squared, unit_sum, unit_root, unit_done = (sem(n) for n in ("squared", "unit_sum", "unit_root", "unit_done"))
        k_twice = sem("k_twice")
        att_ready, max_found = sem("att_ready"), sem("max_found")
        p_hi, p_ready, p_added, pt_used = sem("p_hi"), sem("p_ready"), sem("p_added"), sem("pt_used")
        sums_begun, ot_whole, ot_hi, ot_ready = sem("sums_begun"), sem("ot_whole"), sem("ot_hi"), sem("ot_ready")
        place, uses = {}, [0] * BANKS

        def plan(key, bank_):
            uses[bank_] += 1
            assert key not in place
            place[key] = (bank_, uses[bank_])

        ring_at = [0]

        def plan_ring(keys, ring=tuple(range(BANKS))):
            for key in keys:
                plan(key, ring[ring_at[0] % len(ring)])
                ring_at[0] += 1

        plan_ring([("xt", 0, i) for i in range(NT)])
        plan_ring([("wt", w, ib) for w in ("k", "2") for ib in range(FB)])
        plan_ring([("vec",)])
        plan_ring([("mi", b) for b in range(FB)])
        plan_ring([("g", b) for b in range(FB)])
        plan_ring([("wt", "q", ib) for ib in range(FB)])
        for b in range(FB + 1):
            if b == 0:
                plan_ring([("k", 0, c) for c in range(3)])
            if b + 1 < FB:
                plan_ring([("k", b + 1, c) for c in range(3)])
            if b < FB:
                plan_ring([("kt", b, q) for q in range(3)])
                plan_ring([("c1", b), ("c1t", b)])
            if b > 0:
                plan_ring([("cx", b - 1)])
        plan_ring([("q", 0)])
        for i in range(NT):
            if i + 1 < NT:
                plan_ring([("q", i + 1)])
            plan_ring([("qt", i), ("mo", i)])
        plan_ring([("wt", w, ib) for w in torch_w for ib in range(FB)])
        plan_ring([("ix",), ("wv",)])
        before_edges = list(uses)
        plan_ring([("cb", 0), ("cb", 1), ("cb", 2), ("cc",)])

        plan_ring([("y1", i) for i in range(NT)])
        plan_ring([("r1", f, c) for f in range(FB) for c in range(3)])
        plan_ring([("a1", f, c) for f in range(FB) for c in range(3)])
        plan_ring([("y2", i) for i in range(NT)])
        plan_ring([("r2", i) for i in range(NT)])
        for i in range(NT + 1):
            if i < NT:
                plan_ring([("a2", i)])
            if i >= 1:
                plan_ring([("xt", 1, i - 1)])
        lnno = {(s, i): NT * s + i for s in range(3) for i in range(NT)}
        lnno |= {(3 + s, i): 3 * NT + 2 * i + s for s in range(2) for i in range(NT)}
        UNITS = [("W1", 0), ("Wv", 1), ("Wl1", 0), ("Wr1", 1), ("Wl2", 0), ("Wr2", 1)]
        UNITS += [("Wqk1", 1), ("Wqk0", 0), ("gW1a", 1), ("gW2a", 0), ("gW1b", 1), ("gW2b", 0)]
        UNITS += [("aWv", 1), ("aWq", 0), ("aWk", 1), ("aWo", 0)]
        X_LOADS = ["x", "xmix", "xr2", "xa2", "xm0", "xq", "xa3", "xm1"]
        X_STORES = ["xmix", "xr2", "xa2", "xm0", "xq", "xa3", "xm1"]
        def plan_moe(s):
            plan_ring([("lt", s, c) for c in range(3)] + [("lg", s)])
            plan_ring([("gt", s, q) for q in range(3)])
            plan_ring([("ac", s, i) for i in range(NT)])
            hd = lambda e: plan_ring([("hd", s, e, f, c) for f in range(2) for c in range(3)])
            eo = lambda e: plan_ring([("eo", s, e, i) for i in range(NT)])
            hd(0)
            for h, o in ((1, 0), (2, 1)):
                hd(h)
                eo(o)
            for b in range(BANKS):
                uses[b] += 4 * (PAIRS - 1)
            hd(7)
            eo(6)
            if s == 1:
                eo(7)
            else:
                for i in range(NT + 1):
                    if i < NT:
                        plan_ring([("eo", s, 7, i)])
                    if i >= 1:
                        plan_ring([("xt", 2, i - 1)])

        PAIRS = E // 2 - 1
        plan_moe(0)
        LOW = (0, 1, 2, 3)
        for b in range(FB):
            plan(("kv", b), 4 + b)
        plan_ring([("k2", i) for i in range(NT)], LOW)
        plan(("ks",), 3)
        ring_at[0] = 0
        NQ = N // QC
        for g in range(NQ + 1):
            if g < NQ:
                plan_ring([("q2", g, f) for f in range(FB)])
            if g > 0:
                plan_ring([(k, i) for i in (2 * g - 2, 2 * g - 1) for k in ("dn", "mx")])
        plan_ring([("z", f, c) for f in range(FB) for c in range(3)])
        for hf in range(2):
            plan_ring([("h1", hf, f, c) for f in range(FB) for c in range(3)])
            plan_ring([("yy", hf, i) for i in range(NT)])
        for i in range(NT + 1):
            if i < NT:
                plan_ring([("a3", i)])
            if i >= 1:
                plan_ring([("xt", 4, i - 1)])
        HX = [(f, c) for f in range(FB) for c in range(3)]
        plan_ring([("pv", i) for i in range(NT)])
        for w in ("q", "k"):
            for i in range(NT + 1):
                if i < NT:
                    plan_ring([("p" + w, i)])
                if i >= 1:
                    plan_ring([("t" + w, i - 1)])
        STEPS = [(b, c, a, j) for b in range(FB) for c in range(3) for a in range(2)
                 for j in range((CH[c][0] + CH[c][1]) // TILE)]
        AT_STEP = {st: g for g, st in enumerate(STEPS)}
        PER_PAIR = len(STEPS) // FB
        LAG = 2

        def last_key(c):
            return (CH[c][0] + CH[c][1]) // TILE - 1

        def valid(c, j):
            o, w = CH[c]
            return (2 * TILE if TILE * j - o >= 2 * TILE else 0), w

        PIECES = [(a, i, q) for i in range(NT) for a in range(2) for q in range(i // 4 + 1)]

        def piece_width(i, q):
            return min(4, i + 1 - 4 * q) * TILE

        def max_work(b):
            return [("mx", b, *p) for p in PIECES] + [("mt", b, c) for c in range(3)]

        def done_by(g):
            return STEPS[g - LAG] if g >= LAG else None

        plan_ring(max_work(0), (0, 1, 2, 3))
        ring_at[0] = 0
        for b in range(1, FB):
            for key in max_work(b):
                plan(key, 3)
        for g, (b, c, a, j) in enumerate(STEPS):
            plan(("sT", g), g % 3)
        for n, (b, c, a) in enumerate([(b, c, a) for b in range(FB) for c in range(3) for a in range(2)]):
            plan(("ov", b, c, a), 4 + n % 3)
            if a == 0:
                plan(("ss", b, c), 7)
        plan_ring([("wo", f, c) for f, c in HX])
        plan_moe(1)

        def bank(key):
            return PS[:, place[key][0], :]

        def completed(eng, key, later=0):
            b, n = place[key]
            eng.wait_ge(filled[b], later + n)

        def carried(eng, key, later=0):
            b, n = place[key]
            eng.wait_ge(drained[b], later + n)

        def drain(ins, key):
            ins.then_inc(drained[place[key][0]], 1)

        def natural(w):
            return w.rearrange("(b p) n -> p b n", p=128)

        def row(v, parts=TILE):
            return v.rearrange("(a n) -> a n", a=1).broadcast_to((parts, v.shape[0]))

        xin = x.rearrange("(t p) d -> t p d", p=TILE)
        xav = xa.rearrange("(t p) d -> t p d", p=TILE)

        x_no = {}
        for key in [(s, i) for s in X_LOADS for i in range(NT)]:
            n = len(x_no)
            x_no[key] = (n % 2, n // 2 + 1)
        out_no = {}
        for key in [(s, i) for s in X_STORES for i in range(NT)]:
            n = len(out_no)
            out_no[key] = (n % 2, n // 2 + 1)

        def x_stored(eng, key):
            r, n = out_no[key]
            eng.wait_ge(x_out[r], 16 * n)

        unit_no, landed = {}, [0, 0]
        for name, region in UNITS:
            landed[region] += 16
            unit_no[name] = (region, landed[region], len(unit_no) + 1)

        def unit_pair(name):
            return {"W1": W1p, "Wv": Wvp}.get(name, (WA, WB)[unit_no[name][0]])

        def unit_split(eng, name):
            eng.wait_ge(unit_ready, unit_no[name][2])

        def x_landed(eng, key):
            r, n = x_no[key]
            eng.wait_ge(x_in[r], 16 * n)

        act_his, dve_los = [], []

        block = ctx.enter_context(nc.Block())

        @block.sync
        def _(sp):
            def load_x(key, view, i):
                r, n = x_no[key]
                sp.dma_start(xt_[r][:], view[i]).then_inc(x_in[r], 16)

            load_x(("x", 0), xin, 0)
            load_x(("x", 1), xin, 1)
            sp.dma_start(rawk[:], natural(L0_mix_Wk)).then_inc(rawk_in, 16)
            sp.dma_start(raw2[:], natural(L0_mix_W2)).then_inc(raw2_in, 16)
            sp.dma_start(W1p.lo32[:], natural(L0_mix_W1)).then_inc(unit_in[0], 16)
            sp.dma_start(Wvp.lo32[:], natural(L0_mix_Wv)).then_inc(unit_in[1], 16)
            sp.dma_start(rawq[:], natural(L0_mix_Wq)).then_inc(rawq_in, 16)
            v2 = lambda v: v.rearrange("(a p) -> a p", p=128)
            for name, v in (("bl1", v2(L0_gnn_bl1)), ("gb1", v2(L1_gnn_b1)),
                            ("m0b1", L0_ffn_b1.rearrange("e (f p) -> (e f) p", p=128)),
                            ("m1b1", L1_ffn_b1.rearrange("e (f p) -> (e f) p", p=128)),
                            ("ln_g", v2(L1_ffn_ln_g)), ("ln_b", v2(L1_ffn_ln_b))):
                sp.dma_start(vecs[COL[name]:COL[name] + v.shape[0], :], v).then_inc(vecs_in, 16)
            for name, v in (("qn_g", L1_ffn_qn_g), ("kn_g", L1_ffn_kn_g)):
                for h in range(2):
                    sp.dma_start(vecs[COL[name]:COL[name] + 1, h * DH:(h + 1) * DH],
                                 v.rearrange("(a n) -> a n", a=1)).then_inc(vecs_in, 16)
            for i in range(2, NT):
                sp.wait_ge(ln_xnf, i - 1)
                load_x(("x", i), xin, i)
            completed(sp, ("xt", 0, NT - 1))
            sp.wait_ge(ln_lo, NT)
            sp.dma_start(bl2B[:], row(L0_gnn_bl2)).then_inc(bl2_in, 16)
            for i in range(NT + 1):
                if i < NT:
                    if i >= 2:
                        sp.wait_ge(x_out[i % 2], 16 * (i // 2))
                    load_x(("xmix", i), xin, i)
                if i >= 1:
                    carried(sp, ("mo", i - 1))
                    sp.dma_start(xav[i - 1], xt_[(i - 1) % 2][:]).then_inc(x_out[(i - 1) % 2], 16)
            hv = lambda a: a.rearrange("(h p c) -> p h c", h=2, c=125)
            completed(sp, ("c1", FB - 1))
            sp.dma_start(srcI[:], hv(src)).then_inc(idx_in, 16)
            sp.dma_start(dstI[:], hv(dst)).then_inc(idx_in, 16)
            sp.dma_start(grpI[:], dst.rearrange("(g c) -> g c", g=GROUPS)).then_inc(idx_in, 16)
            completed(sp, ("mo", NT - 1))
            names = list(torch_w)
            for n in range(len(names) + 1):
                if n < len(names):
                    if n >= 2:
                        completed(sp, ("wt", names[n - 2], FB - 1))
                    sp.dma_start(wraw[n % 2][:], natural(torch_w[names[n]])).then_inc(wraw_in[n % 2], 16)
                if n >= 1:
                    for ib in range(FB):
                        carried(sp, ("wt", names[n - 1], ib))
                    sp.dma_start(natural(WT[names[n - 1]]), wout[(n - 1) % 2][:]).then_inc(wt_out[(n - 1) % 2], 16)
            def load_unit(name, view):
                region = unit_no[name][0]
                sp.dma_start((WA, WB)[region].lo32[:], view).then_inc(unit_in[region], 16)

            def expert_w1(region, W1, e):
                sp.dma_start(W1P[region].lo32[:], W1[bass.ds(e, 1)].rearrange("a (b p) n -> p (a b) n", p=128))\
                    .then_inc(w_in[region][0], 16)

            def expert_w2(region, W2, e):
                sp.dma_start(W2P[region].lo32[:], W2[bass.ds(e, 1)].rearrange("a (b p) n -> p (a b) n", p=128))\
                    .then_inc(w_in[region][1], 16)

            def expert_into(region, W1, W2, e):
                expert_w1(region, W1, e)
                expert_w2(region, W2, e)

            def load_transposed(name):
                n = names.index(name)
                sp.wait_ge(wt_out[n % 2], 16 * (n // 2 + 1))
                load_unit(name, natural(WT[name]))

            def load_tile(stage, i, view, ring):
                r, n = x_no[(stage, i)]
                sp.dma_start(ring[r][:], view[i]).then_inc(x_in[r], 16)

            def store_tile(stage, i, view, ring):
                r, n = out_no[(stage, i)]
                sp.dma_start(view[i], ring[r][:]).then_inc(x_out[r], 16)

            completed(sp, ("k", FB - 1, 2))
            load_transposed("Wl1")
            load_transposed("Wr1")
            completed(sp, ("y1", NT - 1))
            load_transposed("Wl2")
            sp.wait_ge(a1_ready, 3 * FB)
            load_transposed("Wr2")
            completed(sp, ("y2", NT - 1))
            xbv, xcv = (a.rearrange("(t p) d -> t p d", p=TILE) for a in (xb, xc))
            for i in range(NT + 1):
                if i < NT:
                    if i >= 2:
                        x_stored(sp, ("xr2", i - 2))
                    x_stored(sp, ("xmix", i))
                    load_tile("xr2", i, xav, xw)
                if i >= 1:
                    carried(sp, ("r2", i - 1))
                    store_tile("xr2", i - 1, xbv, xw)
            sp.dma_start(WgP[0].lo32[:], natural(L0_ffn_Wg)).then_inc(moe_in[0], 16)
            sp.dma_start(b2P[0].lo32[:], L0_ffn_b2.rearrange("e (a n) -> e a n", a=1)).then_inc(moe_in[0], 16)
            sp.dma_start(bgB[0][:], row(L0_ffn_bg)).then_inc(moe_in[0], 16)
            expert_into(1, L0_ffn_W1, L0_ffn_W2, 0)
            for i in range(NT + 1):
                if i < NT:
                    if i >= 2:
                        x_stored(sp, ("xa2", i - 2))
                        sp.wait_ge(ln_xnf, lnno[(1, i - 2)] + 1)
                    x_stored(sp, ("xr2", i))
                    load_tile("xa2", i, xbv, xw)
                if i >= 1:
                    carried(sp, ("a2", i - 1))
                    store_tile("xa2", i - 1, xcv, xw)
            def load_experts(s, W1, W2):
                with sp.Fori(0, PAIRS) as k:
                    for e in range(2):
                        completed(sp, ("hd", s, e, 1, 2), k * 4)
                        expert_w1(1 - e, W1, k * 2 + (e + 2))
                    for e in range(2):
                        completed(sp, ("eo", s, e, NT - 1), k * 4)
                        expert_w2(1 - e, W2, k * 2 + (e + 2))

            completed(sp, ("xt", 1, NT - 1))
            x_stored(sp, ("xa2", NT - 2))
            x_stored(sp, ("xa2", NT - 1))
            completed(sp, ("ac", 0, NT - 1))
            expert_into(0, L0_ffn_W1, L0_ffn_W2, 1)
            load_experts(0, L0_ffn_W1, L0_ffn_W2)
            completed(sp, ("eo", 0, E - 2, NT - 1))
            load_transposed("Wqk1")
            xdv = xd.rearrange("(t p) d -> t p d", p=TILE)
            for i in range(NT + 1):
                if i < NT:
                    if i >= 2:
                        x_stored(sp, ("xm0", i - 2))
                        sp.wait_ge(ln_xnf, lnno[(2, i - 2)] + 1)
                    load_tile("xm0", i, xcv, xm)
                if i >= 1:
                    sp.wait_ge(x2_sum, i)
                    store_tile("xm0", i - 1, xdv, xm)
            completed(sp, ("eo", 0, E - 1, NT - 1))
            load_transposed("Wqk0")
            completed(sp, ("k2", NT - 1))
            load_unit("gW1a", natural(L1_gnn_W1[:, 0:D]))
            xev, xfv = (a.rearrange("(t p) d -> t p d", p=TILE) for a in (xe, xf))
            for i in range(NT + 1):
                if i < NT:
                    if i >= 2:
                        x_stored(sp, ("xq", i - 2))
                    if i < 2:
                        completed(sp, ("eo", 0, E - 1, NT - 1))
                    x_stored(sp, ("xm0", i))
                    load_tile("xq", i, xdv, xq)
                if i >= 1:
                    carried(sp, ("mx", i - 1))
                    store_tile("xq", i - 1, xev, xq)
                if i == NT - 1:
                    completed(sp, ("q2", NQ - 1, FB - 1))
                    load_unit("gW2a", natural(L1_gnn_W2[0:D, :]))
            completed(sp, ("h1", 0, FB - 1, 2))
            load_unit("gW1b", natural(L1_gnn_W1[:, D:2 * D]))
            completed(sp, ("yy", 0, NT - 1))
            load_unit("gW2b", natural(L1_gnn_W2[D:2 * D, :]))
            completed(sp, ("h1", 1, FB - 1, 2))
            load_unit("aWv", natural(L1_ffn_Wv))
            completed(sp, ("yy", 1, NT - 1))
            load_unit("aWq", natural(L1_ffn_Wq))
            sp.dma_start(b2B[:], row(L1_gnn_b2)).then_inc(b2_in, 16)
            for i in range(NT + 1):
                if i < NT:
                    if i >= 2:
                        x_stored(sp, ("xa3", i - 2))
                        sp.wait_ge(ln_xnf, lnno[(3, i - 2)] + 1)
                    x_stored(sp, ("xq", i))
                    load_tile("xa3", i, xev, xg)
                if i >= 1:
                    sp.wait_ge(x3_sum, i)
                    store_tile("xa3", i - 1, xfv, xg)
            completed(sp, ("pv", NT - 1))
            load_unit("aWk", natural(L1_ffn_Wk))
            completed(sp, ("pq", NT - 1))
            load_unit("aWo", natural(L1_ffn_Wo))
            last = ("ov", FB - 1, 2, 1)
            carried(sp, last)
            sp.dma_start(WgP[1].lo32[:], natural(L1_ffn_gate_W)).then_inc(moe_in[1], 16)
            sp.dma_start(b2P[1].lo32[:], L1_ffn_b2.rearrange("e (a n) -> e a n", a=1)).then_inc(moe_in[1], 16)
            sp.dma_start(bgB[1][:], row(L1_ffn_gate_b)).then_inc(moe_in[1], 16)
            expert_into(1, L1_ffn_W1, L1_ffn_W2, 0)
            completed(sp, ("wo", FB - 1, 2))
            expert_into(0, L1_ffn_W1, L1_ffn_W2, 1)
            load_experts(1, L1_ffn_W1, L1_ffn_W2)
            outv = out.rearrange("(t p) d -> t p d", p=TILE)
            for i in range(NT + 1):
                if i < NT:
                    if i >= 2:
                        x_stored(sp, ("xm1", i - 2))
                    x_stored(sp, ("xa3", i))
                    load_tile("xm1", i, xfv, xm)
                if i >= 1:
                    sp.wait_ge(x2_sum, NT + i)
                    store_tile("xm1", i - 1, outv, xm)
            x_stored(sp, ("xm1", NT - 2))
            x_stored(sp, ("xm1", NT - 1))

        @block.gpsimd
        def _(pool):
            steps = [0]

            def link(ins):
                steps[0] += 1
                ins.then_inc(pool_step, 1)
                pool.wait_ge(pool_step, steps[0])

            link(pool.memset(ident[:], 0.0))
            pool.affine_select(out=ident[:], in_=ident[:], compare_op=ALU.not_equal, fill=1.0, base=0,
                               pattern=[[-1, 128]], channel_multiplier=1).then_inc(const_ready, 1)
            pool.wait_ge(const_ready, 1)
            link(pool.memset(ones2[:], 1.0))
            link(pool.memset(zero[:], 0.0))
            link(pool.memset(causal[:], 0.0))
            link(pool.affine_select(out=causal[:], in_=causal[:], compare_op=ALU.is_ge, fill=-1e30, base=0,
                                    pattern=[[-1, 125]], channel_multiplier=1))
            link(pool.tensor_copy(identb[:], ident[:]))

            def rounded(pair):
                was = pair.lo32[:]
                none = zero[0:was.shape[0], 0:1].broadcast_to((was.shape[0], was.shape[1] * was.shape[2]))\
                    .rearrange("p (b n) -> p b n", b=was.shape[1])
                return pool.tensor_tensor(pair.hi[:], was, none, ALU.add)

            def split(name):
                region, landed_, _ = unit_no[name]
                pair = unit_pair(name)
                pool.wait_ge(unit_in[region], landed_)
                rounded(pair).then_inc(unit_hi, 1)
                pool.wait_ge(unit_hi, unit_no[name][2])
                pool.tensor_tensor(pair.lo[:], pair.lo32[:], pair.hi32[:], ALU.subtract).then_inc(unit_ready, 1)

            split("W1")
            split("Wv")

            completed(pool, ("c1", FB - 1))
            link(pool.iota(iota[:], pattern=[[1, N]], base=0, channel_multiplier=0,
                           allow_small_or_imprecise_dtypes=True))
            link(pool.iota(bW[:, 0:NT], pattern=[[WIN, NT]], base=0, channel_multiplier=0,
                           allow_small_or_imprecise_dtypes=True))
            link(pool.iota(iotaw[:], pattern=[[1, WIN]], base=0, channel_multiplier=0,
                           allow_small_or_imprecise_dtypes=True))
            link(pool.memset(bW[:, NT - 1:NT], float(LASTWIN)))
            pool.memset(onesA[:], 1.0).then_inc(const_ready, 1)
            completed(pool, ("mo", NT - 1))
            pool.memset(AT[:].bitcast(F32), 0.0).then_inc(at_zero, 1)

            for name in ("Wl1", "Wr1", "Wl2", "Wr2"):
                split(name)
            def split_gate_weights(s):
                pool.wait_ge(moe_in[s], 48)
                for n, pair in enumerate((WgP[s], b2P[s])):
                    rounded(pair).then_inc(wg_hi, 1)
                    pool.wait_ge(wg_hi, 2 * s + n + 1)
                    pool.tensor_tensor(pair.lo[:], pair.lo32[:], pair.hi32[:], ALU.subtract).then_inc(wg_ready, 1)

            def split_experts(s):
                def part(e, e_, m):
                    region = 1 - e % 2
                    pair = (W1P, W2P)[m][region]
                    pool.wait_ge(w_in[region][m], (e_ - e % 2) * 8 + (64 * s + 16))
                    rounded(pair).then_inc(w_hi[m], 1)
                    pool.wait_ge(w_hi[m], e_ + (E * s + 1))
                    pool.tensor_tensor(pair.lo[:], pair.lo32[:], pair.hi32[:], ALU.subtract).then_inc(w_ready[m], 1)

                for e in range(2):
                    part(e, e, 0)
                    part(e, e, 1)
                with pool.Fori(0, PAIRS) as k:
                    for m in range(2):
                        for e in (2, 3):
                            part(e, k * 2 + e, m)

            completed(pool, ("y2", NT - 1))
            pool.iota(iota8[:], pattern=[[1, E]], base=0, channel_multiplier=0,
                      allow_small_or_imprecise_dtypes=True).then_inc(iota_ready, 1)
            split_gate_weights(0)
            split_experts(0)
            split("Wqk1")
            pool.wait_ge(xn2_lo, NT)
            completed(pool, ("xt", 2, NT - 1))
            pool.memset(kacc[:], 0.0).then_inc(kacc_done, 1)
            for i in range(NT):
                if i == 1:
                    split("Wqk0")
                carried(pool, ("k2", i))
                pool.wait_ge(kacc_done, i + 1)
                pool.tensor_tensor(kacc[:], kacc[:], kx[i % 3][:], ALU.add).then_inc(kacc_done, 1)
            completed(pool, ("kv", FB - 1))
            for i in range(NT):
                pool.tensor_tensor(xn2.lo32[:, i, :], xn2.hi32[:, i, :], xn2.lo[:, i, :].bitcast(F32), ALU.add)\
                    .then_inc(xs_whole, 1)
            for name in ("gW1a", "gW2a", "gW1b", "gW2b", "aWv", "aWq", "aWk"):
                split(name)
            completed(pool, ("pk", NT - 1))
            none = zero[0:TILE, 0:1].broadcast_to((TILE, D))
            for i in range(NT):
                pool.tensor_tensor(V.hi[:, i, :], V32[:, i, :], none, ALU.add).then_inc(v_hi, 1)
                pool.wait_ge(v_hi, i + 1)
                pool.tensor_tensor(V.lo[:, i, :], V32[:, i, :], V.hi32[:, i, :], ALU.subtract).then_inc(v_ready, 1)
            split("aWo")
            for g, (b, c, a, j) in enumerate(STEPS):
                carried(pool, ("sT", g))
                off, w = valid(c, j)
                if j == 0:
                    if (b, c) != (0, 0):
                        before = (b, c - 1) if c else (b - 1, 2)
                        if a == 0:
                            pool.wait_ge(sums_begun, 3 * b + c)
                        else:
                            completed(pool, ("ss", *before))
                    pool.tensor_tensor(sacc[a][:, 0:w], P[g % NP][:, 0:w], zero[0:TILE, 0:1].broadcast_to((TILE, w)),
                                       ALU.add).then_inc(p_added, 1)
                else:
                    pool.wait_ge(p_added, g)
                    pool.tensor_tensor(sacc[a][:, off:w], sacc[a][:, off:w], P[g % NP][:, off:w], ALU.add)\
                        .then_inc(p_added, 1)
            split_gate_weights(1)
            split_experts(1)

        @block.scalar
        def _(act):
            def hi(key, dst_, src_):
                completed(act, key)
                act_his.append(key)
                act.activation(dst_, src_, ACT.Copy).then_inc(hi_done, 1)

            def ln_sqrt(s, i):
                n = lnno[(s, i)]
                st = LNS[n % 2]
                act.wait_ge(ln_var, n + 1)
                act.activation(st[:, 9:10], st[:, 8:9], ACT.Sqrt).then_inc(ln_std, 1)

            def ln_T_hi(s, i, T):
                key = ("xt", s, i)
                hi(key, T.hi[:, :, i * TILE:(i + 1) * TILE],
                   bank(key)[:, 0:FB * TILE].rearrange("p (b n) -> p b n", b=FB))

            ln_sqrt(0, 0)
            for i in range(NT + 1):
                if i + 1 < NT:
                    ln_sqrt(0, i + 1)
                if i < NT:
                    act.wait_ge(ln_xnf, i + 1)
                    act.activation(xn.hi[:, i, :], xnf[i % 2][:], ACT.Copy).then_inc(ln_hi, 1)
                if i >= 1:
                    ln_T_hi(0, i - 1, xnT)
            for w, W in (("k", WA), ("2", W2T)):
                for ib in range(FB):
                    hi(("wt", w, ib), W.hi[:, ib, :], bank(("wt", w, ib)))
            for b in range(FB):
                act.wait_ge(mi_sum, b + 1)
                act.activation(MI.hi[:, b, :], MI.lo32[:, b, :], ACT.Copy).then_inc(mi_hi, 1)
            for b in range(FB):
                hi(("g", b), G.hi[:, b, :], bank(("g", b)))
            for ib in range(FB):
                hi(("wt", "q", ib), WB.hi[:, ib, :], bank(("wt", "q", ib)))

            def k_exp(b):
                act.wait_ge(k_max, b + 1)
                if b >= 2:
                    completed(act, ("kt", b - 2, 2))
                o_ = 8 * (b % 2)
                for c, (o, w) in enumerate(CH):
                    drain(act.activation(kT[b % 2][:, o:o + w], bank(("k", b, c))[:, 0:w], ACT.Exp,
                                         bias=cols[:, o_ + 3:o_ + 4],
                                         accum_out=cols[:, o_ + 4 + c:o_ + 5 + c]), ("k", b, c))

            k_exp(0)
            for b in range(FB + 1):
                if b + 1 < FB:
                    k_exp(b + 1)
                if b < FB:
                    for q in range(3):
                        n = min(4, NT - 4 * q)
                        key = ("kt", b, q)
                        hi(key, ek.hi[:, 4 * q:4 * q + n, :],
                           bank(key)[0:TILE, 0:128 * n].rearrange("p (t d) -> p t d", t=n))
                    if b > 0:
                        completed(act, ("c1t", b - 1))
                    completed(act, ("c1", b))
                    drain(act.activation(c1f[:], bank(("c1", b)), ACT.Copy), ("c1", b))
                    hi(("c1t", b), c1[b % 2].hi[:], bank(("c1t", b)).rearrange("p (c d) -> p c d", c=FB))
                if b > 0:
                    carried(act, ("cx", b - 1))
                    act.activation(ctxp.hi[:, b - 1, :], cxt[:], ACT.Copy).then_inc(cx_hi, 1)

            def q_exp(i):
                act.wait_ge(q_max, i + 1)
                if i >= 2:
                    completed(act, ("qt", i - 2))
                c = 16 + 4 * (i % 2)
                drain(act.activation(qe[i % 2][:], bank(("q", i))[0:TILE, :], ACT.Exp,
                                     bias=cols[0:TILE, c:c + 1], accum_out=cols[0:TILE, c + 1:c + 2]), ("q", i))

            q_exp(0)
            for i in range(NT):
                if i + 1 < NT:
                    q_exp(i + 1)
                if i >= 2:
                    completed(act, ("mo", i - 2))
                hi(("qt", i), qT[i % 2].hi[:], bank(("qt", i))[:, 0:FB * TILE].rearrange("p (b n) -> p b n", b=FB))
            for n, name in enumerate(torch_w):
                for ib in range(FB):
                    completed(act, ("wt", name, ib))
                    if n >= 2 and ib == 0:
                        act.wait_ge(wt_out[n % 2], 16 * (n // 2))
                    drain(act.activation(wout[n % 2][:, ib, :], bank(("wt", name, ib)), ACT.Copy), ("wt", name, ib))

            act.wait_ge(edge_ready, 1)
            fit = act.value_load(flags[0:1, 20:21], min_val=0, max_val=1)

            def onehot_dst(g, r, square, ready):
                for t in range(GT):
                    ins = act.activation(ohd[r][:, t, :], iotaw[:], ACT.Square, bias=rel[:, bass.ds(g * GT + t, 1)])
                ins.then_inc(square, 1)
                act.wait_ge(square, g + 1)
                act.activation(ohd[r][:], ohd[r][:], ACT.Relu, bias=1.0, scale=-1.0).then_inc(ready, 1)

            with act.If(fit == 1):
                with act.Fori(0, GROUPS // 2) as k:
                    for r in range(2):
                        act.wait_ge(edge_tiles, k * (2 * GT) + (r * GT + PRIME - GT))
                        onehot_dst(k * 2 + r, r, dst_squared, dst_ready)
                act.wait_ge(edge_tiles, (GROUPS - 1) * GT + PRIME - GT)
                onehot_dst(GROUPS - 1, 0, dst_squared, dst_ready)
            with act.Else():
                with act.Fori(0, NT) as w:
                    act.activation(rel[:], dstF[:], ACT.Identity, bias=bW[:, bass.ds(w, 1)], scale=-1.0)\
                        .then_inc(all_rel, 1)
                    act.wait_ge(all_rel, w + 1)
                    with act.Fori(0, GROUPS) as g:
                        act.wait_ge(all_tiles, w * (GROUPS * GT) + g * GT + 1)
                        for t in range(GT):
                            ins = act.activation(ohd[0][:, t, :], iotaw[:], ACT.Square,
                                                 bias=rel[:, bass.ds(g * GT + t, 1)])
                        ins.then_inc(all_squared, 1)
                        act.wait_ge(all_squared, w * GROUPS + g + 1)
                        act.activation(ohd[0][:], ohd[0][:], ACT.Relu, bias=1.0, scale=-1.0).then_inc(all_dst, 1)
            act.wait_ge(deg_ready, 1)
            act.activation(dinc[:], dinc[:], ACT.Sqrt).then_inc(deg_root, 1)

            for i in range(NT):
                hi(("y1", i), y.hi[:, i, :], bank(("y1", i))[0:TILE, :])
            act.wait_ge(deg_ready, 2)
            act.activation(CNTB[:], CNTB[:], ACT.Sqrt).then_inc(deg_root, 1)
            completed(act, ("ix",))
            for f in range(FB):
                for c, (o, w) in enumerate(CH):
                    key = ("r1", f, c)
                    completed(act, key)
                    drain(act.activation(hT.lo32[:, f, o:o + w], bank(key)[:, 0:w], ACT.Identity,
                                         bias=ccol[:, COL["bl1"] + f:COL["bl1"] + f + 1]), key)
            n = 0
            for f in range(FB):
                for c, (o, w) in enumerate(CH):
                    n += 1
                    act.wait_ge(a1_sum, n)
                    act.activation(hT.hi[:, f, o:o + w], hT.lo32[:, f, o:o + w], ACT.Relu).then_inc(a1_hi, 1)
            for i in range(NT):
                hi(("y2", i), y.hi[:, i, :], bank(("y2", i))[0:TILE, :])
            ln_sqrt(1, 0)
            for i in range(NT):
                if i + 1 < NT:
                    ln_sqrt(1, i + 1)
                ln_T_hi(1, i, xnT)
            def gate_exp(s):
                act.wait_ge(lg_less, s + 1)
                act.activation(ex[s][:], lgt[s][:], ACT.Exp).then_inc(lg_exp, 1)

            def acc_starts(s):
                for c, (o, w) in enumerate(CH):
                    hi(("gt", s, c), gT[s].hi[:, o:o + w], bank(("gt", s, c))[0:E, 0:w])
                for i in range(NT):
                    key = ("ac", s, i)
                    completed(act, key)
                    drain(act.activation(acc[:, i, :], bank(key)[0:TILE, :], ACT.Copy), key)

            def hidden(s, e, e_, later, func):
                act.wait_ge(bias_placed, e_ + (E * s + 1))
                for f in range(2):
                    for c, (o, w) in enumerate(CH):
                        key = ("hd", s, e, f, c)
                        completed(act, key, later)
                        b_ = BIAS + 2 * (e % 2) + f
                        drain(act.activation(hE[e % 2].lo32[:, f, o:o + w], bank(key)[:, 0:w], func,
                                             bias=cols[:, b_:b_ + 1]), key)

            def hiddens(s, func):
                hidden(s, 0, 0, 0, func)
                with act.Fori(0, PAIRS) as k:
                    hidden(s, 1, k * 2 + 1, k * 4, func)
                    hidden(s, 2, k * 2 + 2, k * 4, func)
                hidden(s, 7, 7, 0, func)

            gate_exp(0)
            acc_starts(0)
            hiddens(0, ACT.Relu)
            ln_sqrt(2, 0)
            for i in range(NT + 1):
                if i + 1 < NT:
                    ln_sqrt(2, i + 1)
                if i < NT:
                    act.wait_ge(ln_xnf, lnno[(2, i)] + 1)
                    act.activation(xn2.hi[:, i, :], xnm[i % 2][:], ACT.Copy).then_inc(ln_hi, 1)
                if i >= 1:
                    ln_T_hi(2, i - 1, xnT)
            for i in range(NT):
                act.wait_ge(k_min, i + 1)
                act.activation(kx[i % 3][:], kx[i % 3][:], ACT.Exp).then_inc(k_exped, 1)
                carried(act, ("k2", i))
                if i >= 2:
                    act.wait_ge(k_used, i - 1)
                act.activation(kp[i % 2].hi[:], kx[i % 3][:], ACT.Copy).then_inc(k_hi, 1)
            for b in range(FB):
                hi(("kv", b), kv.hi[:, b, :], bank(("kv", b)))
            hi(("ks",), ksum.hi[:], bank(("ks",))[:, 0:2 * FB].rearrange("p (b a) -> p b a", b=FB))

            def q_exps(g, f):
                act.wait_ge(q_min, g * FB + f + 1)
                q_ = q2[g % 2].lo32[:, f, :]
                act.activation(q_, q_, ACT.Exp).then_inc(q_exped, 1)

            def q_his(g, f):
                carried(act, ("q2", g, f))
                act.activation(q2[g % 2].hi[:, f, :], q2[g % 2].lo32[:, f, :], ACT.Copy).then_inc(q_hi, 1)

            for g in range(NQ):
                for f in range(FB + 1):
                    if f < FB:
                        q_exps(g, f)
                    if f > 0:
                        q_his(g, f - 1)
                for i in (2 * g, 2 * g + 1):
                    act.wait_ge(xs_scaled, i + 1)
                    act.activation(xn2.hi[:, i, :], xn2.lo32[:, i, :], ACT.Copy).then_inc(xs_hi, 1)
            for n, (f, c) in enumerate(HX):
                o, w = CH[c]
                carried(act, ("z", f, c))
                act.activation(zT.hi[:, f, o:o + w], zT.lo32[:, f, o:o + w], ACT.Copy).then_inc(z_hi, 1)
            x_stored(act, ("xq", NT - 2))
            x_stored(act, ("xq", NT - 1))
            for hf in range(2):
                for f, c in HX:
                    o, w = CH[c]
                    key = ("h1", hf, f, c)
                    completed(act, key)
                    b_ = COL["gb1"] + FB * hf + f
                    drain(act.activation(h1T.lo32[:, f, o:o + w], bank(key)[:, 0:w], ACT.Relu,
                                         bias=ccol[:, b_:b_ + 1]), key)
                    carried(act, key)
                    act.activation(h1T.hi[:, f, o:o + w], h1T.lo32[:, f, o:o + w], ACT.Copy).then_inc(h1_hi, 1)
                for i in range(NT):
                    key = ("yy", hf, i)
                    if hf == 0:
                        completed(act, key)
                        drain(act.activation(y3.lo32[:, i, :], bank(key)[0:TILE, :], ACT.Copy,
                                             scale=dinc[:, i:i + 1]), key)
                    else:
                        carried(act, key)
                        act.activation(y3.hi[:, i, :], y3.lo32[:, i, :], ACT.Copy).then_inc(y3_hi, 1)

            def gained(i):
                key = ("xt", 4, i)
                completed(act, key)
                sl = slice(i * TILE, (i + 1) * TILE)
                for b in range(FB):
                    g_, b_ = COL["ln_g"] + b, COL["ln_b"] + b
                    ins = act.activation(hxT.lo32[:, b, sl], bank(key)[:, b * TILE:(b + 1) * TILE], ACT.Identity,
                                         bias=ccol[:, b_:b_ + 1], scale=ccol[:, g_:g_ + 1])
                drain(ins, key)
                carried(act, key)
                act.activation(hxT.hi[:, :, sl], hxT.lo32[:, :, sl], ACT.Copy).then_inc(hx_hi, 1)

            for i in range(NT):
                ln_sqrt(3, i)
                ln_sqrt(4, i)
                if i >= 1:
                    gained(i - 1)
            gained(NT - 1)
            for i in range(NT):
                completed(act, ("pv", i))
                drain(act.activation(V32[:, i, :], bank(("pv", i))[0:TILE, :], ACT.Copy), ("pv", i))

            def squares(s, w, i):
                completed(act, ("p" + w, i))
                if i >= 2 or s:
                    act.wait_ge(unit_sum, NT * s + i - 1)
                act.activation(sqr[i % 2][:], bank(("p" + w, i))[0:TILE, :], ACT.Square).then_inc(squared, 1)

            def roots(s, i):
                c = 8 * (i % 2)
                act.wait_ge(unit_sum, NT * s + i + 1)
                act.activation(cols[0:TILE, 16 + c:24 + c], cols[0:TILE, c:c + 8], ACT.Sqrt).then_inc(unit_root, 1)

            even, odd = slice(0, HEADS, 2), slice(1, HEADS, 2)
            up, down = slice(0, DH), slice(DH, 2 * DH)

            def transposed(w, i):
                return bank(("t" + w, i))[:, 0:FB * TILE].rearrange("p (b n) -> p b n", b=FB)

            for s, (w, dst_, gain) in enumerate((("q", QA, "qn_g"), ("k", KA, "kn_g"))):
                g_ = ccol[:, COL[gain]:COL[gain] + 1]
                squares(s, w, 0)
                roots(s, 0)
                for i in range(NT):
                    if i + 1 < NT:
                        squares(s, w, i + 1)
                        roots(s, i + 1)
                    key = ("t" + w, i)
                    sl = slice(i * TILE, (i + 1) * TILE)
                    completed(act, key)
                    t_ = transposed(w, i)
                    act.activation(dst_[up, even, sl], t_[up], ACT.Copy, scale=g_[up])
                    act_his.append(key)
                    act.activation(dst_[down, odd, sl], t_[down], ACT.Copy, scale=g_[down]).then_inc(hi_done, 1)
                    if w == "k":
                        act.wait_ge(hi_done, len(act_his))
                        act.activation(KA[down, even, sl], KA32[up, even, sl], ACT.Copy)
                        act.activation(KA[up, odd, sl], KA32[down, odd, sl], ACT.Copy).then_inc(k_twice, 1)

            def used_by_v(eng, g):
                b, c, a, j = STEPS[g]
                if j == last_key(c):
                    completed(eng, ("ov", b, c, a))
                else:
                    eng.wait_ge(pt_used, sum(st[3] < last_key(st[1]) for st in STEPS[:g + 1]))

            def pair_out_hi(b):
                act.wait_ge(ot_whole, 3 * (b + 1))
                act.activation(OT[:, b, 0, :], OT32[:, b, :], ACT.Copy).then_inc(ot_hi, 1)

            for g, (b, c, a, j) in enumerate(STEPS):
                key = ("sT", g)
                off, w = valid(c, j)
                completed(act, key)
                if g >= NP:
                    act.wait_ge(p_ready, g - NP + 1)
                    act.wait_ge(p_added, g - NP + 1)
                drain(act.activation(P[g % NP][:, off:w], bank(key)[0:TILE, off:w], ACT.Exp), key)
                carried(act, key)
                if g >= NPT:
                    used_by_v(act, g - NPT)
                act.activation(PT[g % NPT].hi[:, off:w], P[g % NP][:, off:w], ACT.Copy).then_inc(p_hi, 1)
                if b > 0 and (c, a, j) == (0, 1, 0):
                    pair_out_hi(b - 1)
            pair_out_hi(FB - 1)
            for f, c in HX:
                o, w = CH[c]
                hi(("wo", f, c), yT.hi[:, f, o:o + w], bank(("wo", f, c))[:, 0:w])
            gate_exp(1)
            acc_starts(1)
            hiddens(1, ACT.Gelu_apprx_tanh)

        @block.vector
        def _(dve):
            steps = [0]

            def link(ins):
                steps[0] += 1
                ins.then_inc(dve_step, 1)
                dve.wait_ge(dve_step, steps[0])

            def lo(key, dst_, src_, hi_):
                dve_los.append(key)
                dve.wait_ge(hi_done, len(dve_los))
                drain(dve.tensor_tensor(dst_, src_, hi_, ALU.subtract), key)

            def ln_stats(s, i, x_):
                n = lnno[(s, i)]
                st = LNS[n % 2]
                if n >= 2:
                    dve.wait_ge(ln_xnf, n - 1)
                link(dve.bn_stats(st[:, 0:6], x_))
                link(dve.bn_aggr(st[:, 6:8], st[:, 0:6]))
                dve.tensor_scalar(st[:, 8:9], st[:, 7:8], EPS, None, ALU.add).then_inc(ln_var, 1)

            def ln_norm(s, i, x_, xnf_):
                n = lnno[(s, i)]
                st = LNS[n % 2]
                dve.wait_ge(ln_std, n + 1)
                link(dve.reciprocal(st[:, 10:11], st[:, 9:10]))
                dve.tensor_scalar(xnf_, x_, st[:, 6:7], st[:, 10:11], ALU.subtract, ALU.mult).then_inc(ln_xnf, 1)

            def ln_T_lo(s, i, T):
                key = ("xt", s, i)
                sl = slice(i * TILE, (i + 1) * TILE)
                lo(key, T.lo[:, :, sl], bank(key)[:, 0:FB * TILE].rearrange("p (b n) -> p b n", b=FB), T.hi32[:, :, sl])

            x_landed(dve, ("x", 0))
            ln_stats(0, 0, xt_[0][:])
            for i in range(NT + 1):
                if i + 1 < NT:
                    x_landed(dve, ("x", i + 1))
                    ln_stats(0, i + 1, xt_[(i + 1) % 2][:])
                if i < NT:
                    if i >= 2:
                        completed(dve, ("xt", 0, i - 2))
                        dve.wait_ge(ln_lo, i - 1)
                    ln_norm(0, i, xt_[i % 2][:], xnf[i % 2][:])
                    dve.wait_ge(ln_hi, i + 1)
                    dve.tensor_tensor(xn.lo[:, i, :], xnf[i % 2][:], xn.hi32[:, i, :], ALU.subtract)\
                        .then_inc(ln_lo, 1)
                if i >= 1:
                    ln_T_lo(0, i - 1, xnT)
            for w, W in (("k", WA), ("2", W2T)):
                for ib in range(FB):
                    lo(("wt", w, ib), W.lo[:, ib, :], bank(("wt", w, ib)), W.hi32[:, ib, :])
            completed(dve, ("vec",))
            drain(dve.tensor_copy(ccol[:, 0:54], bank(("vec",))[:, 0:54]), ("vec",))
            for b in range(FB):
                key = ("mi", b)
                completed(dve, key)
                drain(dve.tensor_copy(MI.lo32[:, b, :], bank(key)), key)
                carried(dve, key)
                sl = slice(b * 128, (b + 1) * 128)
                dve.tensor_tensor(MI.lo32[:, b, sl], MI.lo32[:, b, sl], ident[:], ALU.add).then_inc(mi_sum, 1)
                dve.wait_ge(mi_hi, b + 1)
                dve.tensor_tensor(MI.lo[:, b, :], MI.lo32[:, b, :], MI.hi32[:, b, :], ALU.subtract)\
                    .then_inc(mi_ready, 1)
            for b in range(FB):
                lo(("g", b), G.lo[:, b, :], bank(("g", b)), G.hi32[:, b, :])
            for ib in range(FB):
                lo(("wt", "q", ib), WB.lo[:, ib, :], bank(("wt", "q", ib)), WB.hi32[:, ib, :])

            def k_maxs(b):
                o_ = 8 * (b % 2)
                for c, (o, w) in enumerate(CH):
                    completed(dve, ("k", b, c))
                    link(dve.tensor_reduce(cols[:, o_ + c:o_ + c + 1], bank(("k", b, c))[:, 0:w], AX_X, ALU.max))
                dve.tensor_reduce(cols[:, o_ + 3:o_ + 4], cols[:, o_:o_ + 3], AX_X, ALU.max,
                                  negate=True).then_inc(k_max, 1)

            k_maxs(0)
            for b in range(FB + 1):
                if b + 1 < FB:
                    k_maxs(b + 1)
                if b < FB:
                    for q in range(3):
                        n = min(4, NT - 4 * q)
                        key = ("kt", b, q)
                        lo(key, ek.lo[:, 4 * q:4 * q + n, :],
                           bank(key)[0:TILE, 0:128 * n].rearrange("p (t d) -> p t d", t=n),
                           ek.hi32[:, 4 * q:4 * q + n, :])
                    o_ = 8 * (b % 2)
                    for c in range(3):
                        carried(dve, ("k", b, c))
                    link(dve.tensor_reduce(cols[:, 24 + b:25 + b], cols[:, o_ + 4:o_ + 7], AX_X, ALU.add))
                    link(dve.reciprocal(cols[:, 28 + b:29 + b], cols[:, 24 + b:25 + b]))
                    lo(("c1t", b), c1[b % 2].lo[:], bank(("c1t", b)).rearrange("p (c d) -> p c d", c=FB),
                       c1[b % 2].hi32[:])
                if b > 0:
                    key = ("cx", b - 1)
                    completed(dve, key)
                    if b > 1:
                        dve.wait_ge(cx_ready, b - 1)
                    drain(dve.tensor_scalar(cxt[:], bank(key), cols[:, 27 + b:28 + b], float(D) ** -0.5,
                                            ALU.mult, ALU.mult), key)
                    dve.wait_ge(cx_hi, b)
                    dve.tensor_tensor(ctxp.lo[:, b - 1, :], cxt[:], ctxp.hi32[:, b - 1, :], ALU.subtract)\
                        .then_inc(cx_ready, 1)

            def q_maxs(i):
                completed(dve, ("q", i))
                c = 16 + 4 * (i % 2)
                dve.tensor_reduce(cols[0:TILE, c:c + 1], bank(("q", i))[0:TILE, :], AX_X, ALU.max,
                                  negate=True).then_inc(q_max, 1)

            def q_norms(i):
                carried(dve, ("q", i))
                c = 16 + 4 * (i % 2)
                link(dve.reciprocal(cols[0:TILE, c + 2:c + 3], cols[0:TILE, c + 1:c + 2]))
                dve.tensor_scalar(qe[i % 2][:], qe[i % 2][:], cols[0:TILE, c + 2:c + 3], None,
                                  ALU.mult).then_inc(q_norm, 1)

            q_maxs(0)
            q_norms(0)
            dve.wait_ge(bl2_in, 16)
            for i in range(NT):
                if i + 1 < NT:
                    q_maxs(i + 1)
                lo(("qt", i), qT[i % 2].lo[:], bank(("qt", i))[:, 0:FB * TILE].rearrange("p (b n) -> p b n", b=FB),
                   qT[i % 2].hi32[:])
                if i + 1 < NT:
                    q_norms(i + 1)
                x_landed(dve, ("xmix", i))
                xr = xt_[i % 2]
                link(dve.tensor_tensor(xr[:], xr[:], bl2B[:], ALU.add))
                completed(dve, ("mo", i))
                drain(dve.tensor_tensor(xr[:], xr[:], bank(("mo", i))[0:TILE, :], ALU.add), ("mo", i))

            dve.wait_ge(idx_in, 48)
            dve.tensor_copy(srcR[:], srcI[:]).then_inc(idx_f, 1)
            dve.tensor_copy(dstR[:], dstI[:]).then_inc(idx_f, 1)
            link(dve.tensor_copy(grpR[:], grpI[:]))
            link(dve.tensor_reduce(gst[:, 0:1], grpR[:], AX_X, ALU.min))
            link(dve.tensor_reduce(gst[:, 1:2], grpR[:], AX_X, ALU.max))
            for a in range(2):
                dve.tensor_scalar(gD[:, a * GROUPS:(a + 1) * GROUPS], ident[0:GROUPS, 0:GROUPS], gst[:, a:a + 1],
                                  None, ALU.mult).then_inc(idx_f, 1)
            completed(dve, ("ix",))
            link(dve.tensor_copy(srcF[:], bank(("ix",))[0:TILE, 0:170]))
            drain(dve.tensor_copy(dstF[:], bank(("ix",))[0:TILE, 170:340]), ("ix",))
            completed(dve, ("wv",))
            drain(dve.tensor_copy(rows[:, 0:2 * GROUPS], bank(("wv",))[0:TILE, 0:2 * GROUPS]), ("wv",))
            carried(dve, ("wv",))
            least, most, r2 = rows[:, 0:GROUPS], rows[:, GROUPS:2 * GROUPS], 2 * GROUPS
            link(dve.tensor_scalar(wB[:, 0:GROUPS], least, float(LASTWIN), None, ALU.min))
            link(dve.tensor_copy(flags[0:1, 0:GROUPS], wB[0:1, 0:GROUPS]))
            link(dve.tensor_tensor(rows[:, r2:r2 + GROUPS], most, wB[:, 0:GROUPS], ALU.subtract))
            link(dve.tensor_scalar(rows[:, r2:r2 + GROUPS], rows[:, r2:r2 + GROUPS], float(WIN - 1), None,
                                   ALU.subtract))
            link(dve.tensor_tensor(rows[:, 3 * GROUPS:4 * GROUPS - 1], most[:, 0:GROUPS - 1], least[:, 1:GROUPS],
                                   ALU.subtract))
            link(dve.tensor_scalar(rows[:, 4 * GROUPS - 1:4 * GROUPS], ones2[0:TILE, 0:1], -1.0, None, ALU.mult))
            link(dve.tensor_reduce(rows[:, 4 * GROUPS:4 * GROUPS + 1], rows[:, r2:4 * GROUPS], AX_X, ALU.max))
            link(dve.tensor_tensor(rows[:, r2:r2 + GROUPS - FEW], most[:, 0:GROUPS - FEW], least[:, FEW:GROUPS],
                                   ALU.subtract))
            link(dve.tensor_scalar(rows[:, r2:r2 + GROUPS - FEW], rows[:, r2:r2 + GROUPS - FEW], 1.0, None, ALU.add))
            link(dve.tensor_reduce(rows[:, 4 * GROUPS + 1:4 * GROUPS + 2], rows[:, r2:r2 + GROUPS - FEW], AX_X,
                                   ALU.max))
            link(dve.tensor_reduce(wB[:, 20:21], rows[:, 4 * GROUPS:4 * GROUPS + 2], AX_X, ALU.max))
            link(dve.tensor_scalar(flags[0:1, 20:21], wB[0:1, 20:21], 0.0, None, ALU.is_le))
            dve.tensor_tensor(rel[:].rearrange("p (g t) -> p g t", g=GROUPS),
                              wB[:, 0:GROUPS].rearrange("p (g a) -> p g a", a=1).broadcast_to((TILE, GROUPS, GT)),
                              dstF[:].rearrange("p (g t) -> p g t", g=GROUPS),
                              ALU.subtract).then_inc(edge_ready, 1)
            dve.wait_ge(edge_ready, 1)
            dve.wait_ge(const_ready, 2)
            dve.memset(cols[:, 39:40], 0.0).then_inc(edge_tiles, PRIME)
            dve.memset(cols[:, 38:39], 0.0).then_inc(window_free, 2)
            dve.memset(cols[:, 37:38], 0.0).then_inc(all_tiles, 1)
            dve.memset(cols[:, 36:37], 0.0).then_inc(all_taken, 1)
            fit = dve.value_load(flags[0:1, 20:21], min_val=0, max_val=1)

            def onehot_src(t, r):
                return dve.tensor_scalar(ohs[r][:], iota[:], srcF[:, bass.ds(t, 1)], None, ALU.is_equal)

            def group_onehots(g, odd):
                for t in range(GT):
                    dve.wait_ge(edge_tiles, g * GT + (t + 1 - NOH + PRIME))
                    onehot_src(g * GT + t, (odd * GT + t) % NOH).then_inc(src_ready, 1)

            def add_group(g, half):
                dve.wait_ge(edge_tiles, g * GT + (GT + PRIME))
                w = dve.value_load(flags[0:1, bass.ds(g, 1)], min_val=0, max_val=LASTWIN)
                a = AT[:, :, bass.ds(w, WIN)]
                a_was = AT[:, :, bass.ds(w, WIN)].bitcast(F32)
                ps = PS[0:TILE, 3 * half:3 * half + 3, :].rearrange("p b (j w) -> p (b j) w", w=WIN)[:, 0:NT, :]
                dve.wait_ge(window_free, g + 2)
                dve.tensor_tensor(a, a_was, ps, ALU.add).then_inc(window_free, 1)

            dve.wait_ge(at_zero, 1)
            with dve.If(fit == 1):
                group_onehots(0, 0)
                with dve.Fori(0, GROUPS // 2) as k:
                    group_onehots(k * 2 + 1, 1)
                    add_group(k * 2, 0)
                    group_onehots(k * 2 + 2, 0)
                    add_group(k * 2 + 1, 1)
                add_group(GROUPS - 1, 0)
                dve.wait_ge(window_free, GROUPS + 2)
                dve.tensor_reduce(colsum[:], AT[:].bitcast(F32).rearrange("p j d -> p d j"), AX_X,
                                  ALU.add).then_inc(sum_ready, 1)
            with dve.Else():
                with dve.Fori(0, NT - 1) as w:
                    with dve.Fori(0, GROUPS) as g:
                        for t in range(GT):
                            dve.wait_ge(all_tiles, w * (GROUPS * GT) + g * GT + (t + 1))
                            onehot_src(g * GT + t, 0).then_inc(all_src, 1)
                    dve.wait_ge(all_tiles, w * (GROUPS * GT) + (GROUPS * GT + 1))
                    dve.tensor_copy(AT32[:, :, bass.ds(w * WIN, WIN)],
                                    PS[0:TILE, 0:3, :].rearrange("p b (j w) -> p (b j) w", w=WIN)[:, 0:NT, :])\
                        .then_inc(all_taken, 1)
                with dve.Fori(0, GROUPS) as g:
                    for t in range(GT):
                        dve.wait_ge(all_tiles, g * GT + (t + 1 + (NT - 1) * GROUPS * GT))
                        onehot_src(g * GT + t, 0).then_inc(all_src, 1)
                dve.wait_ge(all_tiles, NT * GROUPS * GT + 1)
                dve.wait_ge(all_taken, NT)
                dve.tensor_copy(AT32[:, :, LASTWIN:N],
                                PS[0:TILE, 0:3, :].rearrange("p b (j w) -> p (b j) w", w=WIN)[:, 0:NT, :])\
                    .then_inc(all_taken, 1)
                dve.wait_ge(all_taken, NT + 1)
                dve.tensor_reduce(colsum[:], AT32[:].rearrange("p j d -> p d j"), AX_X,
                                  ALU.add).then_inc(sum_ready, 1)
            for c, (o, w) in enumerate(CH):
                completed(dve, ("cb", c))
                drain(dve.tensor_copy(CNTB[:, o:o + w], bank(("cb", c))[:, 0:w]), ("cb", c))
            completed(dve, ("cc",))
            cc = bank(("cc",))[0:TILE, 0:NT]
            link(dve.tensor_scalar(dinc[:], cc, 1.0, None, ALU.add))
            drain(dve.tensor_scalar(invc[:], cc, 1.0, None, ALU.max), ("cc",))
            carried(dve, ("cc",))
            link(dve.reciprocal(invc[:], invc[:]))
            dve.reciprocal(dinc[:], dinc[:]).then_inc(deg_ready, 1)
            link(dve.tensor_scalar(inv0[:], CNTB[:], 1.0, None, ALU.max))
            dve.reciprocal(inv0[:], inv0[:]).then_inc(inv_ready, 1)
            link(dve.tensor_scalar(CNTB[:], CNTB[:], 1.0, None, ALU.add))
            dve.reciprocal(CNTB[:], CNTB[:]).then_inc(deg_ready, 1)
            for i in range(NT):
                lo(("y1", i), y.lo[:, i, :], bank(("y1", i))[0:TILE, :], y.hi32[:, i, :])
            completed(dve, ("r1", FB - 1, 2))
            dve.wait_ge(inv_ready, 1)
            dve.tensor_copy(INVB[:], inv0[:]).then_inc(inv_placed, 1)
            dve.wait_ge(inv_placed, 1)
            n = 0
            for f in range(FB):
                for c, (o, w) in enumerate(CH):
                    key = ("a1", f, c)
                    n += 1
                    t = sc[n % 2][:, 0:w]
                    completed(dve, key)
                    drain(dve.tensor_tensor(t, bank(key)[:, 0:w], INVB[:, o:o + w], ALU.mult), key)
                    carried(dve, key)
                    carried(dve, ("r1", f, c))
                    R = hT.lo32[:, f, o:o + w]
                    dve.tensor_tensor(R, R, t, ALU.add).then_inc(a1_sum, 1)
                    dve.wait_ge(a1_hi, n)
                    dve.scalar_tensor_tensor(out=hT.lo[:, f, o:o + w], in0=R, scalar=0.0,
                                             in1=hT.hi32[:, f, o:o + w], op0=ALU.max, op1=ALU.subtract)\
                        .then_inc(a1_ready, 1)
            for i in range(NT):
                lo(("y2", i), y.lo[:, i, :], bank(("y2", i))[0:TILE, :], y.hi32[:, i, :])
            for i in range(NT):
                x_landed(dve, ("xr2", i))
                completed(dve, ("r2", i))
                drain(dve.tensor_tensor(xw[i % 2][:], xw[i % 2][:], bank(("r2", i))[0:TILE, :], ALU.add), ("r2", i))

            def a2_x(i):
                x_landed(dve, ("xa2", i))
                completed(dve, ("a2", i))
                drain(dve.scalar_tensor_tensor(out=xw[i % 2][:], in0=bank(("a2", i))[0:TILE, :],
                                               scalar=invc[:, i:i + 1], in1=xw[i % 2][:],
                                               op0=ALU.mult, op1=ALU.add), ("a2", i))
                carried(dve, ("a2", i))
                ln_stats(1, i, xw[i % 2][:])

            a2_x(0)
            for i in range(NT):
                if i >= 2:
                    completed(dve, ("xt", 1, i - 2))
                ln_norm(1, i, xw[i % 2][:], xnw[i % 2][:])
                if i + 1 < NT:
                    a2_x(i + 1)
                ln_T_lo(1, i, xnT)
            def over(a):
                return a.rearrange("p (t a) -> p t a", a=1).broadcast_to((TILE, NT, E))

            def logits_less_max(s):
                for c, (o, w) in enumerate(CH):
                    key = ("lt", s, c)
                    completed(dve, key)
                    drain(dve.tensor_copy(gT[s].lo32[:, o:o + w], bank(key)[0:E, 0:w]), key)
                dve.wait_ge(moe_in[s], 48)
                key = ("lg", s)
                completed(dve, key)
                bg_ = bgB[s][:].rearrange("p (a e) -> p a e", a=1).broadcast_to((TILE, NT, E))
                drain(dve.tensor_tensor(lgt[s][:], bank(key)[0:TILE, 0:NT * E].rearrange("p (t e) -> p t e", t=NT),
                                        bg_, ALU.add), key)
                carried(dve, key)
                link(dve.tensor_reduce(gred[s][:, 0, :], lgt[s][:], AX_X, ALU.max))
                dve.tensor_tensor(lgt[s][:], lgt[s][:], over(gred[s][:, 0, :]), ALU.subtract).then_inc(lg_less, 1)

            def softmax_scale(s):
                dve.wait_ge(lg_exp, s + 1)
                link(dve.tensor_reduce(gred[s][:, 1, :], ex[s][:], AX_X, ALU.add))
                link(dve.reciprocal(gred[s][:, 2, :], gred[s][:, 1, :]))

            def gate_transposed(s):
                for c, (o, w) in enumerate(CH):
                    key = ("gt", s, c)
                    lo(key, gT[s].lo[:, o:o + w], bank(key)[0:E, 0:w], gT[s].hi32[:, o:o + w])

            def bias_to_place(s, e, e_):
                c, b_ = COL[f"m{s}b1"], BIAS + 2 * (e % 2)
                dve.tensor_scalar(cols[:, b_:b_ + 2], ccol[:, bass.ds(e_ * 2 + c, 2)], 1.0, None, ALU.mult)\
                    .then_inc(bias_placed, 1)

            def hidden_parts(s, e, e_, later):
                h = hE[e % 2]
                for n, (f, c) in enumerate([(f, c) for f in range(2) for c in range(3)]):
                    o, w = CH[c]
                    carried(dve, ("hd", s, e, f, c), later)
                    dve.tensor_copy(h.hi[:, f, o:o + w], h.lo32[:, f, o:o + w]).then_inc(hid_hi, 1)
                    dve.wait_ge(hid_hi, e_ * 6 + (48 * s + n + 1))
                    dve.tensor_tensor(h.lo[:, f, o:o + w], h.lo32[:, f, o:o + w], h.hi32[:, f, o:o + w],
                                      ALU.subtract).then_inc(hid_ready, 1)

            def expert_added(s, e, e_, later, i):
                key = ("eo", s, e, i)
                completed(dve, key, later)
                drain(dve.scalar_tensor_tensor(out=acc[:, i, :], in0=bank(key)[0:TILE, :],
                                               scalar=gate[:, i, bass.ds(e_, 1)], in1=acc[:, i, :],
                                               op0=ALU.mult, op1=ALU.add), key)

            def experts_added(s):
                bias_to_place(s, 0, 0)
                bias_to_place(s, 1, 1)
                hidden_parts(s, 0, 0, 0)
                with dve.Fori(0, PAIRS) as k:
                    bias_to_place(s, 2, k * 2 + 2)
                    hidden_parts(s, 1, k * 2 + 1, k * 4)
                    for i in range(NT):
                        expert_added(s, 0, k * 2, k * 4, i)
                    bias_to_place(s, 3, k * 2 + 3)
                    hidden_parts(s, 2, k * 2 + 2, k * 4)
                    for i in range(NT):
                        expert_added(s, 1, k * 2 + 1, k * 4, i)
                hidden_parts(s, 7, 7, 0)
                for i in range(NT):
                    expert_added(s, 6, 6, 0, i)

            x_stored(dve, ("xa2", NT - 2))
            x_stored(dve, ("xa2", NT - 1))
            logits_less_max(0)
            softmax_scale(0)
            link(dve.tensor_scalar(cand[:], lgt[0][:], 0.0, None, ALU.is_equal))
            dve.wait_ge(iota_ready, 1)
            io_ = iota8[:].rearrange("p (a e) -> p a e", a=1).broadcast_to((TILE, NT, E))
            link(dve.scalar_tensor_tensor(out=cand[:], in0=cand[:], scalar=-100.0, in1=io_,
                                          op0=ALU.mult, op1=ALU.add))
            link(dve.tensor_reduce(gred[0][:, 3, :], cand[:], AX_X, ALU.min))
            link(dve.tensor_tensor(cand[:], cand[:], over(gred[0][:, 3, :]), ALU.is_equal))
            dve.tensor_tensor(gate[:], cand[:], over(gred[0][:, 2, :]), ALU.mult).then_inc(gate_ready, 1)
            gate_transposed(0)
            experts_added(0)

            def x2_(i):
                expert_added(0, 7, 7, 0, i)
                carried(dve, ("eo", 0, 7, i))
                x_landed(dve, ("xm0", i))
                dve.tensor_tensor(xm[i % 2][:], xm[i % 2][:], acc[:, i, :], ALU.add).then_inc(x2_sum, 1)
                dve.wait_ge(x2_sum, i + 1)
                ln_stats(2, i, xm[i % 2][:])

            x2_(0)
            for i in range(NT + 1):
                if i < NT:
                    if i >= 2:
                        completed(dve, ("xt", 2, i - 2))
                        dve.wait_ge(xn2_lo, i - 1)
                    ln_norm(2, i, xm[i % 2][:], xnm[i % 2][:])
                    if i + 1 < NT:
                        x2_(i + 1)
                    dve.wait_ge(ln_hi, NT + i + 1)
                    dve.tensor_tensor(xn2.lo[:, i, :], xnm[i % 2][:], xn2.hi32[:, i, :], ALU.subtract)\
                        .then_inc(xn2_lo, 1)
                if i >= 1:
                    ln_T_lo(2, i - 1, xnT)
            with dve.If(fit == 1):
                for j in range(NT):
                    sl = slice(j * TILE, (j + 1) * TILE)
                    ins = dve.tensor_tensor(AT[:, j, sl], AT[:, j, sl].bitcast(F32), ident[0:TILE, 0:TILE], ALU.add)
                ins.then_inc(self_loops, 1)
            with dve.Else():
                for j in range(NT):
                    sl = slice(j * TILE, (j + 1) * TILE)
                    ins = dve.tensor_tensor(AT32[:, j, sl], AT32[:, j, sl], ident[0:TILE, 0:TILE], ALU.add)
                ins.then_inc(self_loops, 1)

            x_stored(dve, ("xm0", NT - 2))
            x_stored(dve, ("xm0", NT - 1))
            for i in range(NT):
                key = ("k2", i)
                ps = bank(key)[0:TILE, :]
                completed(dve, key)
                if i >= 3:
                    dve.wait_ge(kacc_done, i - 1)
                    dve.wait_ge(k_ready, i - 2)
                dve.tensor_scalar(kx[i % 3][:], ps, 0.0, None, ALU.min).then_inc(k_min, 1)
                dve.wait_ge(k_exped, i + 1)
                drain(dve.scalar_tensor_tensor(out=kx[i % 3][:], in0=ps, scalar=0.0, in1=kx[i % 3][:],
                                               op0=ALU.max, op1=ALU.add), key)
                dve.wait_ge(k_hi, i + 1)
                dve.tensor_tensor(kp[i % 2].lo[:], kx[i % 3][:], kp[i % 2].hi32[:], ALU.subtract).then_inc(k_ready, 1)
            for b in range(FB):
                lo(("kv", b), kv.lo[:, b, :], bank(("kv", b)), kv.hi32[:, b, :])
            lo(("ks",), ksum.lo[:], bank(("ks",))[:, 0:2 * FB].rearrange("p (b a) -> p b a", b=FB), ksum.hi32[:])

            def q_mins(g, f):
                completed(dve, ("q2", g, f))
                dve.tensor_scalar(q2[g % 2].lo32[:, f, :], bank(("q2", g, f))[:, 0:QC], 0.0, None, ALU.min)\
                    .then_inc(q_min, 1)

            def q_sums(g, f):
                q_ = q2[g % 2].lo32[:, f, :]
                dve.wait_ge(q_exped, g * FB + f + 1)
                drain(dve.scalar_tensor_tensor(out=q_, in0=bank(("q2", g, f))[:, 0:QC], scalar=0.0, in1=q_,
                                               op0=ALU.max, op1=ALU.add), ("q2", g, f))

            def q_los(g, f):
                q_ = q2[g % 2]
                dve.wait_ge(q_hi, g * FB + f + 1)
                dve.tensor_tensor(q_.lo[:, f, :], q_.lo32[:, f, :], q_.hi32[:, f, :], ALU.subtract).then_inc(q_ready, 1)

            def mixed(i):
                c = 24 + 2 * (i % 2)
                completed(dve, ("dn", i))
                drain(dve.tensor_scalar(cols[0:TILE, c:c + 1], bank(("dn", i))[0:TILE, 0:1], 1e-6, None, ALU.add),
                      ("dn", i))
                carried(dve, ("dn", i))
                link(dve.reciprocal(cols[0:TILE, c + 1:c + 2], cols[0:TILE, c:c + 1]))
                x_landed(dve, ("xq", i))
                completed(dve, ("mx", i))
                drain(dve.scalar_tensor_tensor(out=xq[i % 2][:], in0=bank(("mx", i))[0:TILE, :],
                                               scalar=cols[0:TILE, c + 1:c + 2], in1=xq[i % 2][:],
                                               op0=ALU.mult, op1=ALU.add), ("mx", i))

            for g in range(NQ + 1):
                if g < NQ:
                    if g >= 2:
                        completed(dve, ("mx", 2 * g - 3))
                    for f in range(FB + 2):
                        if f < FB:
                            q_mins(g, f)
                        if 0 < f <= FB:
                            q_sums(g, f - 1)
                        if f > 1:
                            q_los(g, f - 2)
                    for i in (2 * g, 2 * g + 1):
                        dve.wait_ge(xs_whole, i + 1)
                        dve.tensor_scalar(xn2.lo32[:, i, :], xn2.lo32[:, i, :], dinc[:, i:i + 1], None, ALU.mult)\
                            .then_inc(xs_scaled, 1)
                        dve.wait_ge(xs_hi, i + 1)
                        dve.tensor_tensor(xn2.lo[:, i, :], xn2.lo32[:, i, :], xn2.hi32[:, i, :], ALU.subtract)\
                            .then_inc(xs_ready, 1)
                if g > 0:
                    mixed(2 * g - 2)
                    mixed(2 * g - 1)

            dve.wait_ge(deg_root, 2)
            for n, (f, c) in enumerate(HX):
                o, w = CH[c]
                key = ("z", f, c)
                z_ = zT.lo32[:, f, o:o + w]
                completed(dve, key)
                drain(dve.tensor_tensor(z_, bank(key)[:, 0:w], CNTB[:, o:o + w], ALU.mult), key)
                dve.wait_ge(z_hi, n + 1)
                dve.tensor_tensor(zT.lo[:, f, o:o + w], z_, zT.hi32[:, f, o:o + w], ALU.subtract).then_inc(z_ready, 1)
            for hf in range(2):
                for n, (f, c) in enumerate(HX):
                    o, w = CH[c]
                    dve.wait_ge(h1_hi, hf * len(HX) + n + 1)
                    dve.tensor_tensor(h1T.lo[:, f, o:o + w], h1T.lo32[:, f, o:o + w], h1T.hi32[:, f, o:o + w],
                                      ALU.subtract).then_inc(h1_ready, 1)
                if hf == 0:
                    continue
                for i in range(NT):
                    key = ("yy", 1, i)
                    carried(dve, ("yy", 0, i))
                    completed(dve, key)
                    y_ = y3.lo32[:, i, :]
                    drain(dve.scalar_tensor_tensor(out=y_, in0=bank(key)[0:TILE, :], scalar=dinc[:, i:i + 1], in1=y_,
                                                   op0=ALU.mult, op1=ALU.add), key)
                    dve.wait_ge(y3_hi, i + 1)
                    dve.tensor_tensor(y3.lo[:, i, :], y_, y3.hi32[:, i, :], ALU.subtract).then_inc(y3_ready, 1)
            dve.wait_ge(b2_in, 16)
            for i in range(NT + 1):
                if i < NT:
                    x_landed(dve, ("xa3", i))
                    completed(dve, ("a3", i))
                    drain(dve.scalar_tensor_tensor(out=gt_[:], in0=bank(("a3", i))[0:TILE, :], scalar=dinc[:, i:i + 1],
                                                   in1=b2B[:], op0=ALU.mult, op1=ALU.add), ("a3", i))
                    carried(dve, ("a3", i))
                    dve.scalar_tensor_tensor(out=xg[i % 2][:], in0=gt_[:], scalar=0.0, in1=xg[i % 2][:],
                                             op0=ALU.max, op1=ALU.add).then_inc(x3_sum, 1)
                    dve.wait_ge(x3_sum, i + 1)
                    ln_stats(3, i, xg[i % 2][:])
                    ln_norm(3, i, xg[i % 2][:], xnA[i % 2][:])
                    dve.wait_ge(ln_xnf, lnno[(3, i)] + 1)
                    ln_stats(4, i, xnA[i % 2][:])
                    if i >= 2:
                        completed(dve, ("xt", 4, i - 2))
                    ln_norm(4, i, xnA[i % 2][:], xnB[i % 2][:])
                if i >= 1:
                    sl = slice((i - 1) * TILE, i * TILE)
                    dve.wait_ge(hx_hi, i)
                    dve.tensor_tensor(hxT.lo[:, :, sl], hxT.lo32[:, :, sl], hxT.hi32[:, :, sl], ALU.subtract)\
                        .then_inc(hx_ready, 1)
            def tt(a, b, out_, op):
                return dve.tensor_tensor(out_, a, b, op)

            def unit_sums(s, i):
                c = 8 * (i % 2)
                dve.wait_ge(squared, NT * s + i + 1)
                if i >= 2 or s:
                    dve.wait_ge(unit_root, NT * s + i - 1)
                link(dve.tensor_reduce(cols[0:TILE, c:c + 8], sqr[i % 2][:].rearrange("p (h d) -> p h d", h=HEADS),
                                       AX_X, ALU.add))
                dve.tensor_scalar(cols[0:TILE, c:c + 8], cols[0:TILE, c:c + 8], 1e-12, (1.0, 1.0 / DH)[s], ALU.add,
                                  ALU.mult).then_inc(unit_sum, 1)

            def unit_norm(s, w, i):
                c = 16 + 8 * (i % 2)
                r = cols[0:TILE, c:c + 8]
                dve.wait_ge(unit_root, NT * s + i + 1)
                link(dve.reciprocal(r, r))
                if i >= 2:
                    completed(dve, ("t" + w, i - 2))
                elif s:
                    completed(dve, ("tq", NT - 2 + i))
                drain(dve.tensor_tensor(unit[i % 2][:].rearrange("p (h d) -> p h d", h=HEADS),
                                        bank(("p" + w, i))[0:TILE, :].rearrange("p (h d) -> p h d", h=HEADS),
                                        r.rearrange("p (h a) -> p h a", a=1).broadcast_to((TILE, HEADS, DH)),
                                        ALU.mult), ("p" + w, i))

            even, odd = slice(0, HEADS, 2), slice(1, HEADS, 2)
            up, down = slice(0, DH), slice(DH, 2 * DH)
            for s, (w, gain) in enumerate((("q", "qn_g"), ("k", "kn_g"))):
                g_ = ccol[:, COL[gain]:COL[gain] + 1]
                unit_sums(s, 0)
                unit_norm(s, w, 0)
                for i in range(NT):
                    if i + 1 < NT:
                        unit_sums(s, i + 1)
                        unit_norm(s, w, i + 1)
                    key = ("t" + w, i)
                    sl = slice(i * TILE, (i + 1) * TILE)
                    t_ = bank(key)[:, 0:FB * TILE].rearrange("p (b n) -> p b n", b=FB)
                    dve_los.append(key)
                    dve.wait_ge(hi_done, len(dve_los))
                    if w == "q":
                        outs = (QA[down, even, sl], QA[up, odd, sl])
                        ins = (QA32[up, even, sl], QA32[down, odd, sl])
                    else:
                        outs = (KLO[up, :, sl], KLO[down, :, sl])
                        ins = (KA32[up, even, sl], KA32[down, odd, sl])
                    for a in range(2):
                        half = (up, down)[a]
                        last = dve.scalar_tensor_tensor(out=outs[a], in0=t_[half], scalar=g_[half], in1=ins[a],
                                                        op0=ALU.mult, op1=ALU.subtract)
                    drain(last, key)

            def max_part(key):
                b = key[1]
                if key[0] == "mx":
                    _, b, a, i, q = key
                    completed(dve, key)
                    ins = dve.tensor_reduce(chmax[:, a, i, q:q + 1], bank(key)[0:TILE, 0:piece_width(i, q)], AX_X,
                                            ALU.max)
                    drain(ins, key)
                    if key == ("mx", b, *PIECES[-1]):
                        carried(dve, key)
                        if b > 0:
                            completed(dve, ("mt", b - 1, 2))
                        dve.tensor_reduce(negm[:].rearrange("p t a -> p a t"), chmax[:], AX_X, ALU.max,
                                          negate=True).then_inc(max_found, 1)
                else:
                    _, b, c = key
                    o, w = CH[c]
                    completed(dve, key)
                    rows_ = slice(32 * b, 32 * b + 2)
                    dve.wait_ge(max_found, b + 1)
                    drain(dve.tensor_copy(rowmax[rows_, o:o + w], bank(key)[0:2, 0:w]), key)

            def pair_out_lo(b):
                dve.wait_ge(ot_hi, b + 1)
                dve.tensor_tensor(OT[:, b, 1, :], OT32[:, b, :], OT[:, b, 0, :].bitcast(F32), ALU.subtract)\
                    .then_inc(ot_ready, 1)

            def chunk_out(b, c):
                o, w = CH[c]
                completed(dve, ("ss", b, c))
                if (b, c) == (0, 0):
                    dve.wait_ge(v_ready, NT)
                drain(dve.reciprocal(OT32[:, b, o:o + w], bank(("ss", b, c))[:, 0:w]), ("ss", b, c))
                carried(dve, ("ss", b, c))
                for a, half in enumerate((up, down)):
                    key = ("ov", b, c, a)
                    completed(dve, key)
                    drain(dve.tensor_tensor(OT32[half, b, o:o + w], OT32[half, b, o:o + w], bank(key)[half, 0:w],
                                            ALU.mult), key)
                carried(dve, ("ov", b, c, 0))
                carried(dve, ("ov", b, c, 1))
                dve.memset(cols[:, 36:37], 0.0).then_inc(ot_whole, 1)

            completed(dve, ("tk", NT - 1))
            dve.memset(chmax[:], -3e38)
            dve.memset(ones64[:], 1.0)
            dve.memset(maskall[:], -1e30)
            for b in range(FB):
                rows_ = slice(32 * b, 32 * b + 2)
                ins = dve.tensor_copy(sel[rows_, :, :],
                                      ident[rows_, 32 * b:32 * b + 2].rearrange("p (a n) -> p a n", n=1)
                                      .broadcast_to((2, 2, 128)))
            ins.then_inc(att_ready, 1)
            dve.wait_ge(att_ready, 1)
            for key in max_work(0):
                max_part(key)
            between = []
            for g, (b, c, a, j) in enumerate(STEPS):
                off, w = valid(c, j)
                if g % PER_PAIR == 0 and b + 1 < FB:
                    between = max_work(b + 1)
                dve.wait_ge(p_hi, g + 1)
                dve.tensor_tensor(PT[g % NPT].lo[:, off:w], P[g % NP][:, off:w], PT[g % NPT].hi32[:, off:w],
                                  ALU.subtract).then_inc(p_ready, 1)
                if between:
                    max_part(between.pop(0))
                if b > 0 and (c, a, j) == (0, 1, 0):
                    pair_out_lo(b - 1)
                ended = done_by(g)
                if ended and ended[2] == 1 and ended[3] == last_key(ended[1]):
                    chunk_out(ended[0], ended[1])
            chunk_out(FB - 1, 2)
            pair_out_lo(FB - 1)
            for f, c in HX:
                o, w = CH[c]
                lo(("wo", f, c), yT.lo[:, f, o:o + w], bank(("wo", f, c))[:, 0:w], yT.hi32[:, f, o:o + w])

            logits_less_max(1)
            softmax_scale(1)
            dve.tensor_tensor(gate[:], ex[1][:], over(gred[1][:, 2, :]), ALU.mult).then_inc(gate_ready, 1)
            gate_transposed(1)
            experts_added(1)
            for i in range(NT):
                expert_added(1, 7, 7, 0, i)
                carried(dve, ("eo", 1, 7, i))
                x_landed(dve, ("xm1", i))
                dve.tensor_tensor(xm[i % 2][:], xm[i % 2][:], acc[:, i, :], ALU.add).then_inc(x2_sum, 1)

        @block.tensor
        def _(pe):
            def mm3(out_, l, r, start, stop):
                pe.matmul(out_, l[0], r[0], start=start, stop=False)
                pe.matmul(out_, l[0], r[1], start=False, stop=False)
                return pe.matmul(out_, l[1], r[0], start=False, stop=stop)

            def opened(key, later=0):
                b, n = place[key]
                if n > 1:
                    pe.wait_ge(drained[b], later + (n - 1))
                return PS[:, b, :]

            def done(ins, key):
                ins.then_inc(filled[place[key][0]], 1)

            def of(p, *idx):
                return (p.hi[idx], p.lo[idx])

            al = slice(None)

            def blk(b, w=128):
                return slice(b * w, (b + 1) * w)

            def product(key, out_, pairs):
                for n, (l, r) in enumerate(pairs):
                    ins = mm3(out_, l, r, n == 0, n == len(pairs) - 1)
                done(ins, key)

            def ln_T(s, i, xnf_):
                pe.wait_ge(ln_xnf, lnno[(s, i)] + 1)
                o = opened(("xt", s, i))
                for b in range(FB):
                    ins = pe.transpose(o[:, blk(b, TILE)], xnf_[:, blk(b)], ident[0:TILE, 0:TILE])
                done(ins, ("xt", s, i))

            def w_T(w, raw_):
                for ib in range(FB):
                    o = opened(("wt", w, ib))
                    for ob in range(FB):
                        ins = pe.transpose(o[:, blk(ob)], raw_[:, ob, blk(ib)], ident[:])
                    done(ins, ("wt", w, ib))

            pe.wait_ge(const_ready, 1)
            for i in range(NT):
                ln_T(0, i, xnf[i % 2])
            pe.wait_ge(rawk_in, 16)
            w_T("k", rawk)
            pe.wait_ge(raw2_in, 16)
            w_T("2", raw2)
            pe.wait_ge(vecs_in, 16 * 10)
            done(pe.transpose(opened(("vec",))[:, 0:54], vecs[:], ident[0:54, 0:54]), ("vec",))
            pe.wait_ge(unit_ready, 1)
            for ib in range(FB):
                carried(pe, ("wt", "2", ib))
            for ib in range(FB):
                product(("mi", ib), opened(("mi", ib)),
                        [(of(W1p, al, jb, blk(ib)), of(W2T, al, jb, al)) for jb in range(FB)])
            pe.wait_ge(unit_ready, 2)
            pe.wait_ge(mi_ready, FB)
            for cb in range(FB):
                product(("g", cb), opened(("g", cb)),
                        [(of(Wvp, al, eb, blk(cb)), of(MI, al, eb, al)) for eb in range(FB)])
            pe.wait_ge(rawq_in, 16)
            w_T("q", rawq)

            for i in range(NT):
                carried(pe, ("xt", 0, i))
            for ib in range(FB):
                carried(pe, ("wt", "k", ib))
                carried(pe, ("wt", "q", ib))
                carried(pe, ("g", ib))

            def k_block(b):
                for c, (o, w) in enumerate(CH):
                    product(("k", b, c), opened(("k", b, c))[:, 0:w],
                            [(of(WA, al, kb, blk(b)), of(xnT, al, kb, slice(o, o + w))) for kb in range(FB)])

            k_block(0)
            for b in range(FB + 1):
                if b + 1 < FB:
                    k_block(b + 1)
                if b < FB:
                    for c in range(3):
                        carried(pe, ("k", b, c))
                    for q in range(3):
                        o = opened(("kt", b, q))
                        for t in range(min(4, NT - 4 * q)):
                            ins = pe.transpose(o[0:TILE, blk(t)], kT[b % 2][:, blk(4 * q + t, TILE)], ident[:])
                        done(ins, ("kt", b, q))
                    for q in range(3):
                        carried(pe, ("kt", b, q))
                    pe.wait_ge(ln_lo, NT)
                    product(("c1", b), opened(("c1", b)),
                            [(of(ek, al, i, al), of(xn, al, i, al)) for i in range(NT)])
                    carried(pe, ("c1", b))
                    o = opened(("c1t", b))
                    for cb in range(FB):
                        ins = pe.transpose(o[:, blk(cb)], c1f[:, blk(cb)], ident[:])
                    done(ins, ("c1t", b))
                if b > 0:
                    carried(pe, ("c1t", b - 1))
                    product(("cx", b - 1), opened(("cx", b - 1)),
                            [(of(c1[(b - 1) % 2], al, cb, al), of(G, al, cb, al)) for cb in range(FB)])

            def q_tile(i):
                product(("q", i), opened(("q", i))[0:TILE, :],
                        [(of(xnT, al, kb, blk(i, TILE)), of(WB, al, kb, al)) for kb in range(FB)])

            q_tile(0)
            pe.wait_ge(cx_ready, FB)
            for i in range(NT):
                if i + 1 < NT:
                    q_tile(i + 1)
                pe.wait_ge(q_norm, i + 1)
                o = opened(("qt", i))
                for b in range(FB):
                    ins = pe.transpose(o[:, blk(b, TILE)], qe[i % 2][:, blk(b)], ident[0:TILE, 0:TILE])
                done(ins, ("qt", i))
                o = opened(("mo", i))[0:TILE, :]
                for kb in range(FB):
                    mm3(o, of(xnT, al, kb, blk(i, TILE)), of(MI, al, kb, al), kb == 0, False)
                carried(pe, ("qt", i))
                for b in range(FB):
                    ins = mm3(o, of(qT[i % 2], al, b, al), of(ctxp, al, b, al), False, b == FB - 1)
                done(ins, ("mo", i))
            for n, name in enumerate(torch_w):
                pe.wait_ge(wraw_in[n % 2], 16 * (n // 2 + 1))
                w_T(name, wraw[n % 2])

            pe.wait_ge(idx_f, 4)
            pe.wait_ge(const_ready, 2)
            o = opened(("ix",))
            for a, rows in enumerate((srcR, dstR)):
                for h in range(2):
                    ins = pe.transpose(o[0:TILE, 170 * a + 85 * h:170 * a + 85 * h + 85], rows[:, h, :], ident[0:85, 0:85])
            done(ins, ("ix",))
            o = opened(("wv",))
            done(pe.matmul(o[0:TILE, 0:2 * GROUPS], onesA[0:GROUPS, 0:TILE], gD[:], start=True, stop=True), ("wv",))
            for b in range(BANKS):
                pe.wait_ge(drained[b], before_edges[b])
            pe.wait_ge(edge_ready, 1)
            fit = pe.value_load(flags[0:1, 20:21], min_val=0, max_val=1)

            def tile_counts(half, os, od, first, last):
                for j in range(NT):
                    o_ = PS[0:TILE, 3 * half + j // 4, blk(j % 4)]
                    ins = pe.matmul(o_, os[:, blk(j, TILE)], od, start=(first and j % 4 == 0), stop=last,
                                    skip_group_check=True)
                return ins

            def group_counts(g, half):
                pe.wait_ge(window_free, g + 1)
                pe.wait_ge(dst_ready, g + 1)
                for t in range(GT):
                    pe.wait_ge(src_ready, g * GT + (t + 1))
                    tile_counts(half, ohs[(half * GT + t) % NOH], ohd[half][:, t, :], t == 0, t == GT - 1)\
                        .then_inc(edge_tiles, 1)

            with pe.If(fit == 1):
                with pe.Fori(0, GROUPS // 2) as k:
                    group_counts(k * 2, 0)
                    group_counts(k * 2 + 1, 1)
                group_counts(GROUPS - 1, 0)
            with pe.Else():
                with pe.Fori(0, NT) as w:
                    def all_group(g, first):
                        pe.wait_ge(all_dst, w * GROUPS + g + 1)
                        for t in range(GT):
                            pe.wait_ge(all_src, w * (GROUPS * GT) + g * GT + (t + 1))
                            tile_counts(0, ohs[0], ohd[0][:, t, :], first and t == 0, False)\
                                .then_inc(all_tiles, 1)

                    pe.wait_ge(all_taken, w + 1)
                    all_group(0, True)
                    with pe.Fori(1, GROUPS) as g:
                        all_group(g, False)

            pe.wait_ge(sum_ready, 1)
            for c, (o_, w_) in enumerate(CH):
                o = opened(("cb", c))
                done(pe.matmul(o[:, 0:w_], onesA[:], colsum[:, o_:o_ + w_], start=True, stop=True), ("cb", c))
            o = opened(("cc",))
            for i in range(NT):
                ins = pe.matmul(o[0:TILE, i:i + 1], colsum[:, blk(i, TILE)], onesA[:, 0:1], start=True, stop=True)
            done(ins, ("cc",))
            unit_split(pe, "Wl1")
            for i in range(NT):
                product(("y1", i), opened(("y1", i))[0:TILE, :],
                        [(of(xnT, al, kb, blk(i, TILE)), of(WA, al, kb, al)) for kb in range(FB)])
            unit_split(pe, "Wr1")
            for f in range(FB):
                for c, (o, w) in enumerate(CH):
                    product(("r1", f, c), opened(("r1", f, c))[:, 0:w],
                            [(of(WB, al, kb, blk(f)), of(xnT, al, kb, slice(o, o + w))) for kb in range(FB)])

            def counts_moving(key, p, f, c, fast_):
                o, w = CH[c]
                out_ = opened(key)[:, 0:w]
                for j in range(NT):
                    if fast_:
                        a = AT[:, j, o:o + w]
                        pe.matmul(out_, p.hi[:, j, blk(f)], a, start=(j == 0), stop=False)
                        ins = pe.matmul(out_, p.lo[:, j, blk(f)], a, start=False, stop=(j == NT - 1))
                    else:
                        a = AT32[:, j, o:o + w]
                        pe.matmul(out_, p.hi32[:, j, blk(f)], a, start=(j == 0), stop=False)
                        ins = pe.matmul(out_, p.lo[:, j, blk(f)].bitcast(F32), a, start=False, stop=(j == NT - 1))
                done(ins, key)

            def counts_still(key, p, i, fast_):
                out_ = opened(key)[0:TILE, :]
                for j in range(NT):
                    if fast_:
                        a = AT[:, j, blk(i, TILE)]
                        pe.matmul(out_, a, p.hi[:, j, :], start=(j == 0), stop=False)
                        ins = pe.matmul(out_, a, p.lo[:, j, :], start=False, stop=(j == NT - 1))
                    else:
                        a = AT32[:, j, blk(i, TILE)]
                        pe.matmul(out_, a, p.hi32[:, j, :], start=(j == 0), stop=False)
                        ins = pe.matmul(out_, a, p.lo[:, j, :].bitcast(F32), start=False, stop=(j == NT - 1))
                done(ins, key)

            def on_both_paths(stage):
                with pe.If(fit == 1):
                    stage(True)
                with pe.Else():
                    stage(False)

            for i in range(NT):
                carried(pe, ("y1", i))

            @on_both_paths
            def _(fast_):
                for f in range(FB):
                    for c in range(3):
                        counts_moving(("a1", f, c), y, f, c, fast_)

            pe.wait_ge(a1_ready, 3 * FB)
            unit_split(pe, "Wl2")
            for i in range(NT):
                product(("y2", i), opened(("y2", i))[0:TILE, :],
                        [(of(hT, al, kb, blk(i, TILE)), of(WA, al, kb, al)) for kb in range(FB)])
            unit_split(pe, "Wr2")
            for i in range(NT):
                product(("r2", i), opened(("r2", i))[0:TILE, :],
                        [(of(hT, al, kb, blk(i, TILE)), of(WB, al, kb, al)) for kb in range(FB)])
            for i in range(NT):
                carried(pe, ("y2", i))

            @on_both_paths
            def _(fast_):
                for i in range(NT + 1):
                    if i < NT:
                        counts_still(("a2", i), y, i, fast_)
                    if i >= 1:
                        ln_T(1, i - 1, xnw[(i - 1) % 2])
            def gate_logits(s, T):
                pe.wait_ge(wg_ready, 2 * s + 1)
                for c, (o, w) in enumerate(CH):
                    key = ("lt", s, c)
                    product(key, opened(key)[0:E, 0:w],
                            [(of(WgP[s], al, kb, al), of(T, al, kb, slice(o, o + w))) for kb in range(FB)])
                for c in range(3):
                    carried(pe, ("lt", s, c))
                o = opened(("lg", s))
                for i in range(NT):
                    ins = pe.transpose(o[0:TILE, E * i:E * i + E], gT[s].lo32[:, blk(i, TILE)], ident[0:E, 0:E])
                done(ins, ("lg", s))

            def gates_and_biases(s):
                pe.wait_ge(gate_ready, s + 1)
                for q, (o_, w_) in enumerate(CH):
                    o = opened(("gt", s, q))
                    for t in range(w_ // TILE):
                        ins = pe.transpose(o[0:E, blk(t, TILE)], gate[:, o_ // TILE + t, :], ident[0:TILE, 0:TILE])
                    done(ins, ("gt", s, q))
                for q in range(3):
                    carried(pe, ("gt", s, q))
                pe.wait_ge(wg_ready, 2 * s + 2)
                for i in range(NT):
                    product(("ac", s, i), opened(("ac", s, i))[0:TILE, :],
                            [(of(gT[s], al, blk(i, TILE)), of(b2P[s], al, 0, al))])

            def hidden_products(s, e, e_, later, T):
                pe.wait_ge(w_ready[0], e_ + (E * s + 1))
                w1 = W1P[1 - e % 2]
                for f in range(2):
                    for c, (o, w) in enumerate(CH):
                        key = ("hd", s, e, f, c)
                        product(key, opened(key, later)[:, 0:w],
                                [(of(w1, al, kb, blk(f)), of(T, al, kb, slice(o, o + w))) for kb in range(FB)])

            def output_product(s, e, e_, later, i):
                if i == 0:
                    pe.wait_ge(w_ready[1], e_ + (E * s + 1))
                    pe.wait_ge(hid_ready, e_ * 6 + (48 * s + 6))
                w2 = W2P[1 - e % 2]
                key = ("eo", s, e, i)
                product(key, opened(key, later)[0:TILE, :],
                        [(of(hE[e % 2], al, f, blk(i, TILE)), of(w2, al, f, al)) for f in range(2)])

            def experts(s, T):
                hidden_products(s, 0, 0, 0, T)
                with pe.Fori(0, PAIRS) as k:
                    hidden_products(s, 1, k * 2 + 1, k * 4, T)
                    for i in range(NT):
                        output_product(s, 0, k * 2, k * 4, i)
                    hidden_products(s, 2, k * 2 + 2, k * 4, T)
                    for i in range(NT):
                        output_product(s, 1, k * 2 + 1, k * 4, i)
                hidden_products(s, 7, 7, 0, T)
                for i in range(NT):
                    output_product(s, 6, 6, 0, i)

            for i in range(NT):
                carried(pe, ("xt", 1, i))
            gate_logits(0, xnT)
            gates_and_biases(0)
            experts(0, xnT)
            for i in range(NT + 1):
                if i < NT:
                    output_product(0, 7, 7, 0, i)
                if i >= 1:
                    ln_T(2, i - 1, xnm[(i - 1) % 2])
            def k2_tile(i):
                product(("k2", i), opened(("k2", i))[0:TILE, :],
                        [(of(xnT, al, kb, blk(i, TILE)), of(WB, al, kb, al)) for kb in range(FB)])

            for i in range(NT):
                carried(pe, ("xt", 2, i))
            unit_split(pe, "Wqk1")
            k2_tile(0)
            pe.wait_ge(xn2_lo, NT)
            for i in range(NT):
                if i + 1 < NT:
                    k2_tile(i + 1)
                pe.wait_ge(k_ready, i + 1)
                for b in range(FB):
                    o = opened(("kv", b)) if i == 0 else bank(("kv", b))
                    ins = mm3(o, of(kp[i % 2], al, blk(b)), of(xn2, al, i, al), i == 0, i == NT - 1)
                    if i == NT - 1:
                        done(ins, ("kv", b))
                if i < NT - 1:
                    ins.then_inc(k_used, 1)
            pe.wait_ge(kacc_done, NT + 1)
            o = opened(("ks",))
            for b in range(FB):
                ins = pe.matmul(o[:, 2 * b:2 * b + 2], kacc[:, blk(b)], ones2[0:TILE, 0:2], start=True, stop=True)
            done(ins, ("ks",))
            unit_split(pe, "Wqk0")
            for g in range(NQ + 1):
                if g < NQ:
                    for f in range(FB):
                        product(("q2", g, f), opened(("q2", g, f))[:, 0:QC],
                                [(of(WA, al, kb, blk(f)), of(xnT, al, kb, blk(g, QC))) for kb in range(FB)])
                if g > 0:
                    if g == 1:
                        carried(pe, ("kv", FB - 1))
                        carried(pe, ("ks",))
                    pe.wait_ge(q_ready, g * FB)
                    q_ = q2[(g - 1) % 2]
                    for t in range(2):
                        i = 2 * g - 2 + t
                        product(("dn", i), opened(("dn", i))[0:TILE, 0:2],
                                [(of(q_, al, b, blk(t, TILE)), of(ksum, al, b, al)) for b in range(FB)])
                        product(("mx", i), opened(("mx", i))[0:TILE, :],
                                [(of(q_, al, b, blk(t, TILE)), of(kv, al, b, al)) for b in range(FB)])

            pe.wait_ge(self_loops, 1)
            pe.wait_ge(xs_ready, NT)

            @on_both_paths
            def _(fast_):
                for f, c in HX:
                    counts_moving(("z", f, c), xn2, f, c, fast_)

            pe.wait_ge(z_ready, len(HX))
            for hf in range(2):
                unit_split(pe, "gW1" + "ab"[hf])
                for f, c in HX:
                    o, w = CH[c]
                    product(("h1", hf, f, c), opened(("h1", hf, f, c))[:, 0:w],
                            [(of(WB, al, kb, blk(f)), of(zT, al, kb, slice(o, o + w))) for kb in range(FB)])
                unit_split(pe, "gW2" + "ab"[hf])
                pe.wait_ge(h1_ready, (hf + 1) * len(HX))
                for i in range(NT):
                    product(("yy", hf, i), opened(("yy", hf, i))[0:TILE, :],
                            [(of(h1T, al, kb, blk(i, TILE)), of(WA, al, kb, al)) for kb in range(FB)])
            pe.wait_ge(y3_ready, NT)

            @on_both_paths
            def _(fast_):
                for i in range(NT + 1):
                    if i < NT:
                        counts_still(("a3", i), y3, i, fast_)
                    if i >= 1:
                        ln_T(4, i - 1, xnB[(i - 1) % 2])
            pe.wait_ge(hx_ready, NT)
            unit_split(pe, "aWv")
            for i in range(NT):
                product(("pv", i), opened(("pv", i))[0:TILE, :],
                        [(of(hxT, al, kb, blk(i, TILE)), of(WB, al, kb, al)) for kb in range(FB)])
            for w, unit_, W in (("q", "aWq", WA), ("k", "aWk", WB)):
                unit_split(pe, unit_)
                for i in range(NT + 1):
                    if i < NT:
                        product(("p" + w, i), opened(("p" + w, i))[0:TILE, :],
                                [(of(hxT, al, kb, blk(i, TILE)), of(W, al, kb, al)) for kb in range(FB)])
                    if i >= 1:
                        key = ("t" + w, i - 1)
                        carried(pe, ("p" + w, i - 1))
                        o = opened(key)
                        for b in range(FB):
                            ins = pe.transpose(o[:, blk(b, TILE)], unit[(i - 1) % 2][:, blk(b)], ident[0:TILE, 0:TILE])
                        done(ins, key)

            def scores_for_max(key):
                if key[0] == "mx":
                    _, b, a, i, q = key
                    h = 2 * b + a
                    o = opened(key)[0:TILE]
                    w_ = piece_width(i, q)
                    even_w = w_ + w_ % 2
                    diagonal = q == i // 4
                    ins = pe.matmul(o[:, 0:even_w], QA[:, h, blk(i, TILE)], KA[:, h, 500 * q:500 * q + even_w],
                                    start=True, stop=not diagonal)
                    if diagonal:
                        ins = pe.matmul(o[:, w_ - TILE:w_], identb[0:TILE, 0:TILE], causal[:], start=False, stop=True)
                    done(ins, key)
                else:
                    _, b, c = key
                    o_, w_ = CH[c]
                    pe.wait_ge(max_found, b + 1)
                    o = opened(key)
                    for t in range(w_ // TILE):
                        ins = pe.transpose(o[0:2, blk(t, TILE)], negm[:, o_ // TILE + t, :], ident[0:TILE, 0:TILE])
                    done(ins, key)

            def scores(g):
                b, c, a, j = STEPS[g]
                h, hi_rows = 2 * b + a, slice(DH * a, DH * a + DH)
                q0 = CH[c][0]
                off, w = valid(c, j)
                key = ("sT", g)
                o = opened(key)[0:TILE]
                qs = slice(q0 + off, q0 + w)
                pe.matmul(o[:, off:w], KA[:, h, blk(j, TILE)], QA[:, h, qs], start=True, stop=False)
                pe.matmul(o[:, off:w], KLO[hi_rows, b, blk(j, TILE)], QA[hi_rows, h, qs], start=False, stop=False)
                d = TILE * j - q0
                rows_ = slice(32 * b, 32 * b + 2)
                ins = pe.matmul(o[:, off:w], sel[rows_, a, 0:TILE], rowmax[rows_, qs], start=False, stop=d < 0)
                if d >= 0:
                    if d > off:
                        pe.matmul(o[:, off:d], maskall[:], identb[0:TILE, 0:TILE], start=False, stop=False)
                    ins = pe.matmul(o[:, d:d + TILE], causal[:], identb[0:TILE, 0:TILE], start=False, stop=True)
                done(ins, key)

            def product_with_v(g):
                b, c, a, j = STEPS[g]
                off, w = valid(c, j)
                key = ("ov", b, c, a)
                pe.wait_ge(p_ready, g + 1)
                pe.wait_ge(v_ready, j + 1)
                o = opened(key) if j == 0 else bank(key)
                ins = mm3(o[:, off:w], of(V, al, j, blk(b)), of(PT[g % NPT], al, slice(off, w)), j == 0,
                          j == last_key(c))
                if j < last_key(c):
                    ins.then_inc(pt_used, 1)
                    return
                done(ins, key)
                pe.wait_ge(p_added, g + 1)
                o = opened(("ss", b, c)) if a == 0 else bank(("ss", b, c))
                ins = pe.matmul(o[DH * a:DH * a + DH, 0:w], ones64[:], sacc[a][:, 0:w], start=True, stop=True)
                if a == 0:
                    ins.then_inc(sums_begun, 1)
                else:
                    done(ins, ("ss", b, c))

            pe.wait_ge(k_twice, NT)
            carried(pe, ("tk", NT - 1))
            pe.wait_ge(att_ready, 1)
            for key in max_work(0):
                scores_for_max(key)
            between = []
            for g, (b, c, a, j) in enumerate(STEPS):
                if g % PER_PAIR == 0:
                    for c_ in range(3):
                        carried(pe, ("mt", b, c_))
                    if b + 1 < FB:
                        between = max_work(b + 1)
                scores(g)
                if g >= LAG:
                    product_with_v(g - LAG)
                if between:
                    scores_for_max(between.pop(0))
            for g in range(len(STEPS) - LAG, len(STEPS)):
                product_with_v(g)

            pe.wait_ge(ot_ready, FB)
            unit_split(pe, "aWo")
            for f, c in HX:
                o, w = CH[c]
                product(("wo", f, c), opened(("wo", f, c))[:, 0:w],
                        [(of(WA, al, kb, blk(f)), (OT[:, kb, 0, o:o + w], OT[:, kb, 1, o:o + w])) for kb in range(FB)])
            for f, c in HX:
                carried(pe, ("wo", f, c))
            gate_logits(1, yT)
            gates_and_biases(1)
            experts(1, yT)
            for i in range(NT):
                output_product(1, 7, 7, 0, i)

        assert act_his == dve_los


_INS = ['x', 'src', 'dst', 'L0_gnn_Wl1', 'L0_gnn_bl1', 'L0_gnn_Wr1', 'L0_gnn_Wl2', 'L0_gnn_bl2', 'L0_gnn_Wr2',
        'L0_mix_Wq', 'L0_mix_Wk', 'L0_mix_Wv', 'L0_mix_W1', 'L0_mix_W2', 'L0_ffn_Wg', 'L0_ffn_bg', 'L0_ffn_W1',
        'L0_ffn_b1', 'L0_ffn_W2', 'L0_ffn_b2', 'L1_gnn_W1', 'L1_gnn_b1', 'L1_gnn_W2', 'L1_gnn_b2', 'L1_mix_W_qk',
        'L1_ffn_ln_g', 'L1_ffn_ln_b', 'L1_ffn_Wq', 'L1_ffn_Wk', 'L1_ffn_Wv', 'L1_ffn_Wo', 'L1_ffn_qn_g',
        'L1_ffn_kn_g', 'L1_ffn_gate_W', 'L1_ffn_gate_b', 'L1_ffn_W1', 'L1_ffn_b1', 'L1_ffn_W2', 'L1_ffn_b2']


def kernel(**inputs):
    import numpy as _np
    import concourse.bacc as _bacc
    from concourse import mybir as _mybir
    from concourse.bass_utils import run_bass_kernel_spmd as _run

    nc = _bacc.Bacc("TRN2", target_bir_lowering=False, num_devices=1)
    arrays, args = {}, []
    for name in _INS:
        a = _np.ascontiguousarray(inputs[name])
        arrays[f"in_{name}_dram"] = a
        args.append(nc.dram_tensor(f"in_{name}_dram", a.shape, _mybir.dt.from_np(a.dtype), kind="ExternalInput").ap())
    args.append(nc.dram_tensor("out_0_dram", (N, D), _mybir.dt.float32, kind="ExternalOutput").ap())
    build(nc, *args)
    r = _run(nc, [arrays], core_ids=[0])
    return r.results[0]["out_0_dram"]
```

```python
from contextlib import ExitStack

import concourse.bass as bass
from concourse import mybir

F32 = mybir.dt.float32
F32R = mybir.dt.float32r
BF16 = mybir.dt.bfloat16
F16 = mybir.dt.float16
I32 = mybir.dt.int32
ALU = mybir.AluOpType
ACT = mybir.ActivationFunctionType
AX_X = mybir.AxisListType.X

N = 1250
D = 512
TILE = 125
NT = N // TILE
FB = D // 128
CH = [(0, 500), (500, 500), (1000, 250)]
E = 8
HID = 256
HEADS, DH = 8, 64
GROUPS, GT = 17, 10
NOH = 4
PRIME = 2 * GT
WIN = 128
LASTWIN = N - WIN
FEW = 3
EPS = 1e-5
BANKS = 8
WIDE = 4


def build(nc, x, src, dst, L0_gnn_Wl1, L0_gnn_bl1, L0_gnn_Wr1, L0_gnn_Wl2, L0_gnn_bl2, L0_gnn_Wr2,
          L0_mix_Wq, L0_mix_Wk, L0_mix_Wv, L0_mix_W1, L0_mix_W2,
          L0_ffn_Wg, L0_ffn_bg, L0_ffn_W1, L0_ffn_b1, L0_ffn_W2, L0_ffn_b2,
          L1_gnn_W1, L1_gnn_b1, L1_gnn_W2, L1_gnn_b2, L1_mix_W_qk,
          L1_ffn_ln_g, L1_ffn_ln_b, L1_ffn_Wq, L1_ffn_Wk, L1_ffn_Wv, L1_ffn_Wo, L1_ffn_qn_g, L1_ffn_kn_g,
          L1_ffn_gate_W, L1_ffn_gate_b, L1_ffn_W1, L1_ffn_b1, L1_ffn_W2, L1_ffn_b2, out):
    COL = {"bl1": 0, "gb1": 4, "m0b1": 12, "m1b1": 28, "ln_g": 44, "ln_b": 48, "qn_g": 52, "kn_g": 53}
    ctx = ExitStack()
    with ctx:
        def at(name, shape, dt, offset):
            return nc.alloc_sbuf_tensor_at(name, shape, dt, offset=offset)

        class AsF32:

            def __init__(self, t):
                self.t = t

            def __getitem__(self, idx):
                return self.t[idx].bitcast(F32)

        class Pair:

            def __init__(self, name, shape, offset, size=None, lo_at=None):
                size = lo_at - offset if lo_at else size or 4 * width(shape[1:])
                self.hi = at(name + "_hi", shape, F32R, offset)
                self.hi32 = AsF32(self.hi)
                self.lo = at(name + "_lo", shape, F32R, offset + size)
                self.lo32 = at(name + "_was", shape, F32, offset + size)

        def width(xs):
            p = 1
            for v in xs:
                p *= v
            return p

        BASE = 16512
        A0 = BASE
        SLOT = 20480
        S = [A0 + 50016 + SLOT * k for k in range(6)]
        WA0 = S[5] + SLOT
        WB0 = WA0 + 16384
        M0 = WB0 + 16384

        CNTB = at("CNTB", [128, N], F32, M0)
        ident = at("ident", [128, 128], F32, M0 + 5024)
        identb = at("identb", [128, 128], BF16, M0 + 5536)
        causal = at("causal", [125, 125], BF16, M0 + 5792)
        m = M0 + 6048
        LNS = [at(f"LNS{r}", [125, 16], F32, m + 64 * r) for r in range(2)]
        cols = at("cols", [128, 40], F32, m + 128)
        ccol = at("ccol", [128, 56], F32, m + 288)
        gate = at("gate", [125, NT, E], F32, m + 512)
        invc = at("invc", [125, NT], F32, m + 832)
        dinc = at("dinc", [125, NT], F32, m + 896)
        ones2 = at("ones2", [128, 8], F32, m + 960)
        flags = at("flags", [1, 24], I32, m + 992)
        zero = at("zero", [128, 8], F32, m + 1088)

        xn = Pair("xn", [125, NT, D], S[0], SLOT)
        xnT = Pair("xnT", [128, FB, N], S[2], SLOT)
        rawk = at("rawk", [128, FB, D], F32, S[4])
        raw2 = at("raw2", [128, FB, D], F32, S[4] + 8192)
        vecs = at("vecs", [54, 128], F32, A0 + 40960)
        rawq = at("rawq", [128, FB, D], F32, A0 + 32768)
        MI = Pair("MI", [128, FB, D], S[4])
        G = Pair("G", [128, FB, D], S[4] + 16384)
        T0 = S[4] + 32768
        xt_ = [at(f"x_t{r}", [125, D], F32, T0 + 2048 * r) for r in range(2)]
        xnf = [at(f"xnf{r}", [125, D], F32, T0 + 4096 + 2048 * r) for r in range(2)]
        bl2B = at("bl2B", [125, D], F32, T0 + 4096)
        W1p = Pair("W1p", [128, FB, D], A0)
        W2T = Pair("W2T", [128, FB, D], A0 + 16384)
        Wvp = Pair("Wvp", [128, FB, D], WB0)
        WA = Pair("WA", [128, FB, D], WA0)
        WB = Pair("WB", [128, FB, D], WB0)
        ctxp = Pair("ctx", [128, FB, D], A0)
        kT = [at(f"kT{r}", [128, N], F32, A0 + 16384 + 5024 * r) for r in range(2)]
        ek = Pair("ek", [125, NT, 128], A0 + 26432)
        c1 = [Pair(f"c1{r}", [128, FB, 128], A0 + 36672 + 4096 * r) for r in range(2)]
        cxt = at("cxt", [128, D], F32, A0 + 44864)
        c1f = at("c1f", [128, D], F32, A0 + 46912)
        qe = [at(f"qe{r}", [125, D], F32, A0 + 16384 + 2048 * r) for r in range(2)]
        qT = [Pair(f"qT{r}", [128, FB, TILE], A0 + 26432 + 4032 * r, 2016) for r in range(2)]
        AT = at("AT", [125, NT, N], F32R, A0)
        AT32 = at("AT32", [125, NT, N], F32, A0)
        e0 = S[0]
        srcI = at("srcI", [85, 2, 125], I32, e0)
        dstI = at("dstI", [85, 2, 125], I32, e0 + 1024)
        grpI = at("grpI", [GROUPS, N], I32, e0 + 2048)
        srcR = at("srcR", [85, 2, 125], F32, e0 + 7072)
        dstR = at("dstR", [85, 2, 125], F32, e0 + 8096)
        grpR = at("grpR", [GROUPS, N], F32, e0 + 9120)
        srcF = at("srcF", [125, 170], F32, e0 + 14144)
        dstF = at("dstF", [125, 170], F32, e0 + 14848)
        gst = at("gst", [GROUPS, 8], F32, e0 + 15552)
        gD = at("gD", [GROUPS, 2 * GROUPS], F32, e0 + 15584)
        wB = at("wB", [125, 24], F32, e0 + 15744)
        bW = at("bW", [125, 16], F32, e0 + 15872)
        onesA = at("onesA", [125, 128], F32, e0 + 15936)
        e1 = S[1]
        iota = at("iota", [125, N], F16, e1)
        iotaw = at("iotaw", [125, WIN], F16, e1 + 2528)
        onesR = at("onesR", [125, 128], F32R, e0 + 2048)
        ohs = [at(f"ohs{r}", [125, N], BF16, e1 + 7808 + 2528 * r) for r in range(NOH)]
        ohd = [at("ohd0", [125, GT, WIN], BF16, e1 + 17920), at("ohd1", [125, GT, WIN], BF16, e0 + 16448)]
        rows = at("rows", [125, 4 * GROUPS + 4], F32, e0 + 19712)
        rel = at("rel", [125, GROUPS * GT], F32, e0 + 19008)
        wraw = [at(f"wraw{r}", [128, FB, D], F32, (e1 + 2816, S[4] + 16384)[r]) for r in range(2)]
        wout = [at(f"wout{r}", [128, FB, D], F32, (e1 + 11008, S[4] + 24576)[r]) for r in range(2)]

        PS = ctx.enter_context(nc.psum_tensor("PS", [128, BANKS, 512], F32))

        y = Pair("y", [125, NT, D], S[0], SLOT)
        hT = Pair("hT", [128, FB, N], S[4], SLOT)
        inv0 = at("inv0", [128, N], F32, S[4])
        INVB = at("INVB", [128, N], F32, WB0)
        sc = [at(f"sc{r}", [128, 500], F32, WB0 + 5024 + 2016 * r) for r in range(2)]
        xw = [at(f"xw{r}", [125, D], F32, WA0 + 2048 * r) for r in range(WIDE)]
        xnw = [at(f"xnw{r}", [125, D], F32, WA0 + 8192 + 2048 * r) for r in range(2)]
        BIAS = 32
        acc = at("acc", [125, NT, D], F32, S[0])
        hE = [Pair(f"hE{r}", [128, 2, N], S[4 + r], 10016) for r in range(2)]
        W1P = [Pair(f"mW1{r}", [128, FB, HID], (WA0, WB0)[r]) for r in range(2)]
        W2P = [Pair(f"mW2{r}", [128, 2, D], (WA0, WB0)[r] + 8192) for r in range(2)]
        xm = [at(f"xm{r}", [125, D], F32, S[1] + 2048 * r) for r in range(WIDE)]
        xnm = [at(f"xnm{r}", [125, D], F32, S[1] + 8192 + 2048 * r) for r in range(2)]
        GT_ = [S[5] + 10240, A0 + 40000]
        WgP = [Pair(f"WgP{s}", [128, FB, E], GT_[s], 128) for s in range(2)]
        b2P = [Pair(f"b2P{s}", [E, 1, D], GT_[s] + 256) for s in range(2)]
        bgB = [at(f"bgB{s}", [125, E], F32, GT_[s] + 4352) for s in range(2)]
        iota8 = at("iota8", [125, E], F32, GT_[0] + 4384)
        lgt = [at(f"lgt{s}", [125, NT, E], F32, GT_[s] + 4416) for s in range(2)]
        ex = [at(f"ex{s}", [125, NT, E], F32, GT_[s] + 4736) for s in range(2)]
        cand = at("cand", [125, NT, E], F32, GT_[0] + 5056)
        gred = [at(f"gred{s}", [125, 4, NT], F32, GT_[s] + 5376) for s in range(2)]
        gT = [Pair(f"gT{s}", [E, N], (S[5], A0)[s], 5024) for s in range(2)]
        xn2 = Pair("xn2", [125, NT, D], S[4], lo_at=S[0])
        QC = 2 * TILE
        kx = [at(f"kx{r}", [125, D], F32, S[1] + 2048 * r) for r in range(3)]
        kacc = at("kacc", [125, D], F32, S[1] + 6144)
        kp = [Pair(f"kp{r}", [125, D], S[1] + 8192 + 4096 * r) for r in range(2)]
        ksum = Pair("ksum", [128, FB, 2], S[1] + 16384)
        kv = Pair("kv", [128, FB, D], S[5])
        xq = [at(f"xq{r}", [125, D], F32, S[5] + 16384 + 2048 * r) for r in range(2)]
        q2 = [Pair(f"q2_{r}", [128, FB, QC], S[1] + 8064 * r, 4032) for r in range(2)]
        zT = Pair("zT", [128, FB, N], S[2], SLOT)
        h1T = Pair("h1T", [128, FB, N], S[1], lo_at=S[5])
        y3 = Pair("y3", [125, NT, D], S[4], lo_at=S[0])
        xg = [at(f"xg{r}", [125, D], F32, (S[1], S[1] + 2048, S[1] + 16384, S[1] + 18432)[r]) for r in range(WIDE)]
        xnA = [at(f"xnA{r}", [125, D], F32, S[1] + 4096 + 2048 * r) for r in range(2)]
        xnB = [at(f"xnB{r}", [125, D], F32, S[1] + 8192 + 2048 * r) for r in range(2)]
        b2B = at("b2B", [125, D], F32, S[1] + 12288)
        gt_ = at("gt", [125, D], F32, S[1] + 14336)
        hxT = Pair("hxT", [128, FB, N], S[2], SLOT)
        QA = at("QA", [128, HEADS, N], F32R, A0)
        QA32 = AsF32(QA)
        KA = at("KA", [128, HEADS, N], F32R, S[0])
        KA32 = AsF32(KA)
        KLO = at("KLO", [128, FB, N], F32R, S[4])
        V32 = at("V32", [125, NT, D], F32, S[5])
        V = Pair("V", [125, NT, D], S[2], SLOT)
        sqr = [at(f"sqr{r}", [125, D], F32, A0 + 40000 + 2048 * r) for r in range(2)]
        unit = [at(f"unit{r}", [125, D], F32, A0 + 44096 + 2048 * r) for r in range(2)]
        XA, XB = A0 + 40000, WB0
        sel = at("sel", [128, 2, 128], F32R, XA)
        rowmax = at("rowmax", [128, N], F32R, M0)
        sacc = [at(f"sacc{a}", [125, 500], F32, XA + 1024 + 2016 * a) for a in range(2)]
        NP, NPT = 8, 4
        P = [at(f"P{r}", [125, 500], F32, WA0 + 2016 * r) for r in range(NP)]
        Wo = Pair("Wo", [128, FB, D], S[0])
        PT = [Pair(f"PT{r}", [125, 500], XB + 4032 * r, 2016) for r in range(NPT)]
        chmax = at("chmax", [125, 2, NT, 3], F32, XA + 9088)
        negm = at("negm", [125, NT, 2], F32, XA + 9344)
        ones64 = at("ones64", [125, DH], F32, XA + 9440)
        maskall = at("maskall", [125, 125], BF16, XA + 9696)
        OT32 = at("OT32", [128, FB, N], F32, S[5])
        OT = at("OT", [128, FB, 2, N], F32R, A0)
        yT = Pair("yT", [128, FB, N], S[2], SLOT)
        def dram(name, shape):
            return nc.dram_tensor(name, shape, F32, kind="Internal").ap()

        torch_w = {"Wl1": L0_gnn_Wl1, "Wr1": L0_gnn_Wr1, "Wl2": L0_gnn_Wl2, "Wr2": L0_gnn_Wr2,
                   "Wqk0": L1_mix_W_qk[0:D, :], "Wqk1": L1_mix_W_qk[D:2 * D, :]}
        WT = {k: dram("WT_" + k, (D, D)) for k in torch_w}
        xa = dram("x_mixed", (N, D))
        xb = dram("x_r2", (N, D))
        xc = dram("x_one", (N, D))
        xd = dram("x_two", (N, D))
        xe = dram("x_mix1", (N, D))
        xf = dram("x_three", (N, D))

        def sem(name):
            return ctx.enter_context(nc.semaphore(name))

        filled = [sem(f"filled{b}") for b in range(BANKS)]
        drained = [sem(f"drained{b}") for b in range(BANKS)]
        hi_done = sem("hi_done")
        dve_step, act_step, pool_step = sem("dve_step"), sem("act_step"), sem("pool_step")
        const_ready = sem("const_ready")
        rawk_in, raw2_in, rawq_in = sem("rawk_in"), sem("raw2_in"), sem("rawq_in")
        wraw_in = [sem("wraw_in0"), sem("wraw_in1")]
        unit_in = [sem("unit_in0"), sem("unit_in1")]
        unit_hi, unit_ready = sem("unit_hi"), sem("unit_ready")
        x_in = [sem(f"x_in{r}") for r in range(WIDE)]
        x_out = [sem(f"x_out{r}") for r in range(WIDE)]
        ln_var, ln_std, ln_xnf, ln_hi = sem("ln_var"), sem("ln_std"), sem("ln_xnf"), sem("ln_hi")
        ln_lo = sem("ln_lo")
        mi_sum, mi_hi, mi_ready = sem("mi_sum"), sem("mi_hi"), sem("mi_ready")
        k_max = sem("k_max")
        cx_hi, cx_ready = sem("cx_hi"), sem("cx_ready")
        q_max, q_norm = sem("q_max"), sem("q_norm")
        vecs_in, bl2_in = sem("vecs_in"), sem("bl2_in")
        wt_out = [sem("wt_out0"), sem("wt_out1")]
        idx_in, idx_f = sem("idx_in"), sem("idx_f")
        edge_ready = sem("edge_ready")
        src_ready, dst_ready = sem("src_ready"), sem("dst_ready")
        edge_tiles, window_free = sem("edge_tiles"), sem("window_free")
        dst_squared, all_squared = sem("dst_squared"), sem("all_squared")
        all_src, all_dst, all_tiles, all_taken, all_rel = sem("all_src"), sem("all_dst"), sem("all_tiles"), sem("all_taken"), sem("all_rel")
        at_zero, at_built = sem("at_zero"), sem("at_built")
        deg_ready, deg_root = sem("deg_ready"), sem("deg_root")
        inv_ready = sem("inv_ready")

        inv_placed, a1_sum, a1_hi, a1_ready = sem("inv_placed"), sem("a1_sum"), sem("a1_hi"), sem("a1_ready")
        moe_in = [sem("moe0_in"), sem("moe1_in")]
        iota_ready = sem("iota_ready")
        wg_hi, wg_ready = sem("wg_hi"), sem("wg_ready")
        lg_less, lg_exp, gate_ready = sem("lg_less"), sem("lg_exp"), sem("gate_ready")
        hid_done, hid_hi, hid_ready = sem("hid_done"), sem("hid_hi"), sem("hid_ready")
        w_in = [[sem(f"w{m + 1}_in{r}") for m in range(2)] for r in range(2)]
        w_hi = [sem(f"w{m + 1}_hi") for m in range(2)]
        w_ready = [sem(f"w{m + 1}_ready") for m in range(2)]
        bias_placed = sem("bias_placed")
        x2_sum, xn2_lo = sem("x2_sum"), sem("xn2_lo")
        k_min, k_exped, k_hi, k_ready, k_used = (sem(n) for n in ("k_min", "k_exped", "k_hi", "k_ready", "k_used"))
        q_min, q_exped, q_hi, q_ready = (sem(n) for n in ("q_min", "q_exped", "q_hi", "q_ready"))
        kacc_done, self_loops = sem("kacc_done"), sem("self_loops")
        xs_whole, xs_scaled, xs_hi, xs_ready = (sem(n) for n in ("xs_whole", "xs_scaled", "xs_hi", "xs_ready"))
        z_hi, z_ready = sem("z_hi"), sem("z_ready")
        h1_hi, h1_ready = sem("h1_hi"), sem("h1_ready")
        y3_hi, y3_ready = sem("y3_hi"), sem("y3_ready")
        b2_in, x3_sum = sem("b2_in"), sem("x3_sum")
        hx_hi, hx_ready = sem("hx_hi"), sem("hx_ready")
        v_hi, v_ready = sem("v_hi"), sem("v_ready")
        squared, unit_sum, unit_root, unit_done = (sem(n) for n in ("squared", "unit_sum", "unit_root", "unit_done"))
        k_twice = sem("k_twice")
        att_ready, max_found = sem("att_ready"), sem("max_found")
        p_hi, p_ready, p_added, pt_used = sem("p_hi"), sem("p_ready"), sem("p_added"), sem("pt_used")
        wo_in, wo_hi, wo_ready = sem("wo_in"), sem("wo_hi"), sem("wo_ready")
        ot_whole, ot_hi, ot_ready = sem("ot_whole"), sem("ot_hi"), sem("ot_ready")
        place, uses = {}, [0] * BANKS

        def plan(key, bank_):
            uses[bank_] += 1
            assert key not in place
            place[key] = (bank_, uses[bank_])

        ring_at = [0]

        def plan_ring(keys, ring=tuple(range(BANKS))):
            for key in keys:
                plan(key, ring[ring_at[0] % len(ring)])
                ring_at[0] += 1

        WORK = [("wt", w, ib) for w in ("k", "2") for ib in range(FB)] + [("vec",)]
        WORK += [("mi", b) for b in range(FB)] + [("g", b) for b in range(FB)]
        WORK += [("wt", "q", ib) for ib in range(FB)]

        def work_after(i):
            return WORK[2 * i:2 * i + 2] if i < NT - 1 else WORK[2 * i:]

        for i in range(NT):
            plan_ring([("xt", 0, i)] + work_after(i))
        for b in range(FB + 1):
            if b == 0:
                plan_ring([("k", 0, c) for c in range(3)])
            if b + 1 < FB:
                plan_ring([("k", b + 1, c) for c in range(3)])
            if b < FB:
                plan_ring([("kt", b, q) for q in range(3)])
                plan_ring([("c1", b), ("c1t", b)])
            if b > 0:
                plan_ring([("cx", b - 1)])
        names = list(torch_w)
        TORCH = [("wt", w, ib) for w in names for ib in range(FB)]
        FIRST, PER, PREP = 2, 3, 5
        assert PER * (NT - FIRST) == len(TORCH)

        def torch_after(i):
            return TORCH[PER * (i - FIRST):PER * (i - FIRST + 1)] if i >= FIRST else []

        plan_ring([("q", 0)])
        for i in range(NT):
            if i + 1 < NT:
                plan_ring([("q", i + 1)])
            plan_ring(torch_after(i) + [("qt", i), ("mo", i)])
            if i == PREP:
                plan_ring([("ix",), ("wv",)])
        before_edges = list(uses)
        plan_ring([("cb", 0), ("cb", 1), ("cb", 2), ("cc",)])

        plan_ring([("y1", i) for i in range(NT)])
        plan_ring([("r1", f, c) for f in range(FB) for c in range(3)])
        plan_ring([("a1", f, c) for f in range(FB) for c in range(3)])
        plan_ring([("y2", i) for i in range(NT)])
        plan_ring([("r2", i) for i in range(NT)])
        for i in range(NT + 1):
            if i < NT:
                plan_ring([("a2", i)])
            if i >= 1:
                plan_ring([("xt", 1, i - 1)])
        lnno = {(s, i): NT * s + i for s in range(3) for i in range(NT)}
        lnno |= {(3 + s, i): 3 * NT + 2 * i + s for s in range(2) for i in range(NT)}
        UNITS = [("W1", 0), ("Wv", 1), ("Wl1", 0), ("Wr1", 1), ("Wl2", 0), ("Wr2", 1)]
        UNITS += [("Wqk1", 1), ("Wqk0", 0), ("gW1a", 1), ("gW2a", 0), ("gW1b", 1), ("gW2b", 0)]
        UNITS += [("aWv", 1), ("aWq", 0), ("aWk", 1)]
        WIDE_STAGES = ["xr2", "xa2", "xm0", "xa3", "xm1"]
        X_LOADS = ["x", "xmix", "xr2", "xa2", "xm0", "xq", "xa3", "xm1"]
        X_STORES = ["xmix", "xr2", "xa2", "xm0", "xq", "xa3", "xm1"]
        def plan_moe(s):
            plan_ring([("lt", s, c) for c in range(3)])
            plan_ring([("hd", s, 0, 0, c) for c in range(3)] + [("lg", s)])
            plan_ring([("hd", s, 0, 1, c) for c in range(3)])
            plan_ring([("gt", s, q) for q in range(3)])
            plan_ring([("ac", s, i) for i in range(NT)])
            hd = lambda e: plan_ring([("hd", s, e, f, c) for f in range(2) for c in range(3)])
            eo = lambda e: plan_ring([("eo", s, e, i) for i in range(NT)])
            for h, o in ((1, 0), (2, 1)):
                hd(h)
                eo(o)
            for b in range(BANKS):
                uses[b] += 4 * (PAIRS - 1)
            hd(7)
            eo(6)
            if s == 1:
                eo(7)
            else:
                for i in range(NT + 1):
                    if i < NT:
                        plan_ring([("eo", s, 7, i)])
                    if i >= 1:
                        plan_ring([("xt", 2, i - 1)])

        PAIRS = E // 2 - 1
        plan_moe(0)
        LOW = (0, 1, 2, 3)
        for b in range(FB):
            plan(("kv", b), 4 + b)
        plan_ring([("k2", i) for i in range(NT)], LOW)
        plan(("ks",), 3)
        ring_at[0] = 0
        NQ = N // QC
        for g in range(NQ + 1):
            if g < NQ:
                plan_ring([("q2", g, f) for f in range(FB)])
            if g > 0:
                plan_ring([(k, i) for i in (2 * g - 2, 2 * g - 1) for k in ("dn", "mx")])
        plan_ring([("z", f, c) for f in range(FB) for c in range(3)])
        for hf in range(2):
            plan_ring([("h1", hf, f, c) for f in range(FB) for c in range(3)])
            plan_ring([("yy", hf, i) for i in range(NT)])
        for i in range(NT + 3):
            if i < NT:
                plan_ring([("a3", i)])
            if 2 <= i < NT + 2:
                plan_ring([("xt", 4, i - 2)])
            if i >= 3:
                plan_ring([("pv", i - 3)])
        HX = [(f, c) for f in range(FB) for c in range(3)]
        PIECES = [(a, i, q) for i in range(NT) for a in range(2) for q in range(i // 4 + 1)]

        def piece_width(i, q):
            return min(4, i + 1 - 4 * q) * TILE

        def pieces_of(i):
            return [("mx", 0, *p) for p in PIECES if p[1] == i]

        def max_work(b):
            return [("mx", b, *p) for p in PIECES] + [("mt", b, c) for c in range(3)]

        for w in ("q", "k"):
            for i in range(NT + 1):
                if i < NT:
                    plan_ring([("p" + w, i)])
                if i >= 1:
                    plan_ring([("t" + w, i - 1)])
                if w == "k" and i >= 3:
                    plan_ring(pieces_of(i - 3))
        plan_ring(pieces_of(NT - 2) + pieces_of(NT - 1) + [("mt", 0, c) for c in range(3)])
        STEPS = [(b, c, a, j) for b in range(FB) for c in range(3) for a in range(2)
                 for j in range((CH[c][0] + CH[c][1]) // TILE)]
        PER_PAIR = len(STEPS) // FB
        LAG = 3

        def last_key(c):
            return (CH[c][0] + CH[c][1]) // TILE - 1

        def valid(c, j):
            o, w = CH[c]
            return (2 * TILE if TILE * j - o >= 2 * TILE else 0), w

        def chunk_after(g):
            if g >= LAG:
                b, c, a, j = STEPS[g - LAG]
                if a == 1 and j == last_key(c):
                    return (b, c)
            return None

        ring_at[0] = 0
        ov_no = [0]
        between = []
        for g in range(len(STEPS) + LAG):
            if g < len(STEPS):
                plan(("sT", g), g % 3)
                if g % PER_PAIR == 0 and STEPS[g][0] + 1 < FB:
                    between = max_work(STEPS[g][0] + 1)
            if g >= LAG:
                b, c, a, j = STEPS[g - LAG]
                if j == 0:
                    plan(("ov", b, c, a), 4 + ov_no[0] % 3)
                    ov_no[0] += 1
                if a == 1 and j == last_key(c):
                    plan_ring([("ss", b, c)], (3, 7))
            if between and not chunk_after(g - 1):
                plan_ring([between.pop(0)], (3, 7))
        assert not between
        WO = [(f, c) for c in range(3) for f in range(FB)]
        plan_ring([("wo", f, c) for f, c in WO])
        plan_moe(1)

        def bank(key):
            return PS[:, place[key][0], :]

        def completed(eng, key, later=0):
            b, n = place[key]
            eng.wait_ge(filled[b], later + n)

        def carried(eng, key, later=0):
            b, n = place[key]
            eng.wait_ge(drained[b], later + n)

        def drain(ins, key):
            ins.then_inc(drained[place[key][0]], 1)

        def natural(w):
            return w.rearrange("(b p) n -> p b n", p=128)

        def row(v, parts=TILE):
            return v.rearrange("(a n) -> a n", a=1).broadcast_to((parts, v.shape[0]))

        xin = x.rearrange("(t p) d -> t p d", p=TILE)
        xav = xa.rearrange("(t p) d -> t p d", p=TILE)

        def numbered(stages):
            numbers, had = {}, [0] * WIDE
            for s in stages:
                for i in range(NT):
                    r = i % (WIDE if s in WIDE_STAGES else 2)
                    had[r] += 1
                    numbers[(s, i)] = (r, had[r])
            return numbers

        x_no, out_no = numbered(X_LOADS), numbered(X_STORES)

        def x_stored(eng, key):
            r, n = out_no[key]
            eng.wait_ge(x_out[r], 16 * n)

        unit_no, landed = {}, [0, 0]
        for name, region in UNITS:
            landed[region] += 16
            unit_no[name] = (region, landed[region], len(unit_no) + 1)

        def unit_pair(name):
            return {"W1": W1p, "Wv": Wvp}.get(name, (WA, WB)[unit_no[name][0]])

        def unit_split(eng, name):
            eng.wait_ge(unit_ready, unit_no[name][2])

        def x_landed(eng, key):
            r, n = x_no[key]
            eng.wait_ge(x_in[r], 16 * n)

        act_his, dve_los = [], []

        block = ctx.enter_context(nc.Block())

        @block.sync
        def _(sp):
            def load_x(key, view, i):
                r, n = x_no[key]
                sp.dma_start(xt_[r][:], view[i]).then_inc(x_in[r], 16)

            load_x(("x", 0), xin, 0)
            load_x(("x", 1), xin, 1)
            sp.dma_start(rawk[:], natural(L0_mix_Wk)).then_inc(rawk_in, 16)

            def load_vectors():
                v2 = lambda v: v.rearrange("(a p) -> a p", p=128)
                for name, v in (("bl1", v2(L0_gnn_bl1)), ("gb1", v2(L1_gnn_b1)),
                                ("m0b1", L0_ffn_b1.rearrange("e (f p) -> (e f) p", p=128)),
                                ("m1b1", L1_ffn_b1.rearrange("e (f p) -> (e f) p", p=128)),
                                ("ln_g", v2(L1_ffn_ln_g)), ("ln_b", v2(L1_ffn_ln_b))):
                    sp.dma_start(vecs[COL[name]:COL[name] + v.shape[0], :], v).then_inc(vecs_in, 16)
                for name, v in (("qn_g", L1_ffn_qn_g), ("kn_g", L1_ffn_kn_g)):
                    for h in range(2):
                        sp.dma_start(vecs[COL[name]:COL[name] + 1, h * DH:(h + 1) * DH],
                                     v.rearrange("(a n) -> a n", a=1)).then_inc(vecs_in, 16)

            for i in range(2, NT):
                sp.wait_ge(ln_xnf, i - 1)
                load_x(("x", i), xin, i)
                if i == 2:
                    sp.dma_start(W1p.lo32[:], natural(L0_mix_W1)).then_inc(unit_in[0], 16)
                    sp.dma_start(raw2[:], natural(L0_mix_W2)).then_inc(raw2_in, 16)
                elif i == 3:
                    sp.dma_start(Wvp.lo32[:], natural(L0_mix_Wv)).then_inc(unit_in[1], 16)
                elif i == 4:
                    load_vectors()
                elif i == 5:
                    sp.dma_start(rawq[:], natural(L0_mix_Wq)).then_inc(rawq_in, 16)

            def load_raw(n):
                sp.dma_start(wraw[n % 2][:], natural(torch_w[names[n]])).then_inc(wraw_in[n % 2], 16)

            def store_transpose(n):
                for b in range(FB):
                    carried(sp, ("wt", names[n], b))
                if n + 2 < len(names):
                    load_raw(n + 2)
                sp.dma_start(natural(WT[names[n]]), wout[n % 2][:]).then_inc(wt_out[n % 2], 16)

            def load_edges():
                hv = lambda a: a.rearrange("(h p c) -> p h c", h=2, c=125)
                sp.dma_start(srcI[:], hv(src)).then_inc(idx_in, 16)
                sp.dma_start(dstI[:], hv(dst)).then_inc(idx_in, 16)
                sp.dma_start(grpI[:], dst.rearrange("(g c) -> g c", g=GROUPS)).then_inc(idx_in, 16)

            completed(sp, ("xt", 0, NT - 1))
            sp.wait_ge(ln_lo, NT)
            sp.dma_start(bl2B[:], row(L0_gnn_bl2)).then_inc(bl2_in, 16)
            for i in range(NT + 1):
                if i < NT:
                    if i >= 2:
                        sp.wait_ge(x_out[i % 2], 16 * (i // 2))
                    load_x(("xmix", i), xin, i)
                if i == 1:
                    completed(sp, ("cx", FB - 1))
                    load_raw(0)
                    load_raw(1)
                    load_edges()
                if i >= 1:
                    carried(sp, ("mo", i - 1))
                    sp.dma_start(xav[i - 1], xt_[(i - 1) % 2][:]).then_inc(x_out[(i - 1) % 2], 16)
                    for _, name, ib in torch_after(i - 1):
                        if ib == FB - 1:
                            store_transpose(names.index(name))
            def load_unit(name, view):
                region = unit_no[name][0]
                sp.dma_start((WA, WB)[region].lo32[:], view).then_inc(unit_in[region], 16)

            def expert_w1(region, W1, e):
                sp.dma_start(W1P[region].lo32[:], W1[bass.ds(e, 1)].rearrange("a (b p) n -> p (a b) n", p=128))\
                    .then_inc(w_in[region][0], 16)

            def expert_w2(region, W2, e):
                sp.dma_start(W2P[region].lo32[:], W2[bass.ds(e, 1)].rearrange("a (b p) n -> p (a b) n", p=128))\
                    .then_inc(w_in[region][1], 16)

            def expert_into(region, W1, W2, e):
                expert_w1(region, W1, e)
                expert_w2(region, W2, e)

            def load_transposed(name):
                n = names.index(name)
                sp.wait_ge(wt_out[n % 2], 16 * (n // 2 + 1))
                load_unit(name, natural(WT[name]))

            def load_tile(stage, i, view, ring):
                r, n = x_no[(stage, i)]
                sp.dma_start(ring[r][:], view[i]).then_inc(x_in[r], 16)

            def store_tile(stage, i, view, ring):
                r, n = out_no[(stage, i)]
                sp.dma_start(view[i], ring[r][:]).then_inc(x_out[r], 16)

            completed(sp, ("k", FB - 1, 2))
            load_transposed("Wl1")
            load_transposed("Wr1")
            completed(sp, ("y1", NT - 1))
            load_transposed("Wl2")
            sp.wait_ge(a1_ready, 3 * FB)
            load_transposed("Wr2")
            completed(sp, ("y2", NT - 1))
            xbv, xcv = (a.rearrange("(t p) d -> t p d", p=TILE) for a in (xb, xc))

            def stream(stage, before, src_, dst_, ring, computed, also=None):
                for i in range(NT - (WIDE if before in WIDE_STAGES else 2), NT):
                    x_stored(sp, (before, i))
                for i in range(WIDE - 1):
                    load_tile(stage, i, src_, ring)
                for i in range(NT):
                    computed(i)
                    store_tile(stage, i, dst_, ring)
                    if i + WIDE - 1 < NT:
                        if i >= 1:
                            x_stored(sp, (stage, i - 1))
                            if also:
                                also(i - 1)
                        load_tile(stage, i + WIDE - 1, src_, ring)

            stream("xr2", "xmix", xav, xbv, xw, lambda i: carried(sp, ("r2", i)))
            sp.dma_start(WgP[0].lo32[:], natural(L0_ffn_Wg)).then_inc(moe_in[0], 16)
            sp.dma_start(b2P[0].lo32[:], L0_ffn_b2.rearrange("e (a n) -> e a n", a=1)).then_inc(moe_in[0], 16)
            sp.dma_start(bgB[0][:], row(L0_ffn_bg)).then_inc(moe_in[0], 16)
            expert_into(1, L0_ffn_W1, L0_ffn_W2, 0)
            stream("xa2", "xr2", xbv, xcv, xw, lambda i: carried(sp, ("a2", i)),
                   lambda i: sp.wait_ge(ln_xnf, lnno[(1, i)] + 1))
            def load_experts(s, W1, W2):
                with sp.Fori(0, PAIRS) as k:
                    completed(sp, ("hd", s, 1, 1, 2), k * 4)
                    for e in range(2):
                        expert_w1(1 - e, W1, k * 2 + (e + 2))
                    for e in range(2):
                        completed(sp, ("eo", s, e, NT - 1), k * 4)
                        expert_w2(1 - e, W2, k * 2 + (e + 2))

            completed(sp, ("xt", 1, NT - 1))
            for i in range(NT - WIDE, NT):
                x_stored(sp, ("xa2", i))
            expert_into(0, L0_ffn_W1, L0_ffn_W2, 1)
            load_experts(0, L0_ffn_W1, L0_ffn_W2)
            completed(sp, ("eo", 0, E - 2, NT - 1))
            load_transposed("Wqk1")
            xdv = xd.rearrange("(t p) d -> t p d", p=TILE)
            stream("xm0", "xa2", xcv, xdv, xm, lambda i: carried(sp, ("eo", 0, 7, i)),
                   lambda i: sp.wait_ge(ln_xnf, lnno[(2, i)] + 1))
            completed(sp, ("eo", 0, E - 1, NT - 1))
            load_transposed("Wqk0")
            completed(sp, ("k2", NT - 1))
            load_unit("gW1a", natural(L1_gnn_W1[:, 0:D]))
            xev, xfv = (a.rearrange("(t p) d -> t p d", p=TILE) for a in (xe, xf))
            for i in range(NT + 1):
                if i < NT:
                    if i >= 2:
                        x_stored(sp, ("xq", i - 2))
                    if i < 2:
                        completed(sp, ("eo", 0, E - 1, NT - 1))
                    x_stored(sp, ("xm0", i))
                    load_tile("xq", i, xdv, xq)
                if i >= 1:
                    carried(sp, ("mx", i - 1))
                    store_tile("xq", i - 1, xev, xq)
                if i == NT - 1:
                    completed(sp, ("q2", NQ - 1, FB - 1))
                    load_unit("gW2a", natural(L1_gnn_W2[0:D, :]))
            completed(sp, ("h1", 0, FB - 1, 2))
            load_unit("gW1b", natural(L1_gnn_W1[:, D:2 * D]))
            completed(sp, ("yy", 0, NT - 1))
            load_unit("gW2b", natural(L1_gnn_W2[D:2 * D, :]))
            completed(sp, ("h1", 1, FB - 1, 2))
            load_unit("aWv", natural(L1_ffn_Wv))
            completed(sp, ("yy", 1, NT - 1))
            load_unit("aWq", natural(L1_ffn_Wq))
            sp.dma_start(b2B[:], row(L1_gnn_b2)).then_inc(b2_in, 16)
            stream("xa3", "xq", xev, xfv, xg, lambda i: sp.wait_ge(x3_sum, i + 1),
                   lambda i: sp.wait_ge(ln_xnf, lnno[(3, i)] + 1))
            completed(sp, ("pv", NT - 1))
            load_unit("aWk", natural(L1_ffn_Wk))
            completed(sp, ("sT", 2 * PER_PAIR - 1))
            sp.dma_start(Wo.lo32[:], natural(L1_ffn_Wo)).then_inc(wo_in, 16)
            last = ("ov", FB - 1, 2, 1)
            carried(sp, last)
            sp.dma_start(WgP[1].lo32[:], natural(L1_ffn_gate_W)).then_inc(moe_in[1], 16)
            sp.dma_start(b2P[1].lo32[:], L1_ffn_b2.rearrange("e (a n) -> e a n", a=1)).then_inc(moe_in[1], 16)
            sp.dma_start(bgB[1][:], row(L1_ffn_gate_b)).then_inc(moe_in[1], 16)
            expert_into(1, L1_ffn_W1, L1_ffn_W2, 0)
            expert_into(0, L1_ffn_W1, L1_ffn_W2, 1)
            load_experts(1, L1_ffn_W1, L1_ffn_W2)
            outv = out.rearrange("(t p) d -> t p d", p=TILE)
            stream("xm1", "xa3", xfv, outv, xm, lambda i: carried(sp, ("eo", 1, 7, i)))
            for i in range(NT - WIDE, NT):
                x_stored(sp, ("xm1", i))

        @block.gpsimd
        def _(pool):
            steps = [0]

            def link(ins):
                steps[0] += 1
                ins.then_inc(pool_step, 1)
                pool.wait_ge(pool_step, steps[0])

            link(pool.memset(ident[:], 0.0))
            pool.affine_select(out=ident[:], in_=ident[:], compare_op=ALU.not_equal, fill=1.0, base=0,
                               pattern=[[-1, 128]], channel_multiplier=1).then_inc(const_ready, 1)
            pool.wait_ge(const_ready, 1)
            link(pool.memset(ones2[:], 1.0))
            link(pool.memset(zero[:], 0.0))
            link(pool.memset(causal[:], 0.0))
            link(pool.affine_select(out=causal[:], in_=causal[:], compare_op=ALU.is_ge, fill=-1e30, base=0,
                                    pattern=[[-1, 125]], channel_multiplier=1))
            link(pool.tensor_copy(identb[:], ident[:]))

            def rounded(pair):
                was = pair.lo32[:]
                none = zero[0:was.shape[0], 0:1].broadcast_to((was.shape[0], was.shape[1] * was.shape[2]))\
                    .rearrange("p (b n) -> p b n", b=was.shape[1])
                return pool.tensor_tensor(pair.hi[:], was, none, ALU.add)

            def split(name):
                region, landed_, _ = unit_no[name]
                pair = unit_pair(name)
                pool.wait_ge(unit_in[region], landed_)
                rounded(pair).then_inc(unit_hi, 1)
                pool.wait_ge(unit_hi, unit_no[name][2])
                pool.tensor_tensor(pair.lo[:], pair.lo32[:], pair.hi32[:], ALU.subtract).then_inc(unit_ready, 1)

            split("W1")
            split("Wv")

            completed(pool, ("c1", FB - 1))
            link(pool.iota(iota[:], pattern=[[1, N]], base=0, channel_multiplier=0,
                           allow_small_or_imprecise_dtypes=True))
            link(pool.iota(bW[:, 0:NT], pattern=[[WIN, NT]], base=0, channel_multiplier=0,
                           allow_small_or_imprecise_dtypes=True))
            link(pool.iota(iotaw[:], pattern=[[1, WIN]], base=0, channel_multiplier=0,
                           allow_small_or_imprecise_dtypes=True))
            link(pool.memset(bW[:, NT - 1:NT], float(LASTWIN)))
            pool.memset(onesA[:], 1.0).then_inc(const_ready, 1)
            completed(pool, ("cx", FB - 1))
            carried(pool, ("cx", FB - 1))
            pool.wait_ge(cx_ready, FB)
            pool.memset(AT[:, 7:NT, :].bitcast(F32), 0.0).then_inc(at_zero, 1)
            completed(pool, ("mo", NT - 1))
            pool.memset(AT[:, 0:7, :].bitcast(F32), 0.0).then_inc(at_zero, 1)

            for name in ("Wl1", "Wr1", "Wl2", "Wr2"):
                split(name)
            def split_gate_weights(s):
                pool.wait_ge(moe_in[s], 48)
                for n, pair in enumerate((WgP[s], b2P[s])):
                    rounded(pair).then_inc(wg_hi, 1)
                    pool.wait_ge(wg_hi, 2 * s + n + 1)
                    pool.tensor_tensor(pair.lo[:], pair.lo32[:], pair.hi32[:], ALU.subtract).then_inc(wg_ready, 1)

            def split_experts(s):
                def part(e, e_, m):
                    region = 1 - e % 2
                    pair = (W1P, W2P)[m][region]
                    pool.wait_ge(w_in[region][m], (e_ - e % 2) * 8 + (64 * s + 16))
                    rounded(pair).then_inc(w_hi[m], 1)
                    pool.wait_ge(w_hi[m], e_ + (E * s + 1))
                    pool.tensor_tensor(pair.lo[:], pair.lo32[:], pair.hi32[:], ALU.subtract).then_inc(w_ready[m], 1)

                for e in range(2):
                    part(e, e, 0)
                    part(e, e, 1)
                with pool.Fori(0, PAIRS) as k:
                    for m in range(2):
                        for e in (2, 3):
                            part(e, k * 2 + e, m)

            completed(pool, ("r2", NT - 1))
            pool.iota(iota8[:], pattern=[[1, E]], base=0, channel_multiplier=0,
                      allow_small_or_imprecise_dtypes=True).then_inc(iota_ready, 1)
            split_gate_weights(0)
            split_experts(0)

            def x_plus_acc(s, i):
                carried(pool, ("eo", s, 6, i))
                x_landed(pool, (("xm0", "xm1")[s], i))
                pool.tensor_tensor(xm[i % WIDE][:], xm[i % WIDE][:], acc[:, i, :], ALU.add).then_inc(x2_sum, 1)

            x_plus_acc(0, 0)
            x_plus_acc(0, 1)
            for i in range(NT):
                if i + 2 < NT:
                    x_plus_acc(0, i + 2)
                pool.wait_ge(ln_hi, NT + i + 1)
                pool.tensor_tensor(xn2.lo[:, i, :], xnm[i % 2][:], xn2.hi32[:, i, :], ALU.subtract)\
                    .then_inc(xn2_lo, 1)
            split("Wqk1")
            pool.wait_ge(xn2_lo, NT)
            completed(pool, ("xt", 2, NT - 1))
            for i in range(NT - WIDE, NT):
                x_stored(pool, ("xm0", i))
            pool.memset(kacc[:], 0.0).then_inc(kacc_done, 1)
            for i in range(NT):
                if i == 1:
                    split("Wqk0")
                carried(pool, ("k2", i))
                pool.wait_ge(kacc_done, i + 1)
                pool.tensor_tensor(kacc[:], kacc[:], kx[i % 3][:], ALU.add).then_inc(kacc_done, 1)
            completed(pool, ("kv", FB - 1))
            for i in range(NT):
                pool.tensor_tensor(xn2.lo32[:, i, :], xn2.hi32[:, i, :], xn2.lo[:, i, :].bitcast(F32), ALU.add)\
                    .then_inc(xs_whole, 1)
            for name in ("gW1a", "gW2a", "gW1b", "gW2b", "aWv", "aWq", "aWk"):
                split(name)
            completed(pool, ("pk", NT - 1))
            none = zero[0:TILE, 0:1].broadcast_to((TILE, D))
            for i in range(NT):
                pool.tensor_tensor(V.hi[:, i, :], V32[:, i, :], none, ALU.add).then_inc(v_hi, 1)
                pool.wait_ge(v_hi, i + 1)
                pool.tensor_tensor(V.lo[:, i, :], V32[:, i, :], V.hi32[:, i, :], ALU.subtract).then_inc(v_ready, 1)
            wo_work = [(part, kb) for kb in range(FB) for part in ("hi", "lo")]

            def split_wo(n):
                part, kb = wo_work[n]
                if part == "hi":
                    pool.wait_ge(wo_in, 16)
                    pool.tensor_tensor(Wo.hi[:, kb, :], Wo.lo32[:, kb, :], zero[:, 0:1].broadcast_to((128, D)),
                                       ALU.add).then_inc(wo_hi, 1)
                else:
                    pool.wait_ge(wo_hi, kb + 1)
                    pool.tensor_tensor(Wo.lo[:, kb, :], Wo.lo32[:, kb, :], Wo.hi32[:, kb, :], ALU.subtract)\
                        .then_inc(wo_ready, 1)

            for g, (b, c, a, j) in enumerate(STEPS):
                carried(pool, ("sT", g))
                off, w = valid(c, j)
                if j == 0:
                    if (b, c) != (0, 0):
                        completed(pool, ("ss", *((b, c - 1) if c else (b - 1, 2))))
                    pool.tensor_tensor(sacc[a][:, 0:w], P[g % NP][:, 0:w], zero[0:TILE, 0:1].broadcast_to((TILE, w)),
                                       ALU.add).then_inc(p_added, 1)
                else:
                    pool.wait_ge(p_added, g)
                    pool.tensor_tensor(sacc[a][:, off:w], sacc[a][:, off:w], P[g % NP][:, off:w], ALU.add)\
                        .then_inc(p_added, 1)
                if b == FB - 1 and (g % PER_PAIR) % 4 == 3 and (g % PER_PAIR) // 4 < len(wo_work):
                    split_wo((g % PER_PAIR) // 4)
            split_gate_weights(1)
            split_experts(1)
            for i in range(NT):
                x_plus_acc(1, i)

        @block.scalar
        def _(act):
            def hi(key, dst_, src_):
                completed(act, key)
                act_his.append(key)
                act.activation(dst_, src_, ACT.Copy).then_inc(hi_done, 1)

            def ln_sqrt(s, i):
                n = lnno[(s, i)]
                st = LNS[n % 2]
                act.wait_ge(ln_var, n + 1)
                act.activation(st[:, 9:10], st[:, 8:9], ACT.Sqrt).then_inc(ln_std, 1)

            def ln_T_hi(s, i, T):
                key = ("xt", s, i)
                hi(key, T.hi[:, :, i * TILE:(i + 1) * TILE],
                   bank(key)[:, 0:FB * TILE].rearrange("p (b n) -> p b n", b=FB))

            def work_hi(key):
                if key[0] == "wt":
                    _, w, ib = key
                    hi(key, {"k": WA, "2": W2T, "q": WB}[w].hi[:, ib, :], bank(key))
                elif key[0] == "mi":
                    b = key[1]
                    act.wait_ge(mi_sum, b + 1)
                    act.activation(MI.hi[:, b, :], MI.lo32[:, b, :], ACT.Copy).then_inc(mi_hi, 1)
                elif key[0] == "g":
                    hi(key, G.hi[:, key[1], :], bank(key))

            ln_sqrt(0, 0)
            for i in range(NT + 1):
                if i + 1 < NT:
                    ln_sqrt(0, i + 1)
                if i < NT:
                    act.wait_ge(ln_xnf, i + 1)
                    act.activation(xn.hi[:, i, :], xnf[i % 2][:], ACT.Copy).then_inc(ln_hi, 1)
                if i >= 1:
                    ln_T_hi(0, i - 1, xnT)
                    for key in work_after(i - 1):
                        work_hi(key)

            def k_exp(b):
                act.wait_ge(k_max, b + 1)
                if b >= 2:
                    completed(act, ("kt", b - 2, 2))
                o_ = 8 * (b % 2)
                for c, (o, w) in enumerate(CH):
                    drain(act.activation(kT[b % 2][:, o:o + w], bank(("k", b, c))[:, 0:w], ACT.Exp,
                                         bias=cols[:, o_ + 3:o_ + 4],
                                         accum_out=cols[:, o_ + 4 + c:o_ + 5 + c]), ("k", b, c))

            k_exp(0)
            for b in range(FB + 1):
                if b + 1 < FB:
                    k_exp(b + 1)
                if b < FB:
                    for q in range(3):
                        n = min(4, NT - 4 * q)
                        key = ("kt", b, q)
                        hi(key, ek.hi[:, 4 * q:4 * q + n, :],
                           bank(key)[0:TILE, 0:128 * n].rearrange("p (t d) -> p t d", t=n))
                    if b > 0:
                        completed(act, ("c1t", b - 1))
                    completed(act, ("c1", b))
                    drain(act.activation(c1f[:], bank(("c1", b)), ACT.Copy), ("c1", b))
                    hi(("c1t", b), c1[b % 2].hi[:], bank(("c1t", b)).rearrange("p (c d) -> p c d", c=FB))
                if b > 0:
                    carried(act, ("cx", b - 1))
                    act.activation(ctxp.hi[:, b - 1, :], cxt[:], ACT.Copy).then_inc(cx_hi, 1)

            def q_exp(i):
                act.wait_ge(q_max, i + 1)
                if i >= 2:
                    completed(act, ("qt", i - 2))
                c = 16 + 4 * (i % 2)
                drain(act.activation(qe[i % 2][:], bank(("q", i))[0:TILE, :], ACT.Exp,
                                     bias=cols[0:TILE, c:c + 1], accum_out=cols[0:TILE, c + 1:c + 2]), ("q", i))

            q_exp(0)
            for i in range(NT):
                if i + 1 < NT:
                    q_exp(i + 1)
                for key in torch_after(i):
                    _, name, ib = key
                    n = names.index(name)
                    completed(act, key)
                    if n >= 2 and ib == 0:
                        act.wait_ge(wt_out[n % 2], 16 * (n // 2))
                    drain(act.activation(wout[n % 2][:, ib, :], bank(key), ACT.Copy), key)
                if i >= 2:
                    completed(act, ("mo", i - 2))
                hi(("qt", i), qT[i % 2].hi[:], bank(("qt", i))[:, 0:FB * TILE].rearrange("p (b n) -> p b n", b=FB))
            act.wait_ge(wt_out[0], 16 * 3)
            act.wait_ge(edge_ready, 1)
            fit = act.value_load(flags[0:1, 20:21], min_val=0, max_val=1)

            def onehot_dst(g, r, square, ready):
                for t in range(GT):
                    ins = act.activation(ohd[r][:, t, :], iotaw[:], ACT.Square, bias=rel[:, bass.ds(g * GT + t, 1)])
                ins.then_inc(square, 1)
                act.wait_ge(square, g + 1)
                act.activation(ohd[r][:], ohd[r][:], ACT.Relu, bias=1.0, scale=-1.0).then_inc(ready, 1)

            with act.If(fit == 1):
                with act.Fori(0, GROUPS // 2) as k:
                    for r in range(2):
                        act.wait_ge(edge_tiles, k * (2 * GT) + (r * GT + PRIME - GT))
                        onehot_dst(k * 2 + r, r, dst_squared, dst_ready)
                act.wait_ge(edge_tiles, (GROUPS - 1) * GT + PRIME - GT)
                onehot_dst(GROUPS - 1, 0, dst_squared, dst_ready)
            with act.Else():
                with act.Fori(0, NT) as w:
                    act.activation(rel[:], dstF[:], ACT.Identity, bias=bW[:, bass.ds(w, 1)], scale=-1.0)\
                        .then_inc(all_rel, 1)
                    act.wait_ge(all_rel, w + 1)
                    with act.Fori(0, GROUPS) as g:
                        act.wait_ge(all_tiles, w * (GROUPS * GT) + g * GT + 1)
                        for t in range(GT):
                            ins = act.activation(ohd[0][:, t, :], iotaw[:], ACT.Square,
                                                 bias=rel[:, bass.ds(g * GT + t, 1)])
                        ins.then_inc(all_squared, 1)
                        act.wait_ge(all_squared, w * GROUPS + g + 1)
                        act.activation(ohd[0][:], ohd[0][:], ACT.Relu, bias=1.0, scale=-1.0).then_inc(all_dst, 1)
            act.wait_ge(deg_ready, 1)
            act.activation(dinc[:], dinc[:], ACT.Sqrt).then_inc(deg_root, 1)

            for i in range(NT):
                hi(("y1", i), y.hi[:, i, :], bank(("y1", i))[0:TILE, :])
            act.wait_ge(deg_ready, 2)
            act.activation(CNTB[:], CNTB[:], ACT.Sqrt).then_inc(deg_root, 1)
            completed(act, ("ix",))
            for f in range(FB):
                for c, (o, w) in enumerate(CH):
                    key = ("r1", f, c)
                    completed(act, key)
                    drain(act.activation(hT.lo32[:, f, o:o + w], bank(key)[:, 0:w], ACT.Identity,
                                         bias=ccol[:, COL["bl1"] + f:COL["bl1"] + f + 1]), key)
            n = 0
            for f in range(FB):
                for c, (o, w) in enumerate(CH):
                    n += 1
                    act.wait_ge(a1_sum, n)
                    act.activation(hT.hi[:, f, o:o + w], hT.lo32[:, f, o:o + w], ACT.Relu).then_inc(a1_hi, 1)
            for i in range(NT):
                hi(("y2", i), y.hi[:, i, :], bank(("y2", i))[0:TILE, :])
            ln_sqrt(1, 0)
            for i in range(NT):
                if i + 1 < NT:
                    ln_sqrt(1, i + 1)
                ln_T_hi(1, i, xnT)
            def gate_exp(s):
                act.wait_ge(lg_less, s + 1)
                act.activation(ex[s][:], lgt[s][:], ACT.Exp).then_inc(lg_exp, 1)

            def acc_starts(s):
                for c, (o, w) in enumerate(CH):
                    hi(("gt", s, c), gT[s].hi[:, o:o + w], bank(("gt", s, c))[0:E, 0:w])
                for i in range(NT):
                    key = ("ac", s, i)
                    completed(act, key)
                    drain(act.activation(acc[:, i, :], bank(key)[0:TILE, :], ACT.Copy), key)

            def hidden(s, e, e_, later, func):
                act.wait_ge(bias_placed, e_ + (E * s + 1))
                for f in range(2):
                    if f == 1 and e == 0:
                        gate_exp(s)
                    for c, (o, w) in enumerate(CH):
                        key = ("hd", s, e, f, c)
                        completed(act, key, later)
                        b_ = BIAS + 2 * (e % 2) + f
                        drain(act.activation(hE[e % 2].lo32[:, f, o:o + w], bank(key)[:, 0:w], func,
                                             bias=cols[:, b_:b_ + 1]), key)

            def hiddens(s, func):
                hidden(s, 0, 0, 0, func)
                acc_starts(s)
                with act.Fori(0, PAIRS) as k:
                    hidden(s, 1, k * 2 + 1, k * 4, func)
                    hidden(s, 2, k * 2 + 2, k * 4, func)
                hidden(s, 7, 7, 0, func)

            hiddens(0, ACT.Relu)
            ln_sqrt(2, 0)
            for i in range(NT + 1):
                if i + 1 < NT:
                    ln_sqrt(2, i + 1)
                if i < NT:
                    act.wait_ge(ln_xnf, lnno[(2, i)] + 1)
                    act.activation(xn2.hi[:, i, :], xnm[i % 2][:], ACT.Copy).then_inc(ln_hi, 1)
                if i >= 1:
                    ln_T_hi(2, i - 1, xnT)
            for i in range(NT):
                act.wait_ge(k_min, i + 1)
                act.activation(kx[i % 3][:], kx[i % 3][:], ACT.Exp).then_inc(k_exped, 1)
                carried(act, ("k2", i))
                if i >= 2:
                    act.wait_ge(k_used, i - 1)
                act.activation(kp[i % 2].hi[:], kx[i % 3][:], ACT.Copy).then_inc(k_hi, 1)
            for b in range(FB):
                hi(("kv", b), kv.hi[:, b, :], bank(("kv", b)))
            hi(("ks",), ksum.hi[:], bank(("ks",))[:, 0:2 * FB].rearrange("p (b a) -> p b a", b=FB))

            def q_exps(g, f):
                act.wait_ge(q_min, g * FB + f + 1)
                q_ = q2[g % 2].lo32[:, f, :]
                act.activation(q_, q_, ACT.Exp).then_inc(q_exped, 1)

            def q_his(g, f):
                carried(act, ("q2", g, f))
                act.activation(q2[g % 2].hi[:, f, :], q2[g % 2].lo32[:, f, :], ACT.Copy).then_inc(q_hi, 1)

            for g in range(NQ):
                for f in range(FB + 1):
                    if f < FB:
                        q_exps(g, f)
                    if f > 0:
                        q_his(g, f - 1)
                for i in (2 * g, 2 * g + 1):
                    act.wait_ge(xs_scaled, i + 1)
                    act.activation(xn2.hi[:, i, :], xn2.lo32[:, i, :], ACT.Copy).then_inc(xs_hi, 1)
            for n, (f, c) in enumerate(HX):
                o, w = CH[c]
                carried(act, ("z", f, c))
                act.activation(zT.hi[:, f, o:o + w], zT.lo32[:, f, o:o + w], ACT.Copy).then_inc(z_hi, 1)
            x_stored(act, ("xq", NT - 2))
            x_stored(act, ("xq", NT - 1))
            for hf in range(2):
                for f, c in HX:
                    o, w = CH[c]
                    key = ("h1", hf, f, c)
                    completed(act, key)
                    b_ = COL["gb1"] + FB * hf + f
                    drain(act.activation(h1T.lo32[:, f, o:o + w], bank(key)[:, 0:w], ACT.Relu,
                                         bias=ccol[:, b_:b_ + 1]), key)
                    carried(act, key)
                    act.activation(h1T.hi[:, f, o:o + w], h1T.lo32[:, f, o:o + w], ACT.Copy).then_inc(h1_hi, 1)
                for i in range(NT):
                    key = ("yy", hf, i)
                    if hf == 0:
                        completed(act, key)
                        drain(act.activation(y3.lo32[:, i, :], bank(key)[0:TILE, :], ACT.Copy,
                                             scale=dinc[:, i:i + 1]), key)
                    else:
                        carried(act, key)
                        act.activation(y3.hi[:, i, :], y3.lo32[:, i, :], ACT.Copy).then_inc(y3_hi, 1)

            def gained(i):
                key = ("xt", 4, i)
                completed(act, key)
                sl = slice(i * TILE, (i + 1) * TILE)
                for b in range(FB):
                    g_, b_ = COL["ln_g"] + b, COL["ln_b"] + b
                    ins = act.activation(hxT.lo32[:, b, sl], bank(key)[:, b * TILE:(b + 1) * TILE], ACT.Identity,
                                         bias=ccol[:, b_:b_ + 1], scale=ccol[:, g_:g_ + 1])
                drain(ins, key)
                carried(act, key)
                act.activation(hxT.hi[:, :, sl], hxT.lo32[:, :, sl], ACT.Copy).then_inc(hx_hi, 1)

            def v_out(i):
                completed(act, ("pv", i))
                drain(act.activation(V32[:, i, :], bank(("pv", i))[0:TILE, :], ACT.Copy), ("pv", i))

            for i in range(NT):
                ln_sqrt(3, i)
                ln_sqrt(4, i)
                if i >= 2:
                    gained(i - 2)
                if i >= 3:
                    v_out(i - 3)
            gained(NT - 2)
            v_out(NT - 3)
            gained(NT - 1)
            v_out(NT - 2)
            v_out(NT - 1)
            def squares(s, w, i):
                completed(act, ("p" + w, i))
                if i >= 2 or s:
                    act.wait_ge(unit_sum, NT * s + i - 1)
                act.activation(sqr[i % 2][:], bank(("p" + w, i))[0:TILE, :], ACT.Square).then_inc(squared, 1)

            def roots(s, i):
                c = 8 * (i % 2)
                act.wait_ge(unit_sum, NT * s + i + 1)
                act.activation(cols[0:TILE, 16 + c:24 + c], cols[0:TILE, c:c + 8], ACT.Sqrt).then_inc(unit_root, 1)

            even, odd = slice(0, HEADS, 2), slice(1, HEADS, 2)
            up, down = slice(0, DH), slice(DH, 2 * DH)

            def transposed(w, i):
                return bank(("t" + w, i))[:, 0:FB * TILE].rearrange("p (b n) -> p b n", b=FB)

            for s, (w, dst_, gain) in enumerate((("q", QA, "qn_g"), ("k", KA, "kn_g"))):
                g_ = ccol[:, COL[gain]:COL[gain] + 1]
                squares(s, w, 0)
                roots(s, 0)
                for i in range(NT):
                    if i + 1 < NT:
                        squares(s, w, i + 1)
                        roots(s, i + 1)
                    key = ("t" + w, i)
                    sl = slice(i * TILE, (i + 1) * TILE)
                    completed(act, key)
                    t_ = transposed(w, i)
                    act.activation(dst_[up, even, sl], t_[up], ACT.Copy, scale=g_[up])
                    act_his.append(key)
                    act.activation(dst_[down, odd, sl], t_[down], ACT.Copy, scale=g_[down]).then_inc(hi_done, 1)
                    if w == "k":
                        act.wait_ge(hi_done, len(act_his))
                        act.activation(KA[down, even, sl], KA32[up, even, sl], ACT.Copy)
                        act.activation(KA[up, odd, sl], KA32[down, odd, sl], ACT.Copy).then_inc(k_twice, 1)

            def used_by_v(eng, g):
                b, c, a, j = STEPS[g]
                if j == last_key(c):
                    completed(eng, ("ov", b, c, a))
                else:
                    eng.wait_ge(pt_used, sum(st[3] < last_key(st[1]) for st in STEPS[:g + 1]))

            CHUNKS = [(b, c) for b in range(FB) for c in range(3)]

            def out_hi(n):
                b, c = CHUNKS[n]
                o, w = CH[c]
                act.wait_ge(ot_whole, n + 1)
                act.activation(OT[:, b, 0, o:o + w], OT32[:, b, o:o + w], ACT.Copy).then_inc(ot_hi, 1)

            for g, (b, c, a, j) in enumerate(STEPS):
                key = ("sT", g)
                off, w = valid(c, j)
                completed(act, key)
                if g >= NP:
                    act.wait_ge(p_ready, g - NP + 1)
                    act.wait_ge(p_added, g - NP + 1)
                drain(act.activation(P[g % NP][:, off:w], bank(key)[0:TILE, off:w], ACT.Exp), key)
                carried(act, key)
                if g >= NPT:
                    used_by_v(act, g - NPT)
                act.activation(PT[g % NPT].hi[:, off:w], P[g % NP][:, off:w], ACT.Copy).then_inc(p_hi, 1)
                if (b, c) != (0, 0) and (a, j) == (1, 1):
                    out_hi(3 * b + c - 1)
            out_hi(len(CHUNKS) - 1)
            for f, c in WO:
                o, w = CH[c]
                hi(("wo", f, c), yT.hi[:, f, o:o + w], bank(("wo", f, c))[:, 0:w])
            hiddens(1, ACT.Gelu_apprx_tanh)

        @block.vector
        def _(dve):
            steps = [0]

            def link(ins):
                steps[0] += 1
                ins.then_inc(dve_step, 1)
                dve.wait_ge(dve_step, steps[0])

            def lo(key, dst_, src_, hi_):
                dve_los.append(key)
                dve.wait_ge(hi_done, len(dve_los))
                drain(dve.tensor_tensor(dst_, src_, hi_, ALU.subtract), key)

            def ln_stats(s, i, x_):
                n = lnno[(s, i)]
                st = LNS[n % 2]
                if n >= 2:
                    dve.wait_ge(ln_xnf, n - 1)
                link(dve.bn_stats(st[:, 0:6], x_))
                link(dve.bn_aggr(st[:, 6:8], st[:, 0:6]))
                dve.tensor_scalar(st[:, 8:9], st[:, 7:8], EPS, None, ALU.add).then_inc(ln_var, 1)

            def ln_norm(s, i, x_, xnf_):
                n = lnno[(s, i)]
                st = LNS[n % 2]
                dve.wait_ge(ln_std, n + 1)
                link(dve.reciprocal(st[:, 10:11], st[:, 9:10]))
                dve.tensor_scalar(xnf_, x_, st[:, 6:7], st[:, 10:11], ALU.subtract, ALU.mult).then_inc(ln_xnf, 1)

            def ln_T_lo(s, i, T):
                key = ("xt", s, i)
                sl = slice(i * TILE, (i + 1) * TILE)
                lo(key, T.lo[:, :, sl], bank(key)[:, 0:FB * TILE].rearrange("p (b n) -> p b n", b=FB), T.hi32[:, :, sl])

            def work_lo(key):
                if key[0] == "wt":
                    _, w, ib = key
                    W = {"k": WA, "2": W2T, "q": WB}[w]
                    lo(key, W.lo[:, ib, :], bank(key), W.hi32[:, ib, :])
                elif key[0] == "vec":
                    completed(dve, key)
                    drain(dve.tensor_copy(ccol[:, 0:54], bank(key)[:, 0:54]), key)
                elif key[0] == "mi":
                    b = key[1]
                    completed(dve, key)
                    drain(dve.tensor_copy(MI.lo32[:, b, :], bank(key)), key)
                    carried(dve, key)
                    sl = slice(b * 128, (b + 1) * 128)
                    dve.tensor_tensor(MI.lo32[:, b, sl], MI.lo32[:, b, sl], ident[:], ALU.add).then_inc(mi_sum, 1)
                    dve.wait_ge(mi_hi, b + 1)
                    dve.tensor_tensor(MI.lo[:, b, :], MI.lo32[:, b, :], MI.hi32[:, b, :], ALU.subtract)\
                        .then_inc(mi_ready, 1)
                else:
                    lo(key, G.lo[:, key[1], :], bank(key), G.hi32[:, key[1], :])

            x_landed(dve, ("x", 0))
            ln_stats(0, 0, xt_[0][:])
            for i in range(NT + 1):
                if i + 1 < NT:
                    x_landed(dve, ("x", i + 1))
                    ln_stats(0, i + 1, xt_[(i + 1) % 2][:])
                if i < NT:
                    if i >= 2:
                        completed(dve, ("xt", 0, i - 2))
                        dve.wait_ge(ln_lo, i - 1)
                    ln_norm(0, i, xt_[i % 2][:], xnf[i % 2][:])
                    dve.wait_ge(ln_hi, i + 1)
                    dve.tensor_tensor(xn.lo[:, i, :], xnf[i % 2][:], xn.hi32[:, i, :], ALU.subtract)\
                        .then_inc(ln_lo, 1)
                if i >= 1:
                    ln_T_lo(0, i - 1, xnT)
                    for key in work_after(i - 1):
                        work_lo(key)

            def k_maxs(b):
                o_ = 8 * (b % 2)
                for c, (o, w) in enumerate(CH):
                    completed(dve, ("k", b, c))
                    link(dve.tensor_reduce(cols[:, o_ + c:o_ + c + 1], bank(("k", b, c))[:, 0:w], AX_X, ALU.max))
                dve.tensor_reduce(cols[:, o_ + 3:o_ + 4], cols[:, o_:o_ + 3], AX_X, ALU.max,
                                  negate=True).then_inc(k_max, 1)

            k_maxs(0)
            for b in range(FB + 1):
                if b + 1 < FB:
                    k_maxs(b + 1)
                if b < FB:
                    for q in range(3):
                        n = min(4, NT - 4 * q)
                        key = ("kt", b, q)
                        lo(key, ek.lo[:, 4 * q:4 * q + n, :],
                           bank(key)[0:TILE, 0:128 * n].rearrange("p (t d) -> p t d", t=n),
                           ek.hi32[:, 4 * q:4 * q + n, :])
                    o_ = 8 * (b % 2)
                    for c in range(3):
                        carried(dve, ("k", b, c))
                    link(dve.tensor_reduce(cols[:, 24 + b:25 + b], cols[:, o_ + 4:o_ + 7], AX_X, ALU.add))
                    link(dve.reciprocal(cols[:, 28 + b:29 + b], cols[:, 24 + b:25 + b]))
                    lo(("c1t", b), c1[b % 2].lo[:], bank(("c1t", b)).rearrange("p (c d) -> p c d", c=FB),
                       c1[b % 2].hi32[:])
                if b > 0:
                    key = ("cx", b - 1)
                    completed(dve, key)
                    if b > 1:
                        dve.wait_ge(cx_ready, b - 1)
                    drain(dve.tensor_scalar(cxt[:], bank(key), cols[:, 27 + b:28 + b], float(D) ** -0.5,
                                            ALU.mult, ALU.mult), key)
                    dve.wait_ge(cx_hi, b)
                    dve.tensor_tensor(ctxp.lo[:, b - 1, :], cxt[:], ctxp.hi32[:, b - 1, :], ALU.subtract)\
                        .then_inc(cx_ready, 1)

            def q_maxs(i):
                completed(dve, ("q", i))
                c = 16 + 4 * (i % 2)
                dve.tensor_reduce(cols[0:TILE, c:c + 1], bank(("q", i))[0:TILE, :], AX_X, ALU.max,
                                  negate=True).then_inc(q_max, 1)

            def q_norms(i):
                carried(dve, ("q", i))
                c = 16 + 4 * (i % 2)
                link(dve.reciprocal(cols[0:TILE, c + 2:c + 3], cols[0:TILE, c + 1:c + 2]))
                dve.tensor_scalar(qe[i % 2][:], qe[i % 2][:], cols[0:TILE, c + 2:c + 3], None,
                                  ALU.mult).then_inc(q_norm, 1)

            def edge_rows():
                dve.wait_ge(idx_in, 48)
                dve.tensor_copy(srcR[:], srcI[:]).then_inc(idx_f, 1)
                dve.tensor_copy(dstR[:], dstI[:]).then_inc(idx_f, 1)
                link(dve.tensor_copy(grpR[:], grpI[:]))
                link(dve.tensor_reduce(gst[:, 0:1], grpR[:], AX_X, ALU.min))
                link(dve.tensor_reduce(gst[:, 1:2], grpR[:], AX_X, ALU.max))
                for a in range(2):
                    dve.tensor_scalar(gD[:, a * GROUPS:(a + 1) * GROUPS], ident[0:GROUPS, 0:GROUPS], gst[:, a:a + 1],
                                      None, ALU.mult).then_inc(idx_f, 1)

            def edge_windows():
                completed(dve, ("ix",))
                link(dve.tensor_copy(srcF[:], bank(("ix",))[0:TILE, 0:170]))
                drain(dve.tensor_copy(dstF[:], bank(("ix",))[0:TILE, 170:340]), ("ix",))
                completed(dve, ("wv",))
                drain(dve.tensor_copy(rows[:, 0:2 * GROUPS], bank(("wv",))[0:TILE, 0:2 * GROUPS]), ("wv",))
                carried(dve, ("wv",))
                least, most, r2 = rows[:, 0:GROUPS], rows[:, GROUPS:2 * GROUPS], 2 * GROUPS
                link(dve.tensor_scalar(wB[:, 0:GROUPS], least, float(LASTWIN), None, ALU.min))
                link(dve.tensor_copy(flags[0:1, 0:GROUPS], wB[0:1, 0:GROUPS]))
                link(dve.tensor_tensor(rows[:, r2:r2 + GROUPS], most, wB[:, 0:GROUPS], ALU.subtract))
                link(dve.tensor_scalar(rows[:, r2:r2 + GROUPS], rows[:, r2:r2 + GROUPS], float(WIN - 1), None,
                                       ALU.subtract))
                link(dve.tensor_tensor(rows[:, 3 * GROUPS:4 * GROUPS - 1], most[:, 0:GROUPS - 1], least[:, 1:GROUPS],
                                       ALU.subtract))
                link(dve.tensor_scalar(rows[:, 4 * GROUPS - 1:4 * GROUPS], ones2[0:TILE, 0:1], -1.0, None, ALU.mult))
                link(dve.tensor_reduce(rows[:, 4 * GROUPS:4 * GROUPS + 1], rows[:, r2:4 * GROUPS], AX_X, ALU.max))
                link(dve.tensor_tensor(rows[:, r2:r2 + GROUPS - FEW], most[:, 0:GROUPS - FEW], least[:, FEW:GROUPS],
                                       ALU.subtract))
                link(dve.tensor_scalar(rows[:, r2:r2 + GROUPS - FEW], rows[:, r2:r2 + GROUPS - FEW], 1.0, None, ALU.add))
                link(dve.tensor_reduce(rows[:, 4 * GROUPS + 1:4 * GROUPS + 2], rows[:, r2:r2 + GROUPS - FEW], AX_X,
                                       ALU.max))
                link(dve.tensor_reduce(wB[:, 20:21], rows[:, 4 * GROUPS:4 * GROUPS + 2], AX_X, ALU.max))
                link(dve.tensor_scalar(flags[0:1, 20:21], wB[0:1, 20:21], 0.0, None, ALU.is_le))
                dve.tensor_tensor(rel[:].rearrange("p (g t) -> p g t", g=GROUPS),
                                  wB[:, 0:GROUPS].rearrange("p (g a) -> p g a", a=1).broadcast_to((TILE, GROUPS, GT)),
                                  dstF[:].rearrange("p (g t) -> p g t", g=GROUPS),
                                  ALU.subtract).then_inc(edge_ready, 1)

            q_maxs(0)
            q_norms(0)
            dve.wait_ge(bl2_in, 16)
            for i in range(NT):
                if i + 1 < NT:
                    q_maxs(i + 1)
                lo(("qt", i), qT[i % 2].lo[:], bank(("qt", i))[:, 0:FB * TILE].rearrange("p (b n) -> p b n", b=FB),
                   qT[i % 2].hi32[:])
                if i + 1 < NT:
                    q_norms(i + 1)
                x_landed(dve, ("xmix", i))
                xr = xt_[i % 2]
                link(dve.tensor_tensor(xr[:], xr[:], bl2B[:], ALU.add))
                completed(dve, ("mo", i))
                drain(dve.tensor_tensor(xr[:], xr[:], bank(("mo", i))[0:TILE, :], ALU.add), ("mo", i))
                if i == PREP - 1:
                    edge_rows()
                if i == PREP + 1:
                    edge_windows()

            dve.wait_ge(wt_out[0], 16 * 3)
            dve.wait_ge(edge_ready, 1)
            dve.wait_ge(const_ready, 2)
            link(dve.tensor_copy(onesR[:], onesA[:]))
            dve.memset(cols[:, 39:40], 0.0).then_inc(edge_tiles, PRIME)
            dve.memset(cols[:, 38:39], 0.0).then_inc(window_free, 2)
            dve.memset(cols[:, 37:38], 0.0).then_inc(all_tiles, 1)
            dve.memset(cols[:, 36:37], 0.0).then_inc(all_taken, 1)
            fit = dve.value_load(flags[0:1, 20:21], min_val=0, max_val=1)

            def onehot_src(t, r):
                return dve.tensor_scalar(ohs[r][:], iota[:], srcF[:, bass.ds(t, 1)], None, ALU.is_equal)

            def group_onehots(g, odd):
                for t in range(GT):
                    dve.wait_ge(edge_tiles, g * GT + (t + 1 - NOH + PRIME))
                    onehot_src(g * GT + t, (odd * GT + t) % NOH).then_inc(src_ready, 1)

            def window(g):
                return dve.value_load(flags[0:1, bass.ds(g, 1)], min_val=0, max_val=LASTWIN)

            def add_group(g, half, w):
                dve.wait_ge(edge_tiles, g * GT + (GT + PRIME))
                a = AT[:, :, bass.ds(w, WIN)]
                a_was = AT[:, :, bass.ds(w, WIN)].bitcast(F32)
                ps = PS[0:TILE, 3 * half:3 * half + 3, :].rearrange("p b (j w) -> p (b j) w", w=WIN)[:, 0:NT, :]
                dve.wait_ge(window_free, g + 2)
                dve.wait_ge(at_zero, 2)
                dve.tensor_tensor(a, a_was, ps, ALU.add).then_inc(window_free, 1)

            with dve.If(fit == 1):
                group_onehots(0, 0)
                with dve.Fori(0, GROUPS // 2) as k:
                    w = window(k * 2)
                    group_onehots(k * 2 + 1, 1)
                    add_group(k * 2, 0, w)
                    w = window(k * 2 + 1)
                    group_onehots(k * 2 + 2, 0)
                    add_group(k * 2 + 1, 1, w)
                add_group(GROUPS - 1, 0, window(GROUPS - 1))
                dve.wait_ge(window_free, GROUPS + 2)
            with dve.Else():
                dve.wait_ge(at_zero, 2)
                with dve.Fori(0, NT - 1) as w:
                    with dve.Fori(0, GROUPS) as g:
                        for t in range(GT):
                            dve.wait_ge(all_tiles, w * (GROUPS * GT) + g * GT + (t + 1))
                            onehot_src(g * GT + t, 0).then_inc(all_src, 1)
                    dve.wait_ge(all_tiles, w * (GROUPS * GT) + (GROUPS * GT + 1))
                    dve.tensor_copy(AT32[:, :, bass.ds(w * WIN, WIN)],
                                    PS[0:TILE, 0:3, :].rearrange("p b (j w) -> p (b j) w", w=WIN)[:, 0:NT, :])\
                        .then_inc(all_taken, 1)
                with dve.Fori(0, GROUPS) as g:
                    for t in range(GT):
                        dve.wait_ge(all_tiles, g * GT + (t + 1 + (NT - 1) * GROUPS * GT))
                        onehot_src(g * GT + t, 0).then_inc(all_src, 1)
                dve.wait_ge(all_tiles, NT * GROUPS * GT + 1)
                dve.wait_ge(all_taken, NT)
                dve.tensor_copy(AT32[:, :, LASTWIN:N],
                                PS[0:TILE, 0:3, :].rearrange("p b (j w) -> p (b j) w", w=WIN)[:, 0:NT, :])\
                    .then_inc(all_taken, 1)
            for c, (o, w) in enumerate(CH):
                completed(dve, ("cb", c))
                drain(dve.tensor_copy(CNTB[:, o:o + w], bank(("cb", c))[:, 0:w]), ("cb", c))
            completed(dve, ("cc",))
            cc = bank(("cc",))[0:TILE, 0:NT]
            link(dve.tensor_scalar(dinc[:], cc, 1.0, None, ALU.add))
            drain(dve.tensor_scalar(invc[:], cc, 1.0, None, ALU.max), ("cc",))
            carried(dve, ("cc",))
            link(dve.reciprocal(invc[:], invc[:]))
            dve.reciprocal(dinc[:], dinc[:]).then_inc(deg_ready, 1)
            link(dve.tensor_scalar(inv0[:], CNTB[:], 1.0, None, ALU.max))
            dve.reciprocal(inv0[:], inv0[:]).then_inc(inv_ready, 1)
            link(dve.tensor_scalar(CNTB[:], CNTB[:], 1.0, None, ALU.add))
            dve.reciprocal(CNTB[:], CNTB[:]).then_inc(deg_ready, 1)
            for i in range(NT):
                lo(("y1", i), y.lo[:, i, :], bank(("y1", i))[0:TILE, :], y.hi32[:, i, :])
            completed(dve, ("r1", FB - 1, 2))
            dve.wait_ge(inv_ready, 1)
            dve.tensor_copy(INVB[:], inv0[:]).then_inc(inv_placed, 1)
            dve.wait_ge(inv_placed, 1)
            n = 0
            for f in range(FB):
                for c, (o, w) in enumerate(CH):
                    key = ("a1", f, c)
                    n += 1
                    t = sc[n % 2][:, 0:w]
                    completed(dve, key)
                    drain(dve.tensor_tensor(t, bank(key)[:, 0:w], INVB[:, o:o + w], ALU.mult), key)
                    carried(dve, key)
                    carried(dve, ("r1", f, c))
                    R = hT.lo32[:, f, o:o + w]
                    dve.tensor_tensor(R, R, t, ALU.add).then_inc(a1_sum, 1)
                    dve.wait_ge(a1_hi, n)
                    dve.scalar_tensor_tensor(out=hT.lo[:, f, o:o + w], in0=R, scalar=0.0,
                                             in1=hT.hi32[:, f, o:o + w], op0=ALU.max, op1=ALU.subtract)\
                        .then_inc(a1_ready, 1)
            for i in range(NT):
                lo(("y2", i), y.lo[:, i, :], bank(("y2", i))[0:TILE, :], y.hi32[:, i, :])
            for i in range(NT):
                x_landed(dve, ("xr2", i))
                completed(dve, ("r2", i))
                drain(dve.tensor_tensor(xw[i % WIDE][:], xw[i % WIDE][:], bank(("r2", i))[0:TILE, :], ALU.add), ("r2", i))

            def a2_x(i):
                x_landed(dve, ("xa2", i))
                completed(dve, ("a2", i))
                drain(dve.scalar_tensor_tensor(out=xw[i % WIDE][:], in0=bank(("a2", i))[0:TILE, :],
                                               scalar=invc[:, i:i + 1], in1=xw[i % WIDE][:],
                                               op0=ALU.mult, op1=ALU.add), ("a2", i))
                carried(dve, ("a2", i))
                ln_stats(1, i, xw[i % WIDE][:])

            a2_x(0)
            for i in range(NT):
                if i >= 2:
                    completed(dve, ("xt", 1, i - 2))
                ln_norm(1, i, xw[i % WIDE][:], xnw[i % 2][:])
                if i + 1 < NT:
                    a2_x(i + 1)
                ln_T_lo(1, i, xnT)
            def over(a):
                return a.rearrange("p (t a) -> p t a", a=1).broadcast_to((TILE, NT, E))

            def logits_less_max(s):
                bias_to_place(s, 0, 0)
                bias_to_place(s, 1, 1)
                for c, (o, w) in enumerate(CH):
                    key = ("lt", s, c)
                    completed(dve, key)
                    drain(dve.tensor_copy(gT[s].lo32[:, o:o + w], bank(key)[0:E, 0:w]), key)
                dve.wait_ge(moe_in[s], 48)
                key = ("lg", s)
                completed(dve, key)
                bg_ = bgB[s][:].rearrange("p (a e) -> p a e", a=1).broadcast_to((TILE, NT, E))
                drain(dve.tensor_tensor(lgt[s][:], bank(key)[0:TILE, 0:NT * E].rearrange("p (t e) -> p t e", t=NT),
                                        bg_, ALU.add), key)
                carried(dve, key)
                link(dve.tensor_reduce(gred[s][:, 0, :], lgt[s][:], AX_X, ALU.max))
                dve.tensor_tensor(lgt[s][:], lgt[s][:], over(gred[s][:, 0, :]), ALU.subtract).then_inc(lg_less, 1)

            def softmax_scale(s):
                dve.wait_ge(lg_exp, s + 1)
                link(dve.tensor_reduce(gred[s][:, 1, :], ex[s][:], AX_X, ALU.add))
                link(dve.reciprocal(gred[s][:, 2, :], gred[s][:, 1, :]))

            def gate_transposed(s):
                for c, (o, w) in enumerate(CH):
                    key = ("gt", s, c)
                    lo(key, gT[s].lo[:, o:o + w], bank(key)[0:E, 0:w], gT[s].hi32[:, o:o + w])

            def bias_to_place(s, e, e_):
                c, b_ = COL[f"m{s}b1"], BIAS + 2 * (e % 2)
                dve.tensor_scalar(cols[:, b_:b_ + 2], ccol[:, bass.ds(e_ * 2 + c, 2)], 1.0, None, ALU.mult)\
                    .then_inc(bias_placed, 1)

            def hidden_parts(s, e, e_, later):
                h = hE[e % 2]
                for n, (f, c) in enumerate([(f, c) for f in range(2) for c in range(3)]):
                    o, w = CH[c]
                    carried(dve, ("hd", s, e, f, c), later)
                    dve.tensor_copy(h.hi[:, f, o:o + w], h.lo32[:, f, o:o + w]).then_inc(hid_hi, 1)
                    dve.wait_ge(hid_hi, e_ * 6 + (48 * s + n + 1))
                    dve.tensor_tensor(h.lo[:, f, o:o + w], h.lo32[:, f, o:o + w], h.hi32[:, f, o:o + w],
                                      ALU.subtract).then_inc(hid_ready, 1)

            def expert_added(s, e, e_, later, i):
                key = ("eo", s, e, i)
                completed(dve, key, later)
                drain(dve.scalar_tensor_tensor(out=acc[:, i, :], in0=bank(key)[0:TILE, :],
                                               scalar=gate[:, i, bass.ds(e_, 1)], in1=acc[:, i, :],
                                               op0=ALU.mult, op1=ALU.add), key)

            def experts_added(s):
                hidden_parts(s, 0, 0, 0)
                gate_transposed(s)
                with dve.Fori(0, PAIRS) as k:
                    bias_to_place(s, 2, k * 2 + 2)
                    hidden_parts(s, 1, k * 2 + 1, k * 4)
                    for i in range(NT):
                        expert_added(s, 0, k * 2, k * 4, i)
                    bias_to_place(s, 3, k * 2 + 3)
                    hidden_parts(s, 2, k * 2 + 2, k * 4)
                    for i in range(NT):
                        expert_added(s, 1, k * 2 + 1, k * 4, i)
                hidden_parts(s, 7, 7, 0)
                for i in range(NT):
                    expert_added(s, 6, 6, 0, i)

            logits_less_max(0)
            softmax_scale(0)
            link(dve.tensor_scalar(cand[:], lgt[0][:], 0.0, None, ALU.is_equal))
            dve.wait_ge(iota_ready, 1)
            io_ = iota8[:].rearrange("p (a e) -> p a e", a=1).broadcast_to((TILE, NT, E))
            link(dve.scalar_tensor_tensor(out=cand[:], in0=cand[:], scalar=-100.0, in1=io_,
                                          op0=ALU.mult, op1=ALU.add))
            link(dve.tensor_reduce(gred[0][:, 3, :], cand[:], AX_X, ALU.min))
            link(dve.tensor_tensor(cand[:], cand[:], over(gred[0][:, 3, :]), ALU.is_equal))
            dve.tensor_tensor(gate[:], cand[:], over(gred[0][:, 2, :]), ALU.mult).then_inc(gate_ready, 1)
            experts_added(0)

            def last_added(s, i):
                key = ("eo", s, 7, i)
                dve.wait_ge(x2_sum, NT * s + i + 1)
                completed(dve, key)
                drain(dve.scalar_tensor_tensor(out=xm[i % WIDE][:], in0=bank(key)[0:TILE, :], scalar=gate[:, i, 7:8],
                                               in1=xm[i % WIDE][:], op0=ALU.mult, op1=ALU.add), key)

            def x2_(i):
                last_added(0, i)
                carried(dve, ("eo", 0, 7, i))
                ln_stats(2, i, xm[i % WIDE][:])

            x2_(0)
            for i in range(NT + 1):
                if i < NT:
                    if i >= 2:
                        completed(dve, ("xt", 2, i - 2))
                        dve.wait_ge(xn2_lo, i - 1)
                    ln_norm(2, i, xm[i % WIDE][:], xnm[i % 2][:])
                    if i + 1 < NT:
                        x2_(i + 1)
                if i >= 1:
                    ln_T_lo(2, i - 1, xnT)
            with dve.If(fit == 1):
                for j in range(NT):
                    sl = slice(j * TILE, (j + 1) * TILE)
                    ins = dve.tensor_tensor(AT[:, j, sl], AT[:, j, sl].bitcast(F32), ident[0:TILE, 0:TILE], ALU.add)
                ins.then_inc(self_loops, 1)
            with dve.Else():
                for j in range(NT):
                    sl = slice(j * TILE, (j + 1) * TILE)
                    ins = dve.tensor_tensor(AT32[:, j, sl], AT32[:, j, sl], ident[0:TILE, 0:TILE], ALU.add)
                ins.then_inc(self_loops, 1)

            for i in range(NT - WIDE, NT):
                x_stored(dve, ("xm0", i))
            for i in range(NT):
                key = ("k2", i)
                ps = bank(key)[0:TILE, :]
                completed(dve, key)
                if i >= 3:
                    dve.wait_ge(kacc_done, i - 1)
                    dve.wait_ge(k_ready, i - 2)
                dve.tensor_scalar(kx[i % 3][:], ps, 0.0, None, ALU.min).then_inc(k_min, 1)
                dve.wait_ge(k_exped, i + 1)
                drain(dve.scalar_tensor_tensor(out=kx[i % 3][:], in0=ps, scalar=0.0, in1=kx[i % 3][:],
                                               op0=ALU.max, op1=ALU.add), key)
                dve.wait_ge(k_hi, i + 1)
                dve.tensor_tensor(kp[i % 2].lo[:], kx[i % 3][:], kp[i % 2].hi32[:], ALU.subtract).then_inc(k_ready, 1)
            for b in range(FB):
                lo(("kv", b), kv.lo[:, b, :], bank(("kv", b)), kv.hi32[:, b, :])
            lo(("ks",), ksum.lo[:], bank(("ks",))[:, 0:2 * FB].rearrange("p (b a) -> p b a", b=FB), ksum.hi32[:])

            def q_mins(g, f):
                completed(dve, ("q2", g, f))
                dve.tensor_scalar(q2[g % 2].lo32[:, f, :], bank(("q2", g, f))[:, 0:QC], 0.0, None, ALU.min)\
                    .then_inc(q_min, 1)

            def q_sums(g, f):
                q_ = q2[g % 2].lo32[:, f, :]
                dve.wait_ge(q_exped, g * FB + f + 1)
                drain(dve.scalar_tensor_tensor(out=q_, in0=bank(("q2", g, f))[:, 0:QC], scalar=0.0, in1=q_,
                                               op0=ALU.max, op1=ALU.add), ("q2", g, f))

            def q_los(g, f):
                q_ = q2[g % 2]
                dve.wait_ge(q_hi, g * FB + f + 1)
                dve.tensor_tensor(q_.lo[:, f, :], q_.lo32[:, f, :], q_.hi32[:, f, :], ALU.subtract).then_inc(q_ready, 1)

            def mixed(i):
                c = 24 + 2 * (i % 2)
                completed(dve, ("dn", i))
                drain(dve.tensor_scalar(cols[0:TILE, c:c + 1], bank(("dn", i))[0:TILE, 0:1], 1e-6, None, ALU.add),
                      ("dn", i))
                carried(dve, ("dn", i))
                link(dve.reciprocal(cols[0:TILE, c + 1:c + 2], cols[0:TILE, c:c + 1]))
                x_landed(dve, ("xq", i))
                completed(dve, ("mx", i))
                drain(dve.scalar_tensor_tensor(out=xq[i % 2][:], in0=bank(("mx", i))[0:TILE, :],
                                               scalar=cols[0:TILE, c + 1:c + 2], in1=xq[i % 2][:],
                                               op0=ALU.mult, op1=ALU.add), ("mx", i))

            for g in range(NQ + 1):
                if g < NQ:
                    if g >= 2:
                        completed(dve, ("mx", 2 * g - 3))
                    for f in range(FB + 2):
                        if f < FB:
                            q_mins(g, f)
                        if 0 < f <= FB:
                            q_sums(g, f - 1)
                        if f > 1:
                            q_los(g, f - 2)
                    for i in (2 * g, 2 * g + 1):
                        dve.wait_ge(xs_whole, i + 1)
                        dve.tensor_scalar(xn2.lo32[:, i, :], xn2.lo32[:, i, :], dinc[:, i:i + 1], None, ALU.mult)\
                            .then_inc(xs_scaled, 1)
                        dve.wait_ge(xs_hi, i + 1)
                        dve.tensor_tensor(xn2.lo[:, i, :], xn2.lo32[:, i, :], xn2.hi32[:, i, :], ALU.subtract)\
                            .then_inc(xs_ready, 1)
                if g > 0:
                    mixed(2 * g - 2)
                    mixed(2 * g - 1)

            dve.wait_ge(deg_root, 2)
            for n, (f, c) in enumerate(HX):
                o, w = CH[c]
                key = ("z", f, c)
                z_ = zT.lo32[:, f, o:o + w]
                completed(dve, key)
                drain(dve.tensor_tensor(z_, bank(key)[:, 0:w], CNTB[:, o:o + w], ALU.mult), key)
                dve.wait_ge(z_hi, n + 1)
                dve.tensor_tensor(zT.lo[:, f, o:o + w], z_, zT.hi32[:, f, o:o + w], ALU.subtract).then_inc(z_ready, 1)
            for hf in range(2):
                for n, (f, c) in enumerate(HX):
                    o, w = CH[c]
                    dve.wait_ge(h1_hi, hf * len(HX) + n + 1)
                    dve.tensor_tensor(h1T.lo[:, f, o:o + w], h1T.lo32[:, f, o:o + w], h1T.hi32[:, f, o:o + w],
                                      ALU.subtract).then_inc(h1_ready, 1)
                if hf == 0:
                    continue
                for i in range(NT):
                    key = ("yy", 1, i)
                    carried(dve, ("yy", 0, i))
                    completed(dve, key)
                    y_ = y3.lo32[:, i, :]
                    drain(dve.scalar_tensor_tensor(out=y_, in0=bank(key)[0:TILE, :], scalar=dinc[:, i:i + 1], in1=y_,
                                                   op0=ALU.mult, op1=ALU.add), key)
                    dve.wait_ge(y3_hi, i + 1)
                    dve.tensor_tensor(y3.lo[:, i, :], y_, y3.hi32[:, i, :], ALU.subtract).then_inc(y3_ready, 1)

            def hx_lo(i):
                sl = slice(i * TILE, (i + 1) * TILE)
                dve.wait_ge(hx_hi, i + 1)
                dve.tensor_tensor(hxT.lo[:, :, sl], hxT.lo32[:, :, sl], hxT.hi32[:, :, sl], ALU.subtract)\
                    .then_inc(hx_ready, 1)

            dve.wait_ge(b2_in, 16)
            for i in range(NT + 1):
                if i < NT:
                    x_landed(dve, ("xa3", i))
                    completed(dve, ("a3", i))
                    drain(dve.scalar_tensor_tensor(out=gt_[:], in0=bank(("a3", i))[0:TILE, :], scalar=dinc[:, i:i + 1],
                                                   in1=b2B[:], op0=ALU.mult, op1=ALU.add), ("a3", i))
                    carried(dve, ("a3", i))
                    dve.scalar_tensor_tensor(out=xg[i % WIDE][:], in0=gt_[:], scalar=0.0, in1=xg[i % WIDE][:],
                                             op0=ALU.max, op1=ALU.add).then_inc(x3_sum, 1)
                    dve.wait_ge(x3_sum, i + 1)
                    ln_stats(3, i, xg[i % WIDE][:])
                if i >= 1:
                    if i >= 3:
                        completed(dve, ("xt", 4, i - 3))
                    ln_norm(4, i - 1, xnA[(i - 1) % 2][:], xnB[(i - 1) % 2][:])
                if i < NT:
                    ln_norm(3, i, xg[i % WIDE][:], xnA[i % 2][:])
                    dve.wait_ge(ln_xnf, lnno[(3, i)] + 1)
                    ln_stats(4, i, xnA[i % 2][:])
                if i >= 2:
                    hx_lo(i - 2)
            hx_lo(NT - 1)
            def tt(a, b, out_, op):
                return dve.tensor_tensor(out_, a, b, op)

            def unit_sums(s, i):
                c = 8 * (i % 2)
                dve.wait_ge(squared, NT * s + i + 1)
                if i >= 2 or s:
                    dve.wait_ge(unit_root, NT * s + i - 1)
                link(dve.tensor_reduce(cols[0:TILE, c:c + 8], sqr[i % 2][:].rearrange("p (h d) -> p h d", h=HEADS),
                                       AX_X, ALU.add))
                dve.tensor_scalar(cols[0:TILE, c:c + 8], cols[0:TILE, c:c + 8], 1e-12, (1.0, 1.0 / DH)[s], ALU.add,
                                  ALU.mult).then_inc(unit_sum, 1)

            def unit_norm(s, w, i):
                c = 16 + 8 * (i % 2)
                r = cols[0:TILE, c:c + 8]
                dve.wait_ge(unit_root, NT * s + i + 1)
                link(dve.reciprocal(r, r))
                if i >= 2:
                    completed(dve, ("t" + w, i - 2))
                elif s:
                    completed(dve, ("tq", NT - 2 + i))
                drain(dve.tensor_tensor(unit[i % 2][:].rearrange("p (h d) -> p h d", h=HEADS),
                                        bank(("p" + w, i))[0:TILE, :].rearrange("p (h d) -> p h d", h=HEADS),
                                        r.rearrange("p (h a) -> p h a", a=1).broadcast_to((TILE, HEADS, DH)),
                                        ALU.mult), ("p" + w, i))

            def max_part(key):
                b = key[1]
                if key[0] == "mx":
                    _, b, a, i, q = key
                    completed(dve, key)
                    ins = dve.tensor_reduce(chmax[:, a, i, q:q + 1], bank(key)[0:TILE, 0:piece_width(i, q)], AX_X,
                                            ALU.max)
                    drain(ins, key)
                    if key == ("mx", b, *PIECES[-1]):
                        carried(dve, key)
                        if b > 0:
                            completed(dve, ("mt", b - 1, 2))
                        dve.tensor_reduce(negm[:].rearrange("p t a -> p a t"), chmax[:], AX_X, ALU.max,
                                          negate=True).then_inc(max_found, 1)
                else:
                    _, b, c = key
                    o, w = CH[c]
                    completed(dve, key)
                    rows_ = slice(32 * b, 32 * b + 2)
                    dve.wait_ge(max_found, b + 1)
                    drain(dve.tensor_copy(rowmax[rows_, o:o + w], bank(key)[0:2, 0:w]), key)

            even, odd = slice(0, HEADS, 2), slice(1, HEADS, 2)
            up, down = slice(0, DH), slice(DH, 2 * DH)
            completed(dve, ("a3", NT - 1))
            dve.memset(chmax[:], -3e38).then_inc(att_ready, 1)
            for s, (w, gain) in enumerate((("q", "qn_g"), ("k", "kn_g"))):
                g_ = ccol[:, COL[gain]:COL[gain] + 1]
                unit_sums(s, 0)
                unit_norm(s, w, 0)
                for i in range(NT):
                    if i + 1 < NT:
                        unit_sums(s, i + 1)
                        unit_norm(s, w, i + 1)
                    key = ("t" + w, i)
                    sl = slice(i * TILE, (i + 1) * TILE)
                    t_ = bank(key)[:, 0:FB * TILE].rearrange("p (b n) -> p b n", b=FB)
                    dve_los.append(key)
                    dve.wait_ge(hi_done, len(dve_los))
                    if w == "q":
                        outs = (QA[down, even, sl], QA[up, odd, sl])
                        ins = (QA32[up, even, sl], QA32[down, odd, sl])
                    else:
                        outs = (KLO[up, :, sl], KLO[down, :, sl])
                        ins = (KA32[up, even, sl], KA32[down, odd, sl])
                    for a in range(2):
                        half = (up, down)[a]
                        last = dve.scalar_tensor_tensor(out=outs[a], in0=t_[half], scalar=g_[half], in1=ins[a],
                                                        op0=ALU.mult, op1=ALU.subtract)
                    drain(last, key)
                    if w == "k" and i >= 2:
                        dve.wait_ge(att_ready, 1)
                        for key in pieces_of(i - 2):
                            max_part(key)

            def out_lo(n):
                b, c = n // 3, n % 3
                o, w = CH[c]
                dve.wait_ge(ot_hi, n + 1)
                dve.tensor_tensor(OT[:, b, 1, o:o + w], OT32[:, b, o:o + w], OT[:, b, 0, o:o + w].bitcast(F32),
                                  ALU.subtract).then_inc(ot_ready, 1)

            def chunk_out(b, c):
                o, w = CH[c]
                completed(dve, ("ss", b, c))
                if (b, c) == (0, 0):
                    dve.wait_ge(v_ready, NT)
                drain(dve.reciprocal(OT32[:, b, o:o + w], bank(("ss", b, c))[:, 0:w]), ("ss", b, c))
                carried(dve, ("ss", b, c))
                for a, half in enumerate((up, down)):
                    key = ("ov", b, c, a)
                    completed(dve, key)
                    drain(dve.tensor_tensor(OT32[half, b, o:o + w], OT32[half, b, o:o + w], bank(key)[half, 0:w],
                                            ALU.mult), key)
                carried(dve, ("ov", b, c, 0))
                carried(dve, ("ov", b, c, 1))
                dve.memset(cols[:, 36:37], 0.0).then_inc(ot_whole, 1)

            completed(dve, ("tk", NT - 1))
            dve.memset(ones64[:], 1.0)
            dve.memset(maskall[:], -1e30)
            for b in range(FB):
                rows_ = slice(32 * b, 32 * b + 2)
                ins = dve.tensor_copy(sel[rows_, :, :],
                                      ident[rows_, 32 * b:32 * b + 2].rearrange("p (a n) -> p a n", n=1)
                                      .broadcast_to((2, 2, 128)))
            ins.then_inc(att_ready, 1)
            for key in pieces_of(NT - 2) + pieces_of(NT - 1) + [("mt", 0, c) for c in range(3)]:
                max_part(key)
            between, asked = [], []
            for g, (b, c, a, j) in enumerate(STEPS):
                off, w = valid(c, j)
                if g % PER_PAIR == 0 and b + 1 < FB:
                    between = max_work(b + 1)
                if asked:
                    max_part(asked.pop())
                if between and not chunk_after(g - 1):
                    asked.append(between.pop(0))
                dve.wait_ge(p_hi, g + 1)
                dve.tensor_tensor(PT[g % NPT].lo[:, off:w], P[g % NP][:, off:w], PT[g % NPT].hi32[:, off:w],
                                  ALU.subtract).then_inc(p_ready, 1)
                if (b, c) != (0, 0) and (a, j) == (1, 2):
                    out_lo(3 * b + c - 1)
                if chunk_after(g):
                    chunk_out(*chunk_after(g))
            chunk_out(FB - 1, 2)
            out_lo(3 * FB - 1)
            for f, c in WO:
                o, w = CH[c]
                lo(("wo", f, c), yT.lo[:, f, o:o + w], bank(("wo", f, c))[:, 0:w], yT.hi32[:, f, o:o + w])

            logits_less_max(1)
            softmax_scale(1)
            dve.tensor_tensor(gate[:], ex[1][:], over(gred[1][:, 2, :]), ALU.mult).then_inc(gate_ready, 1)
            experts_added(1)
            for i in range(NT):
                last_added(1, i)

        @block.tensor
        def _(pe):
            def mm3(out_, l, r, start, stop):
                pe.matmul(out_, l[0], r[0], start=start, stop=False)
                pe.matmul(out_, l[0], r[1], start=False, stop=False)
                return pe.matmul(out_, l[1], r[0], start=False, stop=stop)

            def opened(key, later=0):
                b, n = place[key]
                if n > 1:
                    pe.wait_ge(drained[b], later + (n - 1))
                return PS[:, b, :]

            def done(ins, key):
                ins.then_inc(filled[place[key][0]], 1)

            def of(p, *idx):
                return (p.hi[idx], p.lo[idx])

            al = slice(None)

            def blk(b, w=128):
                return slice(b * w, (b + 1) * w)

            def product(key, out_, pairs):
                for n, (l, r) in enumerate(pairs):
                    ins = mm3(out_, l, r, n == 0, n == len(pairs) - 1)
                done(ins, key)

            def ln_T(s, i, xnf_):
                pe.wait_ge(ln_xnf, lnno[(s, i)] + 1)
                o = opened(("xt", s, i))
                for b in range(FB):
                    ins = pe.transpose(o[:, blk(b, TILE)], xnf_[:, blk(b)], ident[0:TILE, 0:TILE])
                done(ins, ("xt", s, i))

            def w_T(w, raw_):
                for ib in range(FB):
                    w_block_T(w, raw_, ib)

            def w_block_T(w, raw_, ib):
                o = opened(("wt", w, ib))
                for ob in range(FB):
                    ins = pe.transpose(o[:, blk(ob)], raw_[:, ob, blk(ib)], ident[:])
                done(ins, ("wt", w, ib))

            def work(key):
                if key[0] == "wt":
                    _, w, ib = key
                    raw_, raw_in = {"k": (rawk, rawk_in), "2": (raw2, raw2_in), "q": (rawq, rawq_in)}[w]
                    if ib == 0:
                        pe.wait_ge(raw_in, 16)
                    w_block_T(w, raw_, ib)
                elif key[0] == "vec":
                    pe.wait_ge(vecs_in, 16 * 10)
                    done(pe.transpose(opened(key)[:, 0:54], vecs[:], ident[0:54, 0:54]), key)
                elif key[0] == "mi":
                    if key[1] == 0:
                        pe.wait_ge(unit_ready, 1)
                        for b in range(FB):
                            carried(pe, ("wt", "2", b))
                    product(key, opened(key), [(of(W1p, al, jb, blk(key[1])), of(W2T, al, jb, al)) for jb in range(FB)])
                else:
                    if key[1] == 0:
                        pe.wait_ge(unit_ready, 2)
                        pe.wait_ge(mi_ready, FB)
                    product(key, opened(key), [(of(Wvp, al, eb, blk(key[1])), of(MI, al, eb, al)) for eb in range(FB)])

            pe.wait_ge(const_ready, 1)
            for i in range(NT):
                ln_T(0, i, xnf[i % 2])
                for key in work_after(i):
                    work(key)

            for i in range(NT):
                carried(pe, ("xt", 0, i))
            for ib in range(FB):
                carried(pe, ("wt", "k", ib))
                carried(pe, ("wt", "q", ib))
                carried(pe, ("g", ib))

            def k_block(b):
                for c, (o, w) in enumerate(CH):
                    product(("k", b, c), opened(("k", b, c))[:, 0:w],
                            [(of(WA, al, kb, blk(b)), of(xnT, al, kb, slice(o, o + w))) for kb in range(FB)])

            k_block(0)
            for b in range(FB + 1):
                if b + 1 < FB:
                    k_block(b + 1)
                if b < FB:
                    for c in range(3):
                        carried(pe, ("k", b, c))
                    for q in range(3):
                        o = opened(("kt", b, q))
                        for t in range(min(4, NT - 4 * q)):
                            ins = pe.transpose(o[0:TILE, blk(t)], kT[b % 2][:, blk(4 * q + t, TILE)], ident[:])
                        done(ins, ("kt", b, q))
                    for q in range(3):
                        carried(pe, ("kt", b, q))
                    pe.wait_ge(ln_lo, NT)
                    product(("c1", b), opened(("c1", b)),
                            [(of(ek, al, i, al), of(xn, al, i, al)) for i in range(NT)])
                    carried(pe, ("c1", b))
                    o = opened(("c1t", b))
                    for cb in range(FB):
                        ins = pe.transpose(o[:, blk(cb)], c1f[:, blk(cb)], ident[:])
                    done(ins, ("c1t", b))
                if b > 0:
                    carried(pe, ("c1t", b - 1))
                    product(("cx", b - 1), opened(("cx", b - 1)),
                            [(of(c1[(b - 1) % 2], al, cb, al), of(G, al, cb, al)) for cb in range(FB)])

            def edge_columns():
                pe.wait_ge(idx_f, 4)
                pe.wait_ge(const_ready, 2)
                o = opened(("ix",))
                for a, rows in enumerate((srcR, dstR)):
                    for h in range(2):
                        ins = pe.transpose(o[0:TILE, 170 * a + 85 * h:170 * a + 85 * h + 85], rows[:, h, :], ident[0:85, 0:85])
                done(ins, ("ix",))
                o = opened(("wv",))
                done(pe.matmul(o[0:TILE, 0:2 * GROUPS], onesA[0:GROUPS, 0:TILE], gD[:], start=True, stop=True), ("wv",))

            def q_tile(i):
                product(("q", i), opened(("q", i))[0:TILE, :],
                        [(of(xnT, al, kb, blk(i, TILE)), of(WB, al, kb, al)) for kb in range(FB)])

            q_tile(0)
            pe.wait_ge(cx_ready, FB)
            for i in range(NT):
                if i + 1 < NT:
                    q_tile(i + 1)
                for _, name, ib in torch_after(i):
                    n = names.index(name)
                    if ib == 0:
                        pe.wait_ge(wraw_in[n % 2], 16 * (n // 2 + 1))
                    w_block_T(name, wraw[n % 2], ib)
                pe.wait_ge(q_norm, i + 1)
                o = opened(("qt", i))
                for b in range(FB):
                    ins = pe.transpose(o[:, blk(b, TILE)], qe[i % 2][:, blk(b)], ident[0:TILE, 0:TILE])
                done(ins, ("qt", i))
                o = opened(("mo", i))[0:TILE, :]
                for kb in range(FB):
                    mm3(o, of(xnT, al, kb, blk(i, TILE)), of(MI, al, kb, al), kb == 0, False)
                carried(pe, ("qt", i))
                for b in range(FB):
                    ins = mm3(o, of(qT[i % 2], al, b, al), of(ctxp, al, b, al), False, b == FB - 1)
                done(ins, ("mo", i))
                if i == PREP:
                    edge_columns()

            for b in range(BANKS):
                pe.wait_ge(drained[b], before_edges[b])
            pe.wait_ge(edge_ready, 1)
            fit = pe.value_load(flags[0:1, 20:21], min_val=0, max_val=1)

            def tile_counts(half, os, od, first, last):
                for j in range(NT):
                    o_ = PS[0:TILE, 3 * half + j // 4, blk(j % 4)]
                    ins = pe.matmul(o_, os[:, blk(j, TILE)], od, start=(first and j % 4 == 0), stop=last,
                                    skip_group_check=True)
                return ins

            def in_degrees(counts, ones):
                for c, (o_, w_) in enumerate(CH):
                    o = opened(("cb", c))
                    for j in range(NT):
                        ins = pe.matmul(o[:, 0:w_], ones[:], counts[:, j, o_:o_ + w_], start=(j == 0), stop=(j == NT - 1))
                    done(ins, ("cb", c))

            def group_counts(g, half):
                pe.wait_ge(window_free, g + 1)
                pe.wait_ge(dst_ready, g + 1)
                for t in range(GT):
                    pe.wait_ge(src_ready, g * GT + (t + 1))
                    tile_counts(half, ohs[(half * GT + t) % NOH], ohd[half][:, t, :], t == 0, t == GT - 1)\
                        .then_inc(edge_tiles, 1)

            with pe.If(fit == 1):
                with pe.Fori(0, GROUPS // 2) as k:
                    group_counts(k * 2, 0)
                    group_counts(k * 2 + 1, 1)
                group_counts(GROUPS - 1, 0)
                pe.wait_ge(window_free, GROUPS + 2)
                in_degrees(AT, onesR)
            with pe.Else():
                with pe.Fori(0, NT) as w:
                    def all_group(g, first):
                        pe.wait_ge(all_dst, w * GROUPS + g + 1)
                        for t in range(GT):
                            pe.wait_ge(all_src, w * (GROUPS * GT) + g * GT + (t + 1))
                            tile_counts(0, ohs[0], ohd[0][:, t, :], first and t == 0, False)\
                                .then_inc(all_tiles, 1)

                    pe.wait_ge(all_taken, w + 1)
                    all_group(0, True)
                    with pe.Fori(1, GROUPS) as g:
                        all_group(g, False)
                pe.wait_ge(all_taken, NT + 1)
                in_degrees(AT32, onesA)

            for c in range(3):
                carried(pe, ("cb", c))
            o = opened(("cc",))
            for i in range(NT):
                ins = pe.transpose(o[0:TILE, i:i + 1], CNTB[0:1, blk(i, TILE)], ident[0:1, 0:1])
            done(ins, ("cc",))
            unit_split(pe, "Wl1")
            for i in range(NT):
                product(("y1", i), opened(("y1", i))[0:TILE, :],
                        [(of(xnT, al, kb, blk(i, TILE)), of(WA, al, kb, al)) for kb in range(FB)])
            unit_split(pe, "Wr1")
            for f in range(FB):
                for c, (o, w) in enumerate(CH):
                    product(("r1", f, c), opened(("r1", f, c))[:, 0:w],
                            [(of(WB, al, kb, blk(f)), of(xnT, al, kb, slice(o, o + w))) for kb in range(FB)])

            def counts_moving(key, p, f, c, fast_):
                o, w = CH[c]
                out_ = opened(key)[:, 0:w]
                for j in range(NT):
                    if fast_:
                        a = AT[:, j, o:o + w]
                        pe.matmul(out_, p.hi[:, j, blk(f)], a, start=(j == 0), stop=False)
                        ins = pe.matmul(out_, p.lo[:, j, blk(f)], a, start=False, stop=(j == NT - 1))
                    else:
                        a = AT32[:, j, o:o + w]
                        pe.matmul(out_, p.hi32[:, j, blk(f)], a, start=(j == 0), stop=False)
                        ins = pe.matmul(out_, p.lo[:, j, blk(f)].bitcast(F32), a, start=False, stop=(j == NT - 1))
                done(ins, key)

            def counts_still(key, p, i, fast_):
                out_ = opened(key)[0:TILE, :]
                for j in range(NT):
                    if fast_:
                        a = AT[:, j, blk(i, TILE)]
                        pe.matmul(out_, a, p.hi[:, j, :], start=(j == 0), stop=False)
                        ins = pe.matmul(out_, a, p.lo[:, j, :], start=False, stop=(j == NT - 1))
                    else:
                        a = AT32[:, j, blk(i, TILE)]
                        pe.matmul(out_, a, p.hi32[:, j, :], start=(j == 0), stop=False)
                        ins = pe.matmul(out_, a, p.lo[:, j, :].bitcast(F32), start=False, stop=(j == NT - 1))
                done(ins, key)

            def on_both_paths(stage):
                with pe.If(fit == 1):
                    stage(True)
                with pe.Else():
                    stage(False)

            for i in range(NT):
                carried(pe, ("y1", i))

            @on_both_paths
            def _(fast_):
                for f in range(FB):
                    for c in range(3):
                        counts_moving(("a1", f, c), y, f, c, fast_)

            pe.wait_ge(a1_ready, 3 * FB)
            unit_split(pe, "Wl2")
            for i in range(NT):
                product(("y2", i), opened(("y2", i))[0:TILE, :],
                        [(of(hT, al, kb, blk(i, TILE)), of(WA, al, kb, al)) for kb in range(FB)])
            unit_split(pe, "Wr2")
            for i in range(NT):
                product(("r2", i), opened(("r2", i))[0:TILE, :],
                        [(of(hT, al, kb, blk(i, TILE)), of(WB, al, kb, al)) for kb in range(FB)])
            for i in range(NT):
                carried(pe, ("y2", i))

            @on_both_paths
            def _(fast_):
                for i in range(NT + 1):
                    if i < NT:
                        counts_still(("a2", i), y, i, fast_)
                    if i >= 1:
                        ln_T(1, i - 1, xnw[(i - 1) % 2])
            def gate_logits(s, T):
                pe.wait_ge(wg_ready, 2 * s + 1)
                for c, (o, w) in enumerate(CH):
                    key = ("lt", s, c)
                    product(key, opened(key)[0:E, 0:w],
                            [(of(WgP[s], al, kb, al), of(T, al, kb, slice(o, o + w))) for kb in range(FB)])
                hidden_products(s, 0, 0, 0, T, (0,))
                for c in range(3):
                    carried(pe, ("lt", s, c))
                o = opened(("lg", s))
                for i in range(NT):
                    ins = pe.transpose(o[0:TILE, E * i:E * i + E], gT[s].lo32[:, blk(i, TILE)], ident[0:E, 0:E])
                done(ins, ("lg", s))
                hidden_products(s, 0, 0, 0, T, (1,))

            def gates_and_biases(s):
                pe.wait_ge(gate_ready, s + 1)
                for q, (o_, w_) in enumerate(CH):
                    o = opened(("gt", s, q))
                    for t in range(w_ // TILE):
                        ins = pe.transpose(o[0:E, blk(t, TILE)], gate[:, o_ // TILE + t, :], ident[0:TILE, 0:TILE])
                    done(ins, ("gt", s, q))
                for q in range(3):
                    carried(pe, ("gt", s, q))
                pe.wait_ge(wg_ready, 2 * s + 2)
                for i in range(NT):
                    product(("ac", s, i), opened(("ac", s, i))[0:TILE, :],
                            [(of(gT[s], al, blk(i, TILE)), of(b2P[s], al, 0, al))])

            def hidden_products(s, e, e_, later, T, halves=(0, 1)):
                pe.wait_ge(w_ready[0], e_ + (E * s + 1))
                w1 = W1P[1 - e % 2]
                for f in halves:
                    for c, (o, w) in enumerate(CH):
                        key = ("hd", s, e, f, c)
                        product(key, opened(key, later)[:, 0:w],
                                [(of(w1, al, kb, blk(f)), of(T, al, kb, slice(o, o + w))) for kb in range(FB)])

            def output_product(s, e, e_, later, i):
                if i == 0:
                    pe.wait_ge(w_ready[1], e_ + (E * s + 1))
                    pe.wait_ge(hid_ready, e_ * 6 + (48 * s + 6))
                w2 = W2P[1 - e % 2]
                key = ("eo", s, e, i)
                product(key, opened(key, later)[0:TILE, :],
                        [(of(hE[e % 2], al, f, blk(i, TILE)), of(w2, al, f, al)) for f in range(2)])

            def experts(s, T):
                with pe.Fori(0, PAIRS) as k:
                    hidden_products(s, 1, k * 2 + 1, k * 4, T)
                    for i in range(NT):
                        output_product(s, 0, k * 2, k * 4, i)
                    hidden_products(s, 2, k * 2 + 2, k * 4, T)
                    for i in range(NT):
                        output_product(s, 1, k * 2 + 1, k * 4, i)
                hidden_products(s, 7, 7, 0, T)
                for i in range(NT):
                    output_product(s, 6, 6, 0, i)

            for i in range(NT):
                carried(pe, ("xt", 1, i))
            gate_logits(0, xnT)
            gates_and_biases(0)
            experts(0, xnT)
            for i in range(NT + 1):
                if i < NT:
                    output_product(0, 7, 7, 0, i)
                if i >= 1:
                    ln_T(2, i - 1, xnm[(i - 1) % 2])
            def k2_tile(i):
                product(("k2", i), opened(("k2", i))[0:TILE, :],
                        [(of(xnT, al, kb, blk(i, TILE)), of(WB, al, kb, al)) for kb in range(FB)])

            for i in range(NT):
                carried(pe, ("xt", 2, i))
            unit_split(pe, "Wqk1")
            k2_tile(0)
            pe.wait_ge(xn2_lo, NT)
            for i in range(NT):
                if i + 1 < NT:
                    k2_tile(i + 1)
                pe.wait_ge(k_ready, i + 1)
                for b in range(FB):
                    o = opened(("kv", b)) if i == 0 else bank(("kv", b))
                    ins = mm3(o, of(kp[i % 2], al, blk(b)), of(xn2, al, i, al), i == 0, i == NT - 1)
                    if i == NT - 1:
                        done(ins, ("kv", b))
                if i < NT - 1:
                    ins.then_inc(k_used, 1)
            pe.wait_ge(kacc_done, NT + 1)
            o = opened(("ks",))
            for b in range(FB):
                ins = pe.matmul(o[:, 2 * b:2 * b + 2], kacc[:, blk(b)], ones2[0:TILE, 0:2], start=True, stop=True)
            done(ins, ("ks",))
            unit_split(pe, "Wqk0")
            for g in range(NQ + 1):
                if g < NQ:
                    for f in range(FB):
                        product(("q2", g, f), opened(("q2", g, f))[:, 0:QC],
                                [(of(WA, al, kb, blk(f)), of(xnT, al, kb, blk(g, QC))) for kb in range(FB)])
                if g > 0:
                    if g == 1:
                        carried(pe, ("kv", FB - 1))
                        carried(pe, ("ks",))
                    pe.wait_ge(q_ready, g * FB)
                    q_ = q2[(g - 1) % 2]
                    for t in range(2):
                        i = 2 * g - 2 + t
                        product(("dn", i), opened(("dn", i))[0:TILE, 0:2],
                                [(of(q_, al, b, blk(t, TILE)), of(ksum, al, b, al)) for b in range(FB)])
                        product(("mx", i), opened(("mx", i))[0:TILE, :],
                                [(of(q_, al, b, blk(t, TILE)), of(kv, al, b, al)) for b in range(FB)])

            pe.wait_ge(self_loops, 1)
            pe.wait_ge(xs_ready, NT)

            @on_both_paths
            def _(fast_):
                for f, c in HX:
                    counts_moving(("z", f, c), xn2, f, c, fast_)

            pe.wait_ge(z_ready, len(HX))
            for hf in range(2):
                unit_split(pe, "gW1" + "ab"[hf])
                for f, c in HX:
                    o, w = CH[c]
                    product(("h1", hf, f, c), opened(("h1", hf, f, c))[:, 0:w],
                            [(of(WB, al, kb, blk(f)), of(zT, al, kb, slice(o, o + w))) for kb in range(FB)])
                unit_split(pe, "gW2" + "ab"[hf])
                pe.wait_ge(h1_ready, (hf + 1) * len(HX))
                for i in range(NT):
                    product(("yy", hf, i), opened(("yy", hf, i))[0:TILE, :],
                            [(of(h1T, al, kb, blk(i, TILE)), of(WA, al, kb, al)) for kb in range(FB)])
            pe.wait_ge(y3_ready, NT)
            unit_split(pe, "aWv")

            @on_both_paths
            def _(fast_):
                for i in range(NT + 3):
                    if i < NT:
                        counts_still(("a3", i), y3, i, fast_)
                    if 2 <= i < NT + 2:
                        ln_T(4, i - 2, xnB[i % 2])
                    if i >= 3:
                        v = i - 3
                        pe.wait_ge(hx_ready, v + 1)
                        product(("pv", v), opened(("pv", v))[0:TILE, :],
                                [(of(hxT, al, kb, blk(v, TILE)), of(WB, al, kb, al)) for kb in range(FB)])
            def scores_for_max(key):
                if key[0] == "mx":
                    _, b, a, i, q = key
                    h = 2 * b + a
                    o = opened(key)[0:TILE]
                    w_ = piece_width(i, q)
                    even_w = w_ + w_ % 2
                    diagonal = q == i // 4
                    ins = pe.matmul(o[:, 0:even_w], QA[:, h, blk(i, TILE)], KA[:, h, 500 * q:500 * q + even_w],
                                    start=True, stop=not diagonal)
                    if diagonal:
                        ins = pe.matmul(o[:, w_ - TILE:w_], identb[0:TILE, 0:TILE], causal[:], start=False, stop=True)
                    done(ins, key)
                else:
                    _, b, c = key
                    o_, w_ = CH[c]
                    pe.wait_ge(max_found, b + 1)
                    o = opened(key)
                    for t in range(w_ // TILE):
                        ins = pe.transpose(o[0:2, blk(t, TILE)], negm[:, o_ // TILE + t, :], ident[0:TILE, 0:TILE])
                    done(ins, key)

            pe.wait_ge(hx_ready, NT)
            for w, unit_, W in (("q", "aWq", WA), ("k", "aWk", WB)):
                unit_split(pe, unit_)
                for i in range(NT + 1):
                    if i < NT:
                        product(("p" + w, i), opened(("p" + w, i))[0:TILE, :],
                                [(of(hxT, al, kb, blk(i, TILE)), of(W, al, kb, al)) for kb in range(FB)])
                    if i >= 1:
                        key = ("t" + w, i - 1)
                        carried(pe, ("p" + w, i - 1))
                        o = opened(key)
                        for b in range(FB):
                            ins = pe.transpose(o[:, blk(b, TILE)], unit[(i - 1) % 2][:, blk(b)], ident[0:TILE, 0:TILE])
                        done(ins, key)
                    if w == "k" and i >= 3:
                        carried(pe, ("tq", NT - 1))
                        pe.wait_ge(k_twice, i - 1)
                        for key in pieces_of(i - 3):
                            scores_for_max(key)

            def scores(g):
                b, c, a, j = STEPS[g]
                h, hi_rows = 2 * b + a, slice(DH * a, DH * a + DH)
                q0 = CH[c][0]
                off, w = valid(c, j)
                key = ("sT", g)
                o = opened(key)[0:TILE]
                qs = slice(q0 + off, q0 + w)
                pe.matmul(o[:, off:w], KA[:, h, blk(j, TILE)], QA[:, h, qs], start=True, stop=False)
                pe.matmul(o[:, off:w], KLO[hi_rows, b, blk(j, TILE)], QA[hi_rows, h, qs], start=False, stop=False)
                d = TILE * j - q0
                rows_ = slice(32 * b, 32 * b + 2)
                ins = pe.matmul(o[:, off:w], sel[rows_, a, 0:TILE], rowmax[rows_, qs], start=False, stop=d < 0)
                if d >= 0:
                    if d > off:
                        pe.matmul(o[:, off:d], maskall[:], identb[0:TILE, 0:TILE], start=False, stop=False)
                    ins = pe.matmul(o[:, d:d + TILE], causal[:], identb[0:TILE, 0:TILE], start=False, stop=True)
                done(ins, key)

            def product_with_v(g):
                b, c, a, j = STEPS[g]
                off, w = valid(c, j)
                key = ("ov", b, c, a)
                pe.wait_ge(p_ready, g + 1)
                pe.wait_ge(v_ready, j + 1)
                o = opened(key) if j == 0 else bank(key)
                ins = mm3(o[:, off:w], of(V, al, j, blk(b)), of(PT[g % NPT], al, slice(off, w)), j == 0,
                          j == last_key(c))
                if j < last_key(c):
                    ins.then_inc(pt_used, 1)
                    return
                done(ins, key)
                if a == 0:
                    return
                pe.wait_ge(p_added, g + 1)
                o = opened(("ss", b, c))
                for a_ in range(2):
                    ins = pe.matmul(o[DH * a_:DH * a_ + DH, 0:w], ones64[:], sacc[a_][:, 0:w], start=True, stop=True)
                done(ins, ("ss", b, c))

            pe.wait_ge(k_twice, NT)
            carried(pe, ("tk", NT - 1))
            for key in pieces_of(NT - 2) + pieces_of(NT - 1) + [("mt", 0, c) for c in range(3)]:
                scores_for_max(key)
            pe.wait_ge(att_ready, 2)
            between = []
            for g, (b, c, a, j) in enumerate(STEPS):
                if g % PER_PAIR == 0:
                    for c_ in range(3):
                        carried(pe, ("mt", b, c_))
                    if b + 1 < FB:
                        between = max_work(b + 1)
                scores(g)
                if g >= LAG:
                    product_with_v(g - LAG)
                if between and not chunk_after(g - 1):
                    scores_for_max(between.pop(0))
            for g in range(len(STEPS) - LAG, len(STEPS)):
                product_with_v(g)

            pe.wait_ge(wo_ready, FB)
            for f, c in WO:
                o, w = CH[c]
                if f == 0:
                    pe.wait_ge(ot_ready, 3 * FB - 2 + c)
                product(("wo", f, c), opened(("wo", f, c))[:, 0:w],
                        [(of(Wo, al, kb, blk(f)), (OT[:, kb, 0, o:o + w], OT[:, kb, 1, o:o + w])) for kb in range(FB)])
            for f, c in HX:
                carried(pe, ("wo", f, c))
            gate_logits(1, yT)
            gates_and_biases(1)
            experts(1, yT)
            for i in range(NT):
                output_product(1, 7, 7, 0, i)

        assert act_his == dve_los


_INS = ['x', 'src', 'dst', 'L0_gnn_Wl1', 'L0_gnn_bl1', 'L0_gnn_Wr1', 'L0_gnn_Wl2', 'L0_gnn_bl2', 'L0_gnn_Wr2',
        'L0_mix_Wq', 'L0_mix_Wk', 'L0_mix_Wv', 'L0_mix_W1', 'L0_mix_W2', 'L0_ffn_Wg', 'L0_ffn_bg', 'L0_ffn_W1',
        'L0_ffn_b1', 'L0_ffn_W2', 'L0_ffn_b2', 'L1_gnn_W1', 'L1_gnn_b1', 'L1_gnn_W2', 'L1_gnn_b2', 'L1_mix_W_qk',
        'L1_ffn_ln_g', 'L1_ffn_ln_b', 'L1_ffn_Wq', 'L1_ffn_Wk', 'L1_ffn_Wv', 'L1_ffn_Wo', 'L1_ffn_qn_g',
        'L1_ffn_kn_g', 'L1_ffn_gate_W', 'L1_ffn_gate_b', 'L1_ffn_W1', 'L1_ffn_b1', 'L1_ffn_W2', 'L1_ffn_b2']


def kernel(**inputs):
    import numpy as _np
    import concourse.bacc as _bacc
    from concourse import mybir as _mybir
    from concourse.bass_utils import run_bass_kernel_spmd as _run

    nc = _bacc.Bacc("TRN2", target_bir_lowering=False, num_devices=1)
    arrays, args = {}, []
    for name in _INS:
        a = _np.ascontiguousarray(inputs[name])
        arrays[f"in_{name}_dram"] = a
        args.append(nc.dram_tensor(f"in_{name}_dram", a.shape, _mybir.dt.from_np(a.dtype), kind="ExternalInput").ap())
    args.append(nc.dram_tensor("out_0_dram", (N, D), _mybir.dt.float32, kind="ExternalOutput").ap())
    build(nc, *args)
    r = _run(nc, [arrays], core_ids=[0])
    return r.results[0]["out_0_dram"]
```
